# Optimizing a Trainium2 kernel written in Bass

```python
import numpy as np
import jax
import jax.numpy as jnp

def _softmax(x, axis=-1):
    return jax.nn.softmax(x, axis=axis)

def _gelu(x):
    return jax.nn.gelu(x, approximate=True)

def _silu(x):
    return jax.nn.silu(x)

def _sigmoid(x):
    return jax.nn.sigmoid(x)

def _layernorm(x, axis=-1, eps=1e-05):
    m = jnp.mean(x, axis=axis, keepdims=True)
    v = jnp.var(x, axis=axis, keepdims=True)
    return (x - m) / jnp.sqrt(v + eps)

def _scatter_add(tgt, idx, src, axis=0):
    return tgt.at[idx].add(src)

def _segment_sum(src, seg, n):
    return jax.ops.segment_sum(src, seg, n)
kernel_name = 'mk_decoder_preln_d2_seqx_r8_debe54'

def setup_inputs(seed: int=0):
    np.random.seed(seed)
    _w = jnp.asarray

    def _rec_inputs():
        import jax
        import jax.numpy as jnp
        _rk = jax.random.key(seed)
        x = -0.000125 + 0.9999 * jax.random.normal(jax.random.fold_in(_rk, 1), (128, 64, 128), jnp.float32)
        _lenS = 64 - jax.random.randint(jax.random.fold_in(_rk, 7), (128,), 0, max(1, 64 // 4) + 1, jnp.int32)
        _lenS2 = 64 - jax.random.randint(jax.random.fold_in(_rk, 8), (128,), 0, max(1, 64 // 4) + 1, jnp.int32)
        _ctx_768P = jax.random.normal(jax.random.fold_in(_rk, 11), (128, 16, 96), jnp.float32)
        _ctx_768c = jax.random.dirichlet(jax.random.fold_in(_rk, 511), 0.3 * jnp.ones((16,), jnp.float32), (128, 64))
        _ctx_768t = jnp.einsum('bsk,bkd->bsd', _ctx_768c, _ctx_768P)
        _ctx_768t = _ctx_768t * jax.lax.rsqrt(jnp.mean(jnp.square(_ctx_768t)) + 1e-12) * 0.953939
        ctx_768 = 0.00272024 + 0.999456 * (_ctx_768t + 0.3 * jax.random.normal(jax.random.fold_in(_rk, 611), (128, 64, 96), jnp.float32))
        return (x, ctx_768)
    x, ctx_768 = _rec_inputs()

    def _L0_attn_setup():
        import jax, jax.numpy as jnp
        import numpy as np
        B, S, E, H = (8, 128, 128, 16)
        EPS = 0.001
        key = jax.random.key(seed)
        ks = jax.random.split(key, 5)
        x = jax.random.normal(ks[0], (B, S, E), dtype=jnp.float32)
        Wq = jax.random.normal(ks[1], (E, E), dtype=jnp.float32) * 0.02
        Wk = jax.random.normal(ks[2], (E, E), dtype=jnp.float32) * 0.02
        Wv = jax.random.normal(ks[3], (E, E), dtype=jnp.float32) * 0.02
        rel_table = jax.random.normal(ks[4], (2 * S - 1, H), dtype=jnp.float32) * 0.02
        gamma = jnp.ones((E,), dtype=jnp.float32)
        beta = jnp.zeros((E,), dtype=jnp.float32)
        return {'x': x, 'Wq': Wq, 'Wk': Wk, 'Wv': Wv, 'rel_table': rel_table, 'gamma': gamma, 'beta': beta}
    _L0_attn_all = _L0_attn_setup()
    _L0_attn_in = {k: v for k, v in _L0_attn_all.items() if k in ('Wq', 'Wk', 'Wv', 'rel_table', 'gamma', 'beta')}
    del _L0_attn_all

    def _L0_xattn_setup():
        import jax, jax.numpy as jnp
        import numpy as np
        N_HEADS = 16
        DIM_EMBED = 128
        DIM_CROSS = 96
        DIM_HEAD = DIM_EMBED // N_HEADS
        key = jax.random.key(seed)
        ks = jax.random.split(key, 10)
        B, Sq, Sk = (8, 512, 77)
        s_e = 1.0 / np.sqrt(DIM_EMBED)
        s_c = 1.0 / np.sqrt(DIM_CROSS)
        return {'x': jax.random.normal(ks[0], (B, Sq, DIM_EMBED), jnp.float32), 'y': jax.random.normal(ks[1], (B, Sk, DIM_CROSS), jnp.float32), 'wq': jax.random.normal(ks[2], (DIM_EMBED, DIM_EMBED), jnp.float32) * s_e, 'bq': jax.random.normal(ks[3], (DIM_EMBED,), jnp.float32) * 0.01, 'wk': jax.random.normal(ks[4], (DIM_CROSS, DIM_EMBED), jnp.float32) * s_c, 'bk': jax.random.normal(ks[5], (DIM_EMBED,), jnp.float32) * 0.01, 'wv': jax.random.normal(ks[6], (DIM_CROSS, DIM_EMBED), jnp.float32) * s_c, 'bv': jax.random.normal(ks[7], (DIM_EMBED,), jnp.float32) * 0.01, 'wo': jax.random.normal(ks[8], (DIM_EMBED, DIM_EMBED), jnp.float32) * s_e, 'bo': jax.random.normal(ks[9], (DIM_EMBED,), jnp.float32) * 0.01}
    _L0_xattn_all = _L0_xattn_setup()
    _L0_xattn_in = {k: v for k, v in _L0_xattn_all.items() if k in ('wq', 'bq', 'wk', 'bk', 'wv', 'bv', 'wo', 'bo')}
    del _L0_xattn_all

    def _L0_ffn_setup():
        import jax, jax.numpy as jnp
        import numpy as np
        D_MODEL = 128
        M = 64
        INNER = 16
        key = jax.random.key(seed)
        ks = jax.random.split(key, 9)

        def init(k, shape, fan_in):
            bound = 1.0 / np.sqrt(fan_in)
            return jax.random.uniform(k, shape, jnp.float32, -bound, bound)
        x = jax.random.normal(ks[0], (16, 512, D_MODEL), dtype=jnp.float32)
        Win = init(ks[1], (D_MODEL, M), D_MODEL)
        bin_ = init(ks[2], (M,), D_MODEL)
        W1 = init(ks[3], (M, INNER), 1)
        b1 = init(ks[4], (M, INNER), 1)
        W2 = init(ks[5], (M, INNER), INNER)
        b2 = init(ks[6], (M,), INNER)
        Wout = init(ks[7], (M, D_MODEL), M)
        bout = init(ks[8], (D_MODEL,), M)
        return {'x': x, 'Win': Win, 'bin_': bin_, 'W1': W1, 'b1': b1, 'W2': W2, 'b2': b2, 'Wout': Wout, 'bout': bout}
    _L0_ffn_all = _L0_ffn_setup()
    _L0_ffn_in = {k: v for k, v in _L0_ffn_all.items() if k in ('Win', 'bin_', 'W1', 'b1', 'W2', 'b2', 'Wout', 'bout')}
    del _L0_ffn_all

    def _L1_attn_setup():
        import jax, jax.numpy as jnp
        import numpy as np
        B, T, C, H = (2, 256, 128, 16)
        D = C // H

        def _alibi_slopes(n_heads):
            return 2.0 ** (-(8.0 / n_heads) * jnp.arange(1, n_heads + 1, dtype=jnp.float32))
        key = jax.random.key(seed)
        k1, k2, k3 = jax.random.split(key, 3)
        return {'x': jax.random.normal(k1, (B, T, C), dtype=jnp.float32), 'w_attn': jax.random.normal(k2, (C, 3 * C), dtype=jnp.float32) * 0.02, 'b_attn': jnp.zeros((3 * C,), dtype=jnp.float32), 'w_proj': jax.random.normal(k3, (C, C), dtype=jnp.float32) * 0.02, 'b_proj': jnp.zeros((C,), dtype=jnp.float32)}
    _L1_attn_all = _L1_attn_setup()
    _L1_attn_in = {k: v for k, v in _L1_attn_all.items() if k in ('w_attn', 'b_attn', 'w_proj', 'b_proj')}
    del _L1_attn_all

    def _L1_xattn_setup():
        import jax, jax.numpy as jnp
        import numpy as np
        import math
        E = 128
        EV = 128
        FFN = 512
        DINO = 96
        B, S, P = (64, 64, 32)

        def bitnet_linear(x, W, b):
            w_scale = jnp.maximum(jnp.mean(jnp.abs(W)), 1e-05)
            qW = jnp.sign(W) * (jnp.abs(W) > 0.5 * w_scale).astype(W.dtype)
            i_scale = jnp.maximum(jnp.max(jnp.abs(x)), 1e-08) / 127.0
            qx = jnp.clip(jnp.round(x / i_scale), -128.0, 127.0)
            out = jnp.einsum('...i,oi->...o', qx, qW) * (w_scale * i_scale)
            return out + b
        key = jax.random.key(seed)
        ks = iter(jax.random.split(key, 32))

        def lin_w(fin, fout):
            return jax.random.normal(next(ks), (fout, fin), jnp.float32) * math.sqrt(2.0 / fin)
        return {'text_embeddings': jax.random.normal(next(ks), (B, S, E), jnp.float32), 'dinov2_features': jax.random.normal(next(ks), (B, P, DINO), jnp.float32), 'W_d2v': lin_w(DINO, EV), 'b_d2v': jnp.zeros((EV,), jnp.float32), 'W_img': lin_w(EV, E), 'b_img': jnp.zeros((E,), jnp.float32), 'W_txt': lin_w(E, E), 'b_txt': jnp.zeros((E,), jnp.float32), 'W_att0': lin_w(E, E // 2), 'b_att0': jnp.zeros((E // 2,), jnp.float32), 'W_att1': lin_w(E, E // 2), 'b_att1': jnp.zeros((E // 2,), jnp.float32), 'W_f1': lin_w(2 * E, FFN), 'b_f1': jnp.zeros((FFN,), jnp.float32), 'W_f2': lin_w(FFN, E), 'b_f2': jnp.zeros((E,), jnp.float32)}
    _L1_xattn_all = _L1_xattn_setup()
    _L1_xattn_in = {k: v for k, v in _L1_xattn_all.items() if k in ('W_d2v', 'b_d2v', 'W_img', 'b_img', 'W_txt', 'b_txt', 'W_att0', 'b_att0', 'W_att1', 'b_att1', 'W_f1', 'b_f1', 'W_f2', 'b_f2')}
    del _L1_xattn_all

    def _L1_ffn_setup():
        import jax, jax.numpy as jnp
        import numpy as np
        HIDDEN = 128
        N_ROUTED = 16
        N_SHARED = 2
        TOP_K = 2
        MID_R = HIDDEN // 4
        MID_S = HIDDEN // 2
        key = jax.random.key(seed)
        ks = jax.random.split(key, 8)
        s = 0.02
        return {'x': jax.random.normal(ks[0], (2, 128, HIDDEN), dtype=jnp.float32), 'router_w': jax.random.normal(ks[1], (HIDDEN, N_ROUTED), dtype=jnp.float32) * s, 'wg_r': jax.random.normal(ks[2], (N_ROUTED, HIDDEN, MID_R), dtype=jnp.float32) * s, 'wu_r': jax.random.normal(ks[3], (N_ROUTED, HIDDEN, MID_R), dtype=jnp.float32) * s, 'wd_r': jax.random.normal(ks[4], (N_ROUTED, MID_R, HIDDEN), dtype=jnp.float32) * s, 'wg_s': jax.random.normal(ks[5], (N_SHARED, HIDDEN, MID_S), dtype=jnp.float32) * s, 'wu_s': jax.random.normal(ks[6], (N_SHARED, HIDDEN, MID_S), dtype=jnp.float32) * s, 'wd_s': jax.random.normal(ks[7], (N_SHARED, MID_S, HIDDEN), dtype=jnp.float32) * s}
    _L1_ffn_all = _L1_ffn_setup()
    _L1_ffn_in = {k: v for k, v in _L1_ffn_all.items() if k in ('router_w', 'wg_r', 'wu_r', 'wd_r', 'wg_s', 'wu_s', 'wd_s')}
    del _L1_ffn_all
    return {'x': x, 'ctx_768': ctx_768, 'L0_attn_Wq': _L0_attn_in['Wq'], 'L0_attn_Wk': _L0_attn_in['Wk'], 'L0_attn_Wv': _L0_attn_in['Wv'], 'L0_attn_rel_table': _L0_attn_in['rel_table'], 'L0_attn_gamma': _L0_attn_in['gamma'], 'L0_attn_beta': _L0_attn_in['beta'], 'L0_xattn_wq': _L0_xattn_in['wq'], 'L0_xattn_bq': _L0_xattn_in['bq'], 'L0_xattn_wk': _L0_xattn_in['wk'], 'L0_xattn_bk': _L0_xattn_in['bk'], 'L0_xattn_wv': _L0_xattn_in['wv'], 'L0_xattn_bv': _L0_xattn_in['bv'], 'L0_xattn_wo': _L0_xattn_in['wo'], 'L0_xattn_bo': _L0_xattn_in['bo'], 'L0_ffn_Win': _L0_ffn_in['Win'], 'L0_ffn_bin_': _L0_ffn_in['bin_'], 'L0_ffn_W1': _L0_ffn_in['W1'], 'L0_ffn_b1': _L0_ffn_in['b1'], 'L0_ffn_W2': _L0_ffn_in['W2'], 'L0_ffn_b2': _L0_ffn_in['b2'], 'L0_ffn_Wout': _L0_ffn_in['Wout'], 'L0_ffn_bout': _L0_ffn_in['bout'], 'L1_attn_w_attn': _L1_attn_in['w_attn'], 'L1_attn_b_attn': _L1_attn_in['b_attn'], 'L1_attn_w_proj': _L1_attn_in['w_proj'], 'L1_attn_b_proj': _L1_attn_in['b_proj'], 'L1_xattn_W_d2v': _L1_xattn_in['W_d2v'], 'L1_xattn_b_d2v': _L1_xattn_in['b_d2v'], 'L1_xattn_W_img': _L1_xattn_in['W_img'], 'L1_xattn_b_img': _L1_xattn_in['b_img'], 'L1_xattn_W_txt': _L1_xattn_in['W_txt'], 'L1_xattn_b_txt': _L1_xattn_in['b_txt'], 'L1_xattn_W_att0': _L1_xattn_in['W_att0'], 'L1_xattn_b_att0': _L1_xattn_in['b_att0'], 'L1_xattn_W_att1': _L1_xattn_in['W_att1'], 'L1_xattn_b_att1': _L1_xattn_in['b_att1'], 'L1_xattn_W_f1': _L1_xattn_in['W_f1'], 'L1_xattn_b_f1': _L1_xattn_in['b_f1'], 'L1_xattn_W_f2': _L1_xattn_in['W_f2'], 'L1_xattn_b_f2': _L1_xattn_in['b_f2'], 'L1_ffn_router_w': _L1_ffn_in['router_w'], 'L1_ffn_wg_r': _L1_ffn_in['wg_r'], 'L1_ffn_wu_r': _L1_ffn_in['wu_r'], 'L1_ffn_wd_r': _L1_ffn_in['wd_r'], 'L1_ffn_wg_s': _L1_ffn_in['wg_s'], 'L1_ffn_wu_s': _L1_ffn_in['wu_s'], 'L1_ffn_wd_s': _L1_ffn_in['wd_s']}

def reference(x, ctx_768, L0_attn_Wq, L0_attn_Wk, L0_attn_Wv, L0_attn_rel_table, L0_attn_gamma, L0_attn_beta, L0_xattn_wq, L0_xattn_bq, L0_xattn_wk, L0_xattn_bk, L0_xattn_wv, L0_xattn_bv, L0_xattn_wo, L0_xattn_bo, L0_ffn_Win, L0_ffn_bin_, L0_ffn_W1, L0_ffn_b1, L0_ffn_W2, L0_ffn_b2, L0_ffn_Wout, L0_ffn_bout, L1_attn_w_attn, L1_attn_b_attn, L1_attn_w_proj, L1_attn_b_proj, L1_xattn_W_d2v, L1_xattn_b_d2v, L1_xattn_W_img, L1_xattn_b_img, L1_xattn_W_txt, L1_xattn_b_txt, L1_xattn_W_att0, L1_xattn_b_att0, L1_xattn_W_att1, L1_xattn_b_att1, L1_xattn_W_f1, L1_xattn_b_f1, L1_xattn_W_f2, L1_xattn_b_f2, L1_ffn_router_w, L1_ffn_wg_r, L1_ffn_wu_r, L1_ffn_wd_r, L1_ffn_wg_s, L1_ffn_wu_s, L1_ffn_wd_s):
    import jax
    import jax.numpy as jnp

    def _L0_attn_ref(x, Wq, Wk, Wv, rel_table, gamma, beta):
        import jax, jax.numpy as jnp
        import numpy as np
        B, S, E, H = (8, 128, 128, 16)
        EPS = 0.001
        b, s, e = x.shape
        h = rel_table.shape[1]
        scale = e ** (-0.5)

        def split_heads(t):
            return t.reshape(b, s, h, -1).transpose(0, 2, 1, 3)
        q = split_heads(x @ Wq)
        k = split_heads(x @ Wk)
        v = split_heads(x @ Wv)
        attn = jnp.einsum('bhqd,bhkd->bhqk', q, k) * scale
        attn = jax.nn.softmax(attn, axis=-1)
        r = jnp.arange(s)
        rel_index = jnp.clip(r[None, :] - r[:, None] + (s - 1), 0, 2 * s - 2)
        bias = rel_table[rel_index]
        bias = bias.reshape(-1).reshape(h, s, s)
        attn = attn + bias[None]
        out = jnp.einsum('bhqk,bhkd->bhqd', attn, v)
        out = out.transpose(0, 2, 1, 3).reshape(b, s, e)
        mu = jnp.mean(out, axis=-1, keepdims=True)
        var = jnp.var(out, axis=-1, keepdims=True)
        out = (out - mu) / jnp.sqrt(var + EPS) * gamma + beta
        return out

    def _L0_xattn_ref(x, y, wq, bq, wk, bk, wv, bv, wo, bo):
        import jax, jax.numpy as jnp
        import numpy as np
        N_HEADS = 16
        DIM_EMBED = 128
        DIM_CROSS = 96
        DIM_HEAD = DIM_EMBED // N_HEADS
        B, Sq, E = x.shape
        H, D = (N_HEADS, DIM_HEAD)
        q = (x @ wq + bq).reshape(B, Sq, H, D).transpose(0, 2, 1, 3)
        k = (y @ wk + bk).reshape(B, -1, H, D).transpose(0, 2, 1, 3)
        v = (y @ wv + bv).reshape(B, -1, H, D).transpose(0, 2, 1, 3)
        scores = jnp.einsum('bhqd,bhkd->bhqk', q, k) / jnp.sqrt(jnp.asarray(D, x.dtype))
        attn = jax.nn.softmax(scores, axis=-1)
        out = jnp.einsum('bhqk,bhkd->bhqd', attn, v)
        out = out.transpose(0, 2, 1, 3).reshape(B, Sq, E)
        return out @ wo + bo

    def _L0_ffn_ref(x, Win, bin_, W1, b1, W2, b2, Wout, bout):
        import jax, jax.numpy as jnp
        import numpy as np
        D_MODEL = 128
        M = 64
        INNER = 16
        s = jnp.einsum('btd,dm->btm', x, Win) + bin_
        h = jax.nn.relu(s[..., None] * W1 + b1)
        g = jnp.einsum('btmh,mh->btm', h, W2) + b2
        out = jnp.einsum('btm,md->btd', g, Wout) + bout
        return out

    def _L1_attn_ref(x, w_attn, b_attn, w_proj, b_proj):
        import jax, jax.numpy as jnp
        import numpy as np
        B, T, C, H = (2, 256, 128, 16)
        D = C // H

        def _alibi_slopes(n_heads):
            return 2.0 ** (-(8.0 / n_heads) * jnp.arange(1, n_heads + 1, dtype=jnp.float32))
        b, t, c = x.shape
        qkv = (x @ w_attn + b_attn).reshape(b, t, 3, H, D).transpose(2, 0, 3, 1, 4)
        q, k, v = (qkv[0], qkv[1], qkv[2])
        scores = jnp.einsum('bhtd,bhsd->bhts', q, k) / jnp.sqrt(jnp.float32(D))
        slopes = _alibi_slopes(H)
        pos = jnp.arange(t, dtype=scores.dtype)
        scores = scores + slopes[None, :, None, None] * pos[None, None, None, :]
        causal = jnp.tril(jnp.ones((t, t), dtype=bool))
        scores = jnp.where(causal[None, None], scores, -jnp.inf)
        attn = jax.nn.softmax(scores, axis=-1)
        y = jnp.einsum('bhts,bhsd->bhtd', attn, v)
        y = y.transpose(0, 2, 1, 3).reshape(b, t, c)
        return y @ w_proj + b_proj

    def _L1_xattn_ref(text_embeddings, dinov2_features, W_d2v, b_d2v, W_img, b_img, W_txt, b_txt, W_att0, b_att0, W_att1, b_att1, W_f1, b_f1, W_f2, b_f2):
        import jax, jax.numpy as jnp
        import numpy as np
        import math
        E = 128
        EV = 128
        FFN = 512
        DINO = 96
        B, S, P = (64, 64, 32)

        def bitnet_linear(x, W, b):
            w_scale = jnp.maximum(jnp.mean(jnp.abs(W)), 1e-05)
            qW = jnp.sign(W) * (jnp.abs(W) > 0.5 * w_scale).astype(W.dtype)
            i_scale = jnp.maximum(jnp.max(jnp.abs(x)), 1e-08) / 127.0
            qx = jnp.clip(jnp.round(x / i_scale), -128.0, 127.0)
            out = jnp.einsum('...i,oi->...o', qx, qW) * (w_scale * i_scale)
            return out + b
        b, s, e = text_embeddings.shape
        vis = bitnet_linear(dinov2_features, W_d2v, b_d2v)
        image_embeds = bitnet_linear(vis, W_img, b_img)
        fused = bitnet_linear(text_embeddings, W_txt, b_txt)
        inv_sqrt_e = 1.0 / math.sqrt(e)
        for Wa, ba in ((W_att0, b_att0), (W_att1, b_att1)):
            kv = bitnet_linear(image_embeds, Wa, ba)
            k = jnp.concatenate([kv, kv], axis=-1)
            scores = jnp.einsum('bse,bpe->bsp', fused, k) * inv_sqrt_e
            attn = jax.nn.softmax(scores, axis=-1)
            fused = fused + 0.1 * jnp.einsum('bsp,bpe->bse', attn, k)
        avg_img = jnp.mean(image_embeds, axis=1, keepdims=True)
        concatenated = jnp.concatenate([fused, jnp.broadcast_to(avg_img, (b, s, e))], axis=-1)
        h = jax.nn.relu(bitnet_linear(concatenated, W_f1, b_f1))
        return bitnet_linear(h, W_f2, b_f2)

    def _L1_ffn_ref(x, router_w, wg_r, wu_r, wd_r, wg_s, wu_s, wd_s):
        import jax, jax.numpy as jnp
        import numpy as np
        HIDDEN = 128
        N_ROUTED = 16
        N_SHARED = 2
        TOP_K = 2
        MID_R = HIDDEN // 4
        MID_S = HIDDEN // 2
        orig_shape = x.shape
        flat = x.reshape(-1, orig_shape[-1])
        gs = jnp.einsum('td,ndm->tnm', flat, wg_s)
        us = jnp.einsum('td,ndm->tnm', flat, wu_s)
        out = jnp.einsum('tnm,nmd->td', jax.nn.silu(gs) * us, wd_s)
        logits = (flat @ router_w).astype(jnp.float32)
        probs = jax.nn.softmax(logits, axis=-1)
        weights, indices = jax.lax.top_k(probs, TOP_K)
        weights = weights / (weights.sum(axis=-1, keepdims=True) + 1e-09)
        weights = weights.astype(x.dtype)
        comb = jnp.sum(jax.nn.one_hot(indices, N_ROUTED, dtype=x.dtype) * weights[..., None], axis=1)
        g = jnp.einsum('td,edm->tem', flat, wg_r)
        u = jnp.einsum('td,edm->tem', flat, wu_r)
        h = jax.nn.silu(g) * u
        h = h * comb[:, :, None]
        out = out + jnp.einsum('tem,emd->td', h, wd_r)
        return out.reshape(orig_shape)
    x = x + _L0_attn_ref(_layernorm(x, axis=-1), L0_attn_Wq, L0_attn_Wk, L0_attn_Wv, L0_attn_rel_table, L0_attn_gamma, L0_attn_beta)
    x = x + _L0_xattn_ref(_layernorm(x, axis=-1), ctx_768, L0_xattn_wq, L0_xattn_bq, L0_xattn_wk, L0_xattn_bk, L0_xattn_wv, L0_xattn_bv, L0_xattn_wo, L0_xattn_bo)
    x = x + _L0_ffn_ref(_layernorm(x, axis=-1), L0_ffn_Win, L0_ffn_bin_, L0_ffn_W1, L0_ffn_b1, L0_ffn_W2, L0_ffn_b2, L0_ffn_Wout, L0_ffn_bout)
    x = x + _L1_attn_ref(_layernorm(x, axis=-1), L1_attn_w_attn, L1_attn_b_attn, L1_attn_w_proj, L1_attn_b_proj)
    x = x + _L1_xattn_ref(_layernorm(x, axis=-1), ctx_768, L1_xattn_W_d2v, L1_xattn_b_d2v, L1_xattn_W_img, L1_xattn_b_img, L1_xattn_W_txt, L1_xattn_b_txt, L1_xattn_W_att0, L1_xattn_b_att0, L1_xattn_W_att1, L1_xattn_b_att1, L1_xattn_W_f1, L1_xattn_b_f1, L1_xattn_W_f2, L1_xattn_b_f2)
    x = x + _L1_ffn_ref(_layernorm(x, axis=-1), L1_ffn_router_w, L1_ffn_wg_r, L1_ffn_wu_r, L1_ffn_wd_r, L1_ffn_wg_s, L1_ffn_wu_s, L1_ffn_wd_s)
    return x

_drawn_inputs = setup_inputs


def setup_inputs(seed=0):
    import zlib

    import numpy as np

    out = dict(_drawn_inputs(seed))
    spreads = {'L0_attn_gamma': (1.0, 0.2),
     'L0_attn_beta': (0.0, 0.1),
     'L1_attn_b_attn': (0.0, 0.474),
     'L1_attn_b_proj': (0.0, 0.1),
     'L1_xattn_b_d2v': (0.0, 0.321),
     'L1_xattn_b_img': (0.0, 0.1),
     'L1_xattn_b_txt': (0.0, 0.1),
     'L1_xattn_b_att0': (0.0, 0.8),
     'L1_xattn_b_att1': (0.0, 0.8),
     'L1_xattn_b_f1': (0.0, 0.1),
     'L1_xattn_b_f2': (0.0, 0.1)}
    factors = {'L0_attn_Wq': 7.08,
     'L0_attn_Wk': 7.109,
     'L0_xattn_bq': 8.0,
     'L0_xattn_bk': 8.0,
     'L0_xattn_bv': 6.262,
     'L0_xattn_bo': 5.943,
     'L0_ffn_bin_': 8.0,
     'L1_xattn_W_att0': 3.729,
     'L1_xattn_W_att1': 3.941,
     'L1_ffn_router_w': 8.0,
     'L1_ffn_wg_r': 8.0,
     'L1_ffn_wu_r': 8.0,
     'L1_ffn_wd_r': 8.0,
     'L1_ffn_wg_s': 8.0,
     'L1_ffn_wu_s': 8.0,
     'L1_ffn_wd_s': 8.0}
    for name, (base, spread) in spreads.items():
        noise = np.random.default_rng([zlib.crc32(name.encode()), seed]).standard_normal(out[name].shape)
        drawn = base * np.exp(spread * noise) if base else spread * noise
        out[name] = jnp.asarray(drawn.astype(out[name].dtype))
    for name, factor in factors.items():
        out[name] = (out[name] * factor).astype(out[name].dtype)
    return out
```

```python
import concourse.bass as bass
from concourse import mybir
from contextlib import ExitStack

F32 = mybir.dt.float32
BF16 = mybir.dt.bfloat16
ACT = mybir.ActivationFunctionType
ALU = mybir.AluOpType
AX = mybir.AxisListType

P = 128
BATCH, SEQ, DIM, CTX = 128, 64, 128, 96
TOK = BATCH * SEQ
NT = TOK // P
NG = TOK // 512
HEADS, HD = 16, 8
PAIRS = HEADS // 2
VW = HD + 1
M_SHRINK, INNER = 64, 16
FFN = 512
EXPERTS, MID = 16, 32
HID_MOE = EXPERTS * MID + 2 * 64
LN_EPS = 1e-5
ROUND = 12582912.0

LAYERS = ("a0", "x0", "a1")


def after(eng, sem, count):
    if isinstance(count, int) and count <= 0:
        return
    eng.wait_ge(sem, count)


def tile_of(step, lag):
    t = step - lag
    if isinstance(t, int) and not 0 <= t < NT:
        return None
    return t


def run_steps(eng, body, last_lag):
    for s in range(8):
        body(s, s)
    with eng.Fori(2, NT // 4) as q:
        for u in range(4):
            body(q * 4 + u, u)
    for s in range(NT, NT + last_lag):
        body(s, s)


def load_inputs(nc, sb, sem, d):
    loaded, ctx_loaded = sem("loaded"), sem("ctx_loaded")
    with nc.Block() as block:
        @block.sync
        def _(sp):
            n = 0
            for c in range(4):
                sp.dma_start(sb["x"][:, 16 * c:16 * c + 16, :], d["x"][:, 16 * c:16 * c + 16, :]).then_inc(loaded, 16)
                n += 16
            for name in d["_small"]:
                sp.dma_start(sb[name][:], d[name]).then_inc(loaded, 16)
                n += 16
            sp.wait_ge(loaded, n)

        @block.scalar
        def _(act):
            act.dma_start(sb["G1"][0:CTX, :], d["ctxT"]).then_inc(ctx_loaded, 16)
            act.wait_ge(ctx_loaded, 16)


def set_constants(nc, sb, sem):
    made = sem("made")
    with nc.Block() as block:
        @block.vector
        def _(dve):
            dve.memset(sb["ones_row"][:], 1.0)
            dve.memset(sb["zeros"][:], 0.0)
            dve.memset(sb["vblk"][:], 0.0).then_inc(made, 1)
            dve.wait_ge(made, 1)
            for i in range(2):
                h = slice(64 * i, 64 * i + 64)
                dve.memset(sb["vblk"][h, :, :, i * VW + HD:i * VW + VW], 1.0)
            for layer, scale in (("x0", HD ** -0.5), ("a1", HD ** -0.5)):
                dve.tensor_scalar(sb["bqs_" + layer][:], sb["bq_" + layer][:], scale, None, ALU.mult)


def first_stats(nc, sb, sem):
    with nc.Block() as block:
        @block.vector
        def _(dve):
            with dve.Fori(0, NT // 2) as q:
                for u in range(2):
                    t = q * 2 + u
                    dve.bn_stats(sb["st6"][:, t, :], sb["x"][:, t, :])


def settle(dve, sb, sem, count):
    after(dve, sem, count)
    dve.memset(sb["scratch"][:], 0.0)


def mean_and_rstd(nc, sb, sem, name, eps):
    s_in, s_d, s_v, s_rooted = (sem(name + n) for n in ("_halves", "_squares", "_variance", "_rooted"))
    st6, mean, rstd, dif, var = (sb[n] for n in ("st6", "mean", "rstd", "dif", "var"))
    with nc.Block() as block:
        @block.vector
        def _(dve):
            dve.tensor_tensor(mean[:], st6[:, :, 1], st6[:, :, 4], ALU.add)
            dve.tensor_tensor(dif[:], st6[:, :, 1], st6[:, :, 4], ALU.subtract)
            dve.tensor_tensor(var[:], st6[:, :, 2], st6[:, :, 5], ALU.add).then_inc(s_in, 1)
            dve.wait_ge(s_in, 1)
            dve.tensor_scalar(mean[:], mean[:], 0.5, None, ALU.mult)
            dve.tensor_tensor(dif[:], dif[:], dif[:], ALU.mult)
            dve.tensor_scalar(var[:], var[:], 1.0 / DIM, eps, ALU.mult, ALU.add).then_inc(s_d, 1)
            dve.wait_ge(s_d, 1)
            dve.scalar_tensor_tensor(out=var[:], in0=dif[:], scalar=0.25, in1=var[:], op0=ALU.mult,
                                     op1=ALU.add).then_inc(s_v, 1)
            dve.wait_ge(s_rooted, 1)
            dve.reciprocal(rstd[:], rstd[:])

        @block.scalar
        def _(act):
            act.wait_ge(s_v, 1)
            act.activation(rstd[:], var[:], ACT.Sqrt).then_inc(s_rooted, 1)


def attention(nc, sb, ps, sem, layer):
    cross, causal, plain = layer == "x0", layer == "a1", layer == "a0"
    S = lambda n: sem(n + "_" + layer)
    s_norm, s_ctx, s_turn, s_ht, s_proj = S("normed"), S("ctx_copied"), S("turned"), S("ht_ready"), S("projected")
    s_q, s_k, s_v = S("q_ready"), S("k_ready"), S("v_ready")
    s_sc, s_max, s_add, s_sub = S("scored"), S("maxed"), S("alibi_added"), S("shifted")
    s_exp, s_pt, s_pe, s_mix = S("exp_ready"), S("p_turned"), S("pt_ready"), S("mixed")
    s_rec, s_y, s_yb = S("sum_inverted"), S("y_ready"), S("y_biased")
    s_yt, s_yc, s_out, s_x = S("y_turned"), S("yt_ready"), S("out_ready"), S("x_updated")
    x, mean, rstd, ctxT, ao = sb["x"], sb["mean"], sb["rstd"], sb["G1"], sb["G3v"]
    wq, wk, wv = sb["wq_" + layer], sb["wk_" + layer], sb["wv_" + layer]
    bk, bv = sb["bk_" + layer], sb["bv_" + layer]
    xn, hT, cT, qT, km, vb = sb["xn"], sb["hT"], sb["cT"], sb["qT"], sb["km"], sb["vblk"]
    sx, pt, y, yT, nmx, rec = sb["sx"], sb["pt"], sb["y"], sb["yT"], sb["nmx"], sb["rec"]
    SB, TB, PB, OB = ps[0:4], ps[4:6], ps[6], ps[7]
    LAST = 6 if plain else 7
    KIN = CTX if cross else P
    scale = DIM ** -0.5 if plain else HD ** -0.5

    with nc.Block() as block:
        @block.tensor
        def _(pe):
            def turn(t, k):
                pe.wait_ge(s_norm, t + 1)
                after(pe, s_q, t)
                after(pe, s_k, t)
                after(pe, s_v, t)
                pe.transpose(PB[:, 384:512], xn[:, k % 2, :], sb["ident"][:]).then_inc(s_turn, 1)

            def project(t, k):
                pe.wait_ge(s_ht, t + 1)
                if cross:
                    pe.wait_ge(s_ctx, t + 1)
                src = cT[0:CTX, k % 4, :] if cross else hT[:, k % 2, :]
                pe.matmul(PB[:, 0:128], lhsT=wq[:], rhs=hT[:, k % 2, :], start=True, stop=True)
                pe.matmul(PB[:, 128:256], lhsT=wk[:], rhs=src, start=True, stop=True)
                for b in range(2):
                    for i in range(2):
                        mm = pe.matmul(PB[64 * i:64 * i + 64, 256 + 64 * b:320 + 64 * b],
                                       lhsT=src[:, 64 * b:64 * b + 64], rhs=wv[:, i, :], start=True, stop=True)
                mm.then_inc(s_proj, 1)

            def score(t, k):
                pe.wait_ge(s_q, t + 1)
                pe.wait_ge(s_k, t + 1)
                for g in range(4):
                    after(pe, s_sub if not causal else s_add, 4 * (t - 1) + g + 1 if not isinstance(t, int) or t else 0)
                    r = slice(32 * g, 32 * g + 32)
                    for b in range(2):
                        mm = pe.matmul(SB[g][64 * b:64 * b + 64, 0:256], lhsT=qT[r, k % 2, 64 * b:64 * b + 64],
                                       rhs=km[r, k % 2, :, 64 * b:64 * b + 64], start=True, stop=True)
                    mm.then_inc(s_sc, 1)

            def turn_p(t, k):
                pe.wait_ge(s_exp, t + 1)
                after(pe, s_pe, 2 * t)
                for n in range(2):
                    for c in range(4):
                        mm = pe.transpose(TB[n][:, 128 * c:128 * c + 128],
                                          sx[:, k % 2, 512 * n + 128 * c:512 * n + 128 * c + 128], sb["ident"][:])
                    mm.then_inc(s_pt, 1)

            def mix(t, k):
                pe.wait_ge(s_pe, 2 * t + 2)
                pe.wait_ge(s_v, t + 1)
                after(pe, s_y, t)
                for c in range(PAIRS):
                    for b in range(2):
                        o = slice(64 * b, 64 * b + 64)
                        mm = pe.matmul(OB[o, 18 * c:18 * c + 18],
                                       lhsT=pt[:, k % 2, 128 * c + 64 * b:128 * c + 64 * b + 64],
                                       rhs=vb[:, k % 4, PAIRS * b + c, :], start=True, stop=True)
                        if plain:
                            mm = pe.matmul(OB[o, 256 + 18 * c:256 + 18 * c + 18], lhsT=sb["biasT"][:, c, :],
                                           rhs=vb[:, k % 4, PAIRS * b + c, :], start=True, stop=True)
                mm.then_inc(s_mix, 1)

            def turn_y(t, k):
                pe.wait_ge(s_y, t + 1)
                after(pe, s_x, t - 1)
                pe.transpose(OB[:, 144:272], y[:, k % 2, :], sb["ident"][:]).then_inc(s_yt, 1)

            def project_out(t, k):
                pe.wait_ge(s_yc, t + 1)
                after(pe, s_x, t)
                pe.matmul(OB[:, 384:512], lhsT=yT[:, k % 2, :], rhs=sb["wo_" + layer][:], start=True, stop=False)
                pe.matmul(OB[:, 384:512], lhsT=sb["ones_row"][:], rhs=sb["bo_" + layer][:],
                          start=False, stop=True).then_inc(s_out, 1)

            def step(s, k):
                t = tile_of(s, 2)
                if t is not None:
                    project(t, k - 2)
                t = tile_of(s, 6)
                if t is not None and not plain:
                    turn_y(t, k - 6)
                t = tile_of(s, 3)
                if t is not None:
                    score(t, k - 3)
                t = tile_of(s, 4)
                if t is not None:
                    turn_p(t, k - 4)
                if not plain:
                    t = tile_of(s, 6)
                    if t is not None:
                        pe.wait_ge(s_yc, t + 1)
                    t = tile_of(s, 7)
                    if t is not None:
                        project_out(t, k - 7)
                t = tile_of(s, 5)
                if t is not None:
                    if not plain:
                        after(pe, s_x, t - 2)
                    mix(t, k - 5)
                t = tile_of(s, 1)
                if t is not None:
                    turn(t, k - 1)

            run_steps(pe, step, LAST)

        @block.scalar
        def _(act):
            def copy_q(t, k):
                act.wait_ge(s_proj, t + 1)
                after(act, s_sc, 4 * (t - 1))
                if plain:
                    act.activation(qT[:, k % 2, :], PB[:, 0:128], ACT.Copy, scale=scale).then_inc(s_q, 1)
                else:
                    act.activation(qT[:, k % 2, :], PB[:, 0:128], ACT.Identity, bias=sb["bqs_" + layer][:, 0:1],
                                   scale=scale).then_inc(s_q, 1)

            def copy_yt(t, k):
                act.wait_ge(s_yt, t + 1)
                act.activation(yT[:, k % 2, :], OB[:, 144:272], ACT.Copy).then_inc(s_yc, 1)

            def copy_pt(t, k):
                after(act, s_mix, t - 1)
                for n in range(2):
                    act.wait_ge(s_pt, 2 * t + n + 1)
                    act.activation(pt[:, k % 2, 512 * n:512 * n + 512], TB[n][:, :], ACT.Copy).then_inc(s_pe, 1)

            def exps(t, k):
                act.wait_ge(s_sub, 4 * t + 4)
                act.activation(sx[:, k % 2, :], sx[:, k % 2, :], ACT.Exp).then_inc(s_exp, 1)

            def copy_ht(t, k):
                act.wait_ge(s_turn, t + 1)
                after(act, s_proj, t - 1)
                act.activation(hT[:, k % 2, :], PB[:, 384:512], ACT.Copy).then_inc(s_ht, 1)

            def step(s, k):
                t = tile_of(s, 2)
                if t is not None:
                    copy_q(t, k - 2)
                t = tile_of(s, 6)
                if t is not None and not plain:
                    copy_yt(t, k - 6)
                t = tile_of(s, 4)
                if t is not None:
                    copy_pt(t, k - 4)
                t = tile_of(s, 3)
                if t is not None:
                    exps(t, k - 3)
                t = tile_of(s, 1)
                if t is not None:
                    copy_ht(t, k - 1)

            run_steps(act, step, LAST)

        @block.vector
        def _(dve):
            def normalise(t, k):
                after(dve, s_turn, t - 1)
                dve.tensor_scalar(xn[:, k % 2, :], x[:, t, :], mean[:, bass.ds(t, 1)], rstd[:, bass.ds(t, 1)],
                                  ALU.subtract, ALU.mult).then_inc(s_norm, 1)

            def copy_k(t, k):
                dve.wait_ge(s_q, t + 1)
                after(dve, s_sc, 4 * (t - 1))
                dve.scalar_tensor_tensor(
                    out=km[:, k % 2, :, :], in0=PB[:, 128:256].unsqueeze(1).to_broadcast([P, 4, P]),
                    scalar=bk[:, 0:1], in1=sb["head_mask"][:].unsqueeze(2).to_broadcast([P, 4, P]),
                    op0=ALU.add, op1=ALU.mult).then_inc(s_k, 1)

            def copy_v(t, k):
                after(dve, s_mix, t - 3)
                for i in range(2):
                    r = slice(64 * i, 64 * i + 64)
                    ins = dve.tensor_tensor(
                        vb[r, k % 4, :, i * VW:i * VW + HD],
                        PB[r, 256:384].rearrange("p (n d) -> p n d", d=HD),
                        bv[r, :].rearrange("p (n d) -> p n d", d=HD), ALU.add)
                ins.then_inc(s_v, 1)

            def shift(t, k):
                after(dve, s_pt, 2 * (t - 1))
                if causal:
                    for g in range(4):
                        dve.wait_ge(s_sc, 4 * t + g + 1)
                        dve.tensor_tensor(sx[:, k % 2, 256 * g:256 * g + 256], SB[g][:, 0:256],
                                          sb["alibi"][:, 256 * g:256 * g + 256], ALU.add).then_inc(s_add, 1)
                    dve.wait_ge(s_add, 4 * t + 4)
                    v = sx[:, k % 2, :].rearrange("p (h k) -> p h k", k=SEQ)
                    dve.tensor_reduce(out=nmx[:, k % 2, :], in_=v, axis=AX.X, op=ALU.max).then_inc(s_max, 1)
                    dve.wait_ge(s_max, t + 1)
                    dve.tensor_tensor(v, v, nmx[:, k % 2, :].unsqueeze(2).to_broadcast([P, HEADS, SEQ]),
                                      ALU.subtract).then_inc(s_sub, 4)
                    return
                for g in range(4):
                    dve.wait_ge(s_sc, 4 * t + g + 1)
                    dve.tensor_reduce(out=nmx[:, k % 2, 4 * g:4 * g + 4],
                                      in_=SB[g][:, 0:256].rearrange("p (h k) -> p h k", k=SEQ),
                                      axis=AX.X, op=ALU.max).then_inc(s_max, 1)
                for g in range(4):
                    dve.wait_ge(s_max, 4 * t + g + 1)
                    dve.tensor_tensor(
                        sx[:, k % 2, 256 * g:256 * g + 256].rearrange("p (h k) -> p h k", k=SEQ),
                        SB[g][:, 0:256].rearrange("p (h k) -> p h k", k=SEQ),
                        nmx[:, k % 2, 4 * g:4 * g + 4].unsqueeze(2).to_broadcast([P, 4, SEQ]),
                        ALU.subtract).then_inc(s_sub, 1)

            def finish(t, k):
                dve.wait_ge(s_mix, t + 1)
                o = OB[:, 0:144].rearrange("p (h e) -> p h e", e=VW)
                dve.reciprocal(rec[:, k % 2, :], o[:, :, HD]).then_inc(s_rec, 1)
                dve.wait_ge(s_rec, t + 1)
                rb = rec[:, k % 2, :].unsqueeze(2).to_broadcast([P, HEADS, HD])
                if not plain:
                    after(dve, s_yt, t - 1)
                    dve.tensor_tensor(y[:, k % 2, :].rearrange("p (h d) -> p h d", d=HD), o[:, :, 0:HD], rb,
                                      ALU.mult).then_inc(s_y, 1)
                    return
                dve.tensor_tensor(y[:, k % 2, :].rearrange("p (h d) -> p h d", d=HD), o[:, :, 0:HD], rb,
                                  ALU.mult).then_inc(s_yb, 1)
                dve.wait_ge(s_yb, t + 1)
                dve.tensor_tensor(ao[:, t, :].rearrange("p (h d) -> p h d", d=HD),
                                  OB[:, 256:400].rearrange("p (h e) -> p h e", e=VW)[:, :, 0:HD],
                                  y[:, k % 2, :].rearrange("p (h d) -> p h d", d=HD), ALU.add).then_inc(s_y, 1)

            def update_x(t, k):
                dve.wait_ge(s_out, t + 1)
                dve.tensor_tensor(x[:, t, :], OB[:, 384:512], x[:, t, :], ALU.add).then_inc(s_x, 1)

            def stats(t, k, finished):
                if not finished:
                    dve.wait_ge(s_y if plain else s_x, t + 1)
                dve.bn_stats(sb["st6"][:, t, :], (ao if plain else x)[:, t, :])

            def step(s, k):
                t = tile_of(s, 2)
                if t is not None:
                    copy_k(t, k - 2)
                    copy_v(t, k - 2)
                t = tile_of(s, 3)
                if t is not None:
                    shift(t, k - 3)
                if not plain:
                    t = tile_of(s, 5)
                    if t is not None:
                        dve.wait_ge(s_mix, t + 1)
                    t = tile_of(s, 7)
                    if t is not None:
                        update_x(t, k - 7)
                t = tile_of(s, 5)
                if t is not None:
                    finish(t, k - 5)
                lag = 6 if plain else 7
                if tile_of(s, lag) is not None:
                    stats(tile_of(s, lag), k - lag, t is not None)
                t = tile_of(s, 0)
                if t is not None:
                    normalise(t, k)

            run_steps(dve, step, LAST)

        if cross:
            @block.gpsimd
            def _(pool):
                with pool.Fori(0, NT // 4) as q:
                    for u in range(4):
                        t = q * 4 + u
                        pool.wait_ge(s_norm, t + 1)
                        pool.wait_ge(s_turn, t + 1)
                        pool.tensor_copy(cT[0:CTX, u, :], ctxT[0:CTX, bass.ds(t * P, P)]).then_inc(s_ctx, 1)


def second_norm(nc, sb, sem):
    s_n, s_g, s_b, s_x = (sem(n) for n in ("o_normed", "o_scaled", "o_shifted", "o_added"))
    x, ao = sb["x"], sb["G3v"]
    tiles = lambda a, g: a[:, bass.ds(g * 4, 4), :]
    wide = lambda b: b[:].unsqueeze(1).to_broadcast([P, 4, DIM])
    with nc.Block() as block:
        @block.vector
        def _(dve):
            def scale(g, k):
                for j in range(4):
                    t = g * 4 + j
                    ins = dve.tensor_scalar(ao[:, t, :], ao[:, t, :], sb["mean"][:, bass.ds(t, 1)],
                                            sb["rstd"][:, bass.ds(t, 1)], ALU.subtract, ALU.mult)
                ins.then_inc(s_n, 1)
                dve.wait_ge(s_n, g + 1)
                dve.tensor_tensor(tiles(ao, g), tiles(ao, g), wide(sb["gammaB"]), ALU.mult).then_inc(s_g, 1)

            def add(g, k):
                dve.wait_ge(s_b, g + 1)
                dve.tensor_tensor(tiles(x, g), tiles(ao, g), tiles(x, g), ALU.add).then_inc(s_x, 1)
                settle(dve, sb, s_x, g + 1)
                stats_of_group(dve, sb, g)

            def step(s, k):
                for lag, do in ((0, scale), (1, add)):
                    g = group_of(s, lag)
                    if g is not None:
                        do(g, k - lag)

            run_groups(dve, step, 1)

        @block.gpsimd
        def _(pool):
            def shift(g, k):
                pool.wait_ge(s_g, g + 1)
                pool.tensor_tensor(tiles(ao, g), tiles(ao, g), wide(sb["betaB"]), ALU.add).then_inc(s_b, 1)

            run_groups(pool, shift, 0)


def store(nc, sb, sem, out):
    stored = sem("stored")
    with nc.Block() as block:
        @block.sync
        def _(sp):
            for c in range(4):
                sp.dma_start(out[:, 16 * c:16 * c + 16, :], sb["x"][:, 16 * c:16 * c + 16, :]).then_inc(stored, 16)
            sp.wait_ge(stored, 64)


def run_groups(eng, body, last_lag, unroll=2):
    for s in range(4):
        body(s, s)
    with eng.Fori(4 // unroll, NG // unroll) as q:
        for u in range(unroll):
            body(q * unroll + u, u)
    for s in range(NG, NG + last_lag):
        body(s, s)


def group_of(step, lag):
    g = step - lag
    if isinstance(g, int) and not 0 <= g < NG:
        return None
    return g


def normalise_group(dve, sb, g, k, done):
    for j in range(4):
        t = g * 4 + j
        ins = dve.tensor_scalar(sb["xn4"][:, k % 2, j, :], sb["x"][:, t, :], sb["mean"][:, bass.ds(t, 1)],
                                sb["rstd"][:, bass.ds(t, 1)], ALU.subtract, ALU.mult)
    ins.then_inc(done, 1)


def stats_of_group(dve, sb, g):
    for j in range(4):
        dve.bn_stats(sb["st6"][:, g * 4 + j, :], sb["x"][:, g * 4 + j, :])


def shrink_ffn(nc, sb, ps, sem):
    s_fold, s_row = sem("w2_folded"), sem("row_ready")
    s_norm, s_turn, s_ht, s_sh, s_sT = sem("f_normed"), sem("f_turned"), sem("f_ht_ready"), sem("f_shrunk"), sem("f_sT_ready")
    s_ex, s_hid, s_dn, s_x = (sem(n) for n in ("f_expanded", "f_hid_ready", "f_down", "f_x"))
    NC = M_SHRINK * INNER // P
    x4 = sb["x"][:].rearrange("p (g j) f -> p g (j f)", j=4)
    hid = sb["G3"][:].rearrange("p (r c n) -> p r c n", r=2, c=NC)
    EB, DB, TB, SB = ps[0:4], ps[4:6], ps[6], ps[7]

    with nc.Block() as block:
        @block.vector
        def _(dve):
            for c in range(NC):
                ins = dve.tensor_scalar(sb["w_out"][:, c, :], sb["w_out"][:, c, :], sb["w_2"][:, c:c + 1], None, ALU.mult)
            dve.wait_ge(s_fold, 1)
            dve.tensor_tensor(sb["row"][:], ps[0][0:1, 0:DIM], sb["b_out"][:], ALU.add)

        @block.tensor
        def _(pe):
            pe.matmul(ps[0][0:1, 0:DIM], lhsT=sb["b_2"][:], rhs=sb["w_outp"][:], start=True, stop=True).then_inc(s_fold, 1)

    with nc.Block() as block:
        @block.tensor
        def _(pe):
            def turn(g, k):
                pe.wait_ge(s_norm, g + 1)
                after(pe, s_ht, g)
                for j in range(4):
                    mm = pe.transpose(TB[:, P * j:P * j + P], sb["xn4"][:, k % 2, j, :], sb["ident"][:])
                mm.then_inc(s_turn, 1)

            def shrink(g, k):
                pe.wait_ge(s_ht, g + 1)
                after(pe, s_sT, g)
                pe.matmul(SB[0:M_SHRINK, :], lhsT=sb["w_in"][:], rhs=sb["hT4"][:, k % 2, :],
                          start=True, stop=True).then_inc(s_sh, 1)

            def expand(g, k):
                pe.wait_ge(s_sT, g + 1)
                for c in range(NC):
                    if c >= 4:
                        pe.wait_ge(s_hid, NC * g + c - 3)
                    else:
                        after(pe, s_hid, NC * g + c - 3)
                    pe.matmul(EB[c % 4][:, :], lhsT=sb["sel_e"][:, c, :], rhs=sb["sT"][0:M_SHRINK, k % 2, :],
                              start=True, stop=True).then_inc(s_ex, 1)

            def down(g, k):
                pe.wait_ge(s_hid, NC * (g + 1))
                after(pe, s_x, g - 1)
                for j in range(4):
                    o = DB[k % 2][:, DIM * j:DIM * j + DIM]
                    for c in range(NC):
                        pe.matmul(o, lhsT=hid[:, k % 2, c, P * j:P * j + P], rhs=sb["w_out"][:, c, :],
                                  start=(c == 0), stop=False)
                    mm = pe.matmul(o, lhsT=sb["ones_row"][:], rhs=sb["row"][:], start=False, stop=True)
                mm.then_inc(s_dn, 1)

            def step(s, k):
                for lag, do in ((2, shrink), (3, down), (2, expand), (1, turn)):
                    g = group_of(s, lag)
                    if g is not None:
                        do(g, k - lag)

            run_groups(pe, step, 4)

        @block.scalar
        def _(act):
            def copy_ht(g, k):
                act.wait_ge(s_turn, g + 1)
                after(act, s_sh, g - 1)
                act.activation(sb["hT4"][:, k % 2, :], TB[:, :], ACT.Copy).then_inc(s_ht, 1)

            def copy_sT(g, k):
                act.wait_ge(s_sh, g + 1)
                after(act, s_ex, NC * (g - 1))
                act.activation(sb["sT"][0:M_SHRINK, k % 2, :], SB[0:M_SHRINK, :], ACT.Identity,
                               bias=sb["b_in"][:, 0:1]).then_inc(s_sT, 1)

            def relus(g, k):
                after(act, s_dn, g - 1)
                for c in range(NC):
                    act.wait_ge(s_ex, NC * g + c + 1)
                    act.activation(hid[:, k % 2, c, :], EB[c % 4][:, :], ACT.Relu, bias=sb["b_1"][:, c:c + 1],
                                   scale=sb["w_1"][:, c:c + 1]).then_inc(s_hid, 1)

            def step(s, k):
                for lag, do in ((2, copy_sT), (2, relus), (1, copy_ht)):
                    g = group_of(s, lag)
                    if g is not None:
                        do(g, k - lag)

            run_groups(act, step, 4)

        @block.vector
        def _(dve):
            def normalise(g, k):
                after(dve, s_turn, g - 1)
                normalise_group(dve, sb, g, k, s_norm)

            def update(g, k):
                dve.wait_ge(s_dn, g + 1)
                dve.tensor_tensor(x4[:, g, :], DB[k % 2][:, :], x4[:, g, :], ALU.add).then_inc(s_x, 1)
                settle(dve, sb, s_x, g + 1)
                stats_of_group(dve, sb, g)

            def step(s, k):
                for lag, do in ((0, normalise), (3, update)):
                    g = group_of(s, lag)
                    if g is not None:
                        do(g, k - lag)

            run_groups(dve, step, 4)


WS = {n: i for i, n in enumerate(("d2v", "img", "txt", "att0", "att1", "f1", "f2"))}
WCOUNT = {"d2v": CTX * P, "img": P * P, "txt": P * P, "att0": P * P, "att1": P * P,
          "f1": 2 * P * FFN, "f2": P * FFN}


def weights_to_ternary(nc, sb, sem):
    s_zero, s_sum, s_all, s_scale, s_thr, s_lt = (sem(n) for n in ("q_zeroed", "q_summed", "q_all", "q_scaled", "q_thr", "q_lt"))
    names = list(WS)
    with nc.Block() as block:
        @block.vector
        def _(dve):
            dve.memset(sb["wsum"][:], 0.0).then_inc(s_zero, 1)
            dve.memset(sb["roundc"][:], ROUND)
            dve.memset(sb["stat"][:], 0.0)
            dve.wait_ge(s_zero, 1)
            for n in names:
                k = CTX if n == "d2v" else P
                ins = dve.tensor_reduce(out=sb["wsum"][0:k, WS[n]:WS[n] + 1], in_=sb["b_" + n][0:k, :], axis=AX.X,
                                        op=ALU.add, apply_absolute_value=True)
            ins.then_inc(s_sum, 1)
            dve.wait_ge(s_all, 1)
            for n in names:
                w = slice(WS[n], WS[n] + 1)
                ins = dve.tensor_scalar(sb["wscale"][:, w], sb["wall"][:, w], 1.0 / WCOUNT[n], 1e-5, ALU.mult, ALU.max)
            ins.then_inc(s_scale, 1)
            dve.wait_ge(s_scale, 1)
            dve.tensor_scalar(sb["wthr"][:], sb["wscale"][:], 0.5, None, ALU.mult)
            dve.tensor_scalar(sb["wnthr"][:], sb["wscale"][:], -0.5, None, ALU.mult).then_inc(s_thr, 1)
            dve.wait_ge(s_thr, 1)
            for i, n in enumerate(names):
                k = CTX if n == "d2v" else P
                w, width = slice(WS[n], WS[n] + 1), sb["b_" + n].shape[1]
                dve.tensor_scalar(sb["wtmp"][0:k, 0:width], sb["b_" + n][0:k, :], sb["wnthr"][0:k, w], None,
                                  ALU.is_lt).then_inc(s_lt, 1)
                dve.wait_ge(s_lt, 2 * i + 1)
                dve.scalar_tensor_tensor(out=sb["t_" + n][0:k, 0:width], in0=sb["b_" + n][0:k, :],
                                         scalar=sb["wthr"][0:k, w], in1=sb["wtmp"][0:k, 0:width],
                                         op0=ALU.is_gt, op1=ALU.subtract).then_inc(s_lt, 1)
                dve.wait_ge(s_lt, 2 * i + 2)

        @block.gpsimd
        def _(pool):
            pool.wait_ge(s_sum, 1)
            pool.partition_all_reduce(sb["wall"][:], sb["wsum"][:], P, bass.bass_isa.ReduceOp.add).then_inc(s_all, 1)


def input_scale(nc, sb, sem, tag, weight, parts=P, extra=None):
    s_max, s_all, s_a, s_b = (sem(n + tag) for n in ("max_", "allmax_", "iscale_", "inv_"))
    with nc.Block() as block:
        @block.vector
        def _(dve):
            dve.tensor_reduce(out=sb["amax"][:], in_=sb["stat"][:], axis=AX.X, op=ALU.max).then_inc(s_max, 1)
            dve.wait_ge(s_all, 1)
            dve.tensor_scalar(sb["isc"][:], sb["amaxall"][:], 1e-8, 1.0 / 127.0, ALU.max, ALU.mult).then_inc(s_a, 1)
            dve.wait_ge(s_a, 1)
            dve.reciprocal(sb["inv"][:], sb["isc"][:])
            dve.tensor_scalar(sb["osc"][:], sb["wscale"][:], sb["isc"][:, 0:1], None, ALU.mult).then_inc(s_b, 1)
            dve.wait_ge(s_b, 1)
            dve.memset(sb["stat"][:], 0.0)

        @block.gpsimd
        def _(pool):
            pool.wait_ge(s_max, 1)
            pool.partition_all_reduce(sb["amaxall"][:], sb["amax"][:], P, bass.bass_isa.ReduceOp.max).then_inc(s_all, 1)


def quantise(nc, sb, sem, tag, src, dst, parts=P):
    s_r, s_q = sem("rounded_" + tag), sem("quantised_" + tag)
    W, N = 1024, TOK // 1024
    with nc.Block() as block:
        @block.scalar
        def _(act):
            def add_round(c, k):
                after(act, s_q, c - 1)
                act.activation(sb["rnd"][0:parts, k % 2, :], src[0:parts, bass.ds(c * W, W)], ACT.Identity,
                               bias=sb["roundc"][0:parts, 0:1], scale=sb["inv"][0:parts, 0:1]).then_inc(s_r, 1)

            add_round(0, 0)
            add_round(1, 1)
            with act.Fori(1, N // 2) as q:
                for u in range(2):
                    add_round(q * 2 + u, u)

        @block.vector
        def _(dve):
            with dve.Fori(0, N // 2) as q:
                for u in range(2):
                    c = q * 2 + u
                    dve.wait_ge(s_r, c + 1)
                    dve.tensor_scalar(dst[0:parts, bass.ds(c * W, W)], sb["rnd"][0:parts, u, :], ROUND, 127.0,
                                      ALU.subtract, ALU.min).then_inc(s_q, 1)


def bit_linear(nc, sb, ps, sem, tag, weight, bias, src, dst, parts=P):
    s_m, s_d, s_a = sem("mm_" + tag), sem("dst_" + tag), sem("absmax_" + tag)
    w = slice(WS[weight], WS[weight] + 1)
    with nc.Block() as block:
        @block.tensor
        def _(pe):
            def multiply(g, k):
                after(pe, s_d, g - 3)
                pe.matmul(ps[k % 4][:, :], lhsT=sb["t_" + weight][0:parts, 0:P],
                          rhs=src[0:parts, bass.ds(g * 512, 512)], start=True, stop=True).then_inc(s_m, 1)

            run_groups(pe, multiply, 0, 4)

        @block.scalar
        def _(act):
            def scale_out(g, k):
                act.wait_ge(s_m, g + 1)
                act.activation(dst[:, bass.ds(g * 512, 512)], ps[k % 4][:, :], ACT.Identity, bias=sb[bias][:, 0:1],
                               scale=sb["osc"][:, w]).then_inc(s_d, 1)

            run_groups(act, scale_out, 0, 4)

        @block.vector
        def _(dve):
            def absmax(g, k):
                dve.wait_ge(s_d, g + 1)
                dve.tensor_reduce(out=sb["stat"][:, bass.ds(g, 1)], in_=dst[:, bass.ds(g * 512, 512)], axis=AX.X,
                                  op=ALU.max, apply_absolute_value=True)

            run_groups(dve, absmax, 0)


def bit_attention(nc, sb, ps, sem, r, qimg):
    S = lambda n: sem(n + f"_r{r}")
    s_kt, s_ktc, s_kk, s_kkc, s_f = S("kT"), S("kT_ready"), S("k"), S("k_ready"), S("fused_copied")
    s_s, s_t, s_m, s_sh, s_e, s_su, s_rc, s_p = (S(n) for n in ("s", "s_masked", "s_max", "s_shift", "s_exp", "s_sum", "s_rec", "p"))
    s_pt, s_ptc, s_o, s_u = S("pT"), S("pT_ready"), S("o"), S("upd")
    name = f"att{r}"
    w = slice(WS[name], WS[name] + 1)
    fused = sb["G3"]
    kT, kk, fz, st, pT, mx, sm = (sb[n] for n in ("b_kT", "b_k", "b_f", "b_s", "b_pT", "b_mx", "b_sm"))
    KT, KK, SS, PT, OO = ps[0:5]
    c = DIM ** -0.5

    def tiles(ap):
        return ap.rearrange("p (j n) -> p j n", j=4)

    with nc.Block() as block:
        @block.tensor
        def _(pe):
            def keys(g, k):
                after(pe, s_ktc, g)
                pe.matmul(KT[:, :], lhsT=sb["t_" + name][:], rhs=qimg[:, bass.ds(g * 512, 512)],
                          start=True, stop=True).then_inc(s_kt, 1)
                after(pe, s_kkc, g)
                for j in range(4):
                    mm = pe.matmul(KK[:, P * j:P * j + P], lhsT=qimg[:, bass.ds(g * 512 + P * j, P)],
                                   rhs=sb["t_" + name][:], start=True, stop=True)
                mm.then_inc(s_kk, 1)

            def scores(g, k):
                pe.wait_ge(s_ktc, g + 1)
                pe.wait_ge(s_f, g + 1)
                after(pe, s_t, g)
                for j in range(4):
                    n = slice(P * j, P * j + P)
                    mm = pe.matmul(SS[:, n], lhsT=fz[:, k % 2, n], rhs=kT[:, k % 2, n], start=True, stop=True)
                mm.then_inc(s_s, 1)

            def turn(g, k):
                pe.wait_ge(s_p, g + 1)
                after(pe, s_ptc, g)
                for j in range(4):
                    n = slice(P * j, P * j + P)
                    mm = pe.transpose(PT[:, n], st[:, k % 2, n], sb["ident"][:])
                mm.then_inc(s_pt, 1)

            def mix(g, k):
                pe.wait_ge(s_ptc, g + 1)
                pe.wait_ge(s_kkc, g + 1)
                after(pe, s_u, g)
                for j in range(4):
                    n = slice(P * j, P * j + P)
                    mm = pe.matmul(OO[:, n], lhsT=kk[:, k % 4, n], rhs=pT[:, k % 2, n], start=True, stop=True)
                mm.then_inc(s_o, 1)

            def step(s, k):
                for lag, do in ((1, scores), (2, turn), (0, keys), (3, mix)):
                    g = group_of(s, lag)
                    if g is not None:
                        do(g, k - lag)

            run_groups(pe, step, 3, 4)

        @block.scalar
        def _(act):
            def copy_kT(g, k):
                act.wait_ge(s_kt, g + 1)
                after(act, s_s, g - 1)
                act.activation(kT[:, k % 2, :], KT[:, :], ACT.Identity, bias=sb[f"bb_{name}"][:, 0:1],
                               scale=sb["osc"][:, w]).then_inc(s_ktc, 1)

            def exps(g, k):
                act.wait_ge(s_sh, g + 1)
                act.activation(st[:, k % 2, :], st[:, k % 2, :], ACT.Exp).then_inc(s_e, 1)

            def copy_pT(g, k):
                act.wait_ge(s_pt, g + 1)
                after(act, s_o, g - 1)
                act.activation(pT[:, k % 2, :], PT[:, :], ACT.Copy).then_inc(s_ptc, 1)

            def step(s, k):
                for lag, do in ((2, copy_pT), (1, exps), (0, copy_kT)):
                    g = group_of(s, lag)
                    if g is not None:
                        do(g, k - lag)

            run_groups(act, step, 3, 4)

        @block.vector
        def _(dve):
            def copy_k(g, k):
                dve.wait_ge(s_kk, g + 1)
                after(dve, s_o, g - 3)
                dve.scalar_tensor_tensor(out=tiles(kk[:, k % 4, :]), in0=tiles(KK[:, :]), scalar=sb["osc"][:, w],
                                         in1=sb[f"bB_{name}"][:].unsqueeze(1).to_broadcast([P, 4, P]),
                                         op0=ALU.mult, op1=ALU.add).then_inc(s_kkc, 1)

            def shift(g, k):
                dve.wait_ge(s_s, g + 1)
                after(dve, s_pt, g - 1)
                v = tiles(st[:, k % 2, :])
                dve.scalar_tensor_tensor(out=v, in0=tiles(SS[:, :]), scalar=c,
                                         in1=sb["block_mask"][:].unsqueeze(1).to_broadcast([P, 4, P]),
                                         op0=ALU.mult, op1=ALU.add).then_inc(s_t, 1)
                dve.wait_ge(s_t, g + 1)
                dve.tensor_reduce(out=mx[:, k % 2, :], in_=v, axis=AX.X, op=ALU.max).then_inc(s_m, 1)
                dve.wait_ge(s_m, g + 1)
                dve.tensor_tensor(v, v, mx[:, k % 2, :].unsqueeze(2).to_broadcast([P, 4, P]),
                                  ALU.subtract).then_inc(s_sh, 1)

            def divide(g, k):
                dve.wait_ge(s_e, g + 1)
                v = tiles(st[:, k % 2, :])
                dve.tensor_reduce(out=sm[:, k % 2, :], in_=v, axis=AX.X, op=ALU.add).then_inc(s_su, 1)
                dve.wait_ge(s_su, g + 1)
                dve.reciprocal(sm[:, k % 2, :], sm[:, k % 2, :]).then_inc(s_rc, 1)
                dve.wait_ge(s_rc, g + 1)
                dve.tensor_tensor(v, v, sm[:, k % 2, :].unsqueeze(2).to_broadcast([P, 4, P]),
                                  ALU.mult).then_inc(s_p, 1)

            def update(g, k):
                dve.wait_ge(s_o, g + 1)
                v = fused[:, bass.ds(g * 512, 512)]
                dve.scalar_tensor_tensor(out=v, in0=OO[:, :], scalar=0.1, in1=v, op0=ALU.mult,
                                         op1=ALU.add).then_inc(s_u, 1)

            def step(s, k):
                for lag, do in ((1, shift), (0, copy_k), (1, divide), (3, update)):
                    g = group_of(s, lag)
                    if g is not None:
                        do(g, k - lag)

            run_groups(dve, step, 3, 4)
            dve.wait_ge(s_u, NG)
            dve.tensor_reduce(out=sb["stat"][:, 0:1], in_=fused[:], axis=AX.X, op=ALU.max, apply_absolute_value=True)

        @block.gpsimd
        def _(pool):
            def copy_fused(g, k):
                after(pool, s_s, g - 1)
                pool.tensor_copy(fz[:, k % 2, :], fused[:, bass.ds(g * 512, 512)]).then_inc(s_f, 1)

            run_groups(pool, copy_fused, 0)


def bitnet(nc, sb, ps, sem, next_phase):
    ctxT = sb["G1"]
    half = sb["G2"][:].bitcast(BF16)
    qa, qb = half[:, 0:TOK], half[:, TOK:2 * TOK]

    weights_to_ternary(nc, sb, sem)
    with nc.Block() as block:
        @block.vector
        def _(dve):
            dve.tensor_reduce(out=sb["stat"][0:CTX, 0:1], in_=ctxT[0:CTX, :], axis=AX.X, op=ALU.max,
                              apply_absolute_value=True)
    input_scale(nc, sb, sem, "ctx", "d2v")
    quantise(nc, sb, sem, "ctx", ctxT, qa, CTX)
    bit_linear(nc, sb, ps, sem, "vis", "d2v", "bb_d2v", qa, sb["G3"], CTX)
    input_scale(nc, sb, sem, "vis", "img")
    quantise(nc, sb, sem, "vis", sb["G3"], qb)
    bit_linear(nc, sb, ps, sem, "img", "img", "bb_img", qb, sb["G1"])
    input_scale(nc, sb, sem, "img", "att0")

    s_av = sem("averaged")
    with nc.Block() as block:
        @block.vector
        def _(dve):
            dve.tensor_copy(sb["osc_img"][:], sb["osc"][:])
            dve.tensor_reduce(out=sb["avg"][:], in_=sb["G1"][:].rearrange("p (b s) -> p b s", s=SEQ), axis=AX.X,
                              op=ALU.add).then_inc(s_av, 1)
            dve.wait_ge(s_av, 1)
            dve.tensor_scalar(sb["avg"][:], sb["avg"][:], 1.0 / SEQ, None, ALU.mult)
    quantise(nc, sb, sem, "img", sb["G1"], qa)
    turn_x(nc, sb, ps, sem, "text")
    input_scale(nc, sb, sem, "text", "txt")
    quantise(nc, sb, sem, "text", sb["G3"], qb)
    bit_linear(nc, sb, ps, sem, "txt", "txt", "bb_txt", qb, sb["G3"])
    with nc.Block() as block:
        @block.vector
        def _(dve):
            dve.tensor_copy(sb["osc"][:], sb["osc_img"][:])
            dve.memset(sb["stat"][:], 0.0)
    for r in range(2):
        next_phase()
        bit_attention(nc, sb, ps, sem, r, qa)
    with nc.Block() as block:
        @block.vector
        def _(dve):
            dve.tensor_reduce(out=sb["stat"][:, 1:2], in_=sb["avg"][:], axis=AX.X, op=ALU.max, apply_absolute_value=True)
    input_scale(nc, sb, sem, "cat", "f1")
    quantise(nc, sb, sem, "cat", sb["G3"], qa)
    s_ra = sem("avg_rounded")
    with nc.Block() as block:
        @block.vector
        def _(dve):
            dve.tensor_scalar(sb["avg"][:], sb["avg"][:], sb["inv"][:, 0:1], ROUND, ALU.mult, ALU.add).then_inc(s_ra, 1)
            dve.wait_ge(s_ra, 1)
            dve.tensor_scalar(sb["qavg"][:], sb["avg"][:], ROUND, 127.0, ALU.subtract, ALU.min)
    next_phase()
    bit_ffn(nc, sb, ps, sem, qa)


def turn_x(nc, sb, ps, sem, tag):
    s_norm, s_turn, s_ht = sem("t_normed" + tag), sem("t_turned" + tag), sem("t_ready" + tag)
    TB = ps[0:2]
    with nc.Block() as block:
        @block.vector
        def _(dve):
            def step(s, k):
                g = group_of(s, 0)
                if g is not None:
                    after(dve, s_turn, g - 1)
                    normalise_group(dve, sb, g, k, s_norm)
                g = group_of(s, 2)
                if g is not None:
                    dve.wait_ge(s_ht, g + 1)
                    dve.tensor_reduce(out=sb["stat"][:, bass.ds(g, 1)], in_=sb["G3"][:, bass.ds(g * 512, 512)],
                                      axis=AX.X, op=ALU.max, apply_absolute_value=True)

            run_groups(dve, step, 2)

        @block.tensor
        def _(pe):
            def turn(g, k):
                pe.wait_ge(s_norm, g + 1)
                after(pe, s_ht, g - 1)
                for j in range(4):
                    mm = pe.transpose(TB[k % 2][:, P * j:P * j + P], sb["xn4"][:, k % 2, j, :], sb["ident"][:])
                mm.then_inc(s_turn, 1)

            run_groups(pe, turn, 0)

        @block.scalar
        def _(act):
            def copy_ht(g, k):
                act.wait_ge(s_turn, g + 1)
                act.activation(sb["G3"][:, bass.ds(g * 512, 512)], TB[k % 2][:, :], ACT.Copy).then_inc(s_ht, 1)

            run_groups(act, copy_ht, 0)


def bit_ffn(nc, sb, ps, sem, qx):
    NC = FFN // P
    s_m, s_r = sem("f1_product"), sem("f1_max")
    s_a, s_b = sem("f1_maxed"), sem("f1_scaled")
    w1 = slice(WS["f1"], WS["f1"] + 1)
    w2 = slice(WS["f2"], WS["f2"] + 1)

    def product(pe, bank, g, c):
        pe.matmul(bank[:, :], lhsT=sb["t_f1"][:, P * c:P * c + P], rhs=qx[:, bass.ds(g * 512, 512)],
                  start=True, stop=False)
        return pe.matmul(bank[:, :].rearrange("p (b s) -> p b s", s=SEQ), lhsT=sb["t_f1"][:, FFN + P * c:FFN + P * c + P],
                         rhs=sb["qavg"][:, bass.ds(g * 8, 8)].unsqueeze(2).to_broadcast([P, 8, SEQ]),
                         start=False, stop=True)

    with nc.Block() as block:
        @block.tensor
        def _(pe):
            def products(g, k):
                for c in range(NC):
                    after(pe, s_r, g * NC + c - 3)
                    product(pe, ps[c], g, c).then_inc(s_m, 1)

            run_groups(pe, products, 0)

        @block.vector
        def _(dve):
            def maxima(g, k):
                for c in range(NC):
                    dve.wait_ge(s_m, g * NC + c + 1)
                    dve.tensor_reduce(out=sb["pmax"][:, c, bass.ds(g, 1)], in_=ps[c][:, :], axis=AX.X,
                                      op=ALU.max).then_inc(s_r, 1)

            run_groups(dve, maxima, 0)
            dve.wait_ge(s_r, NG * NC)
            dve.tensor_reduce(out=sb["hmax"][:], in_=sb["pmax"][:], axis=AX.X, op=ALU.max).then_inc(s_a, 1)
            dve.wait_ge(s_a, 1)
            dve.tensor_scalar(sb["hmax"][:], sb["hmax"][:], sb["osc"][:, w1], None, ALU.mult).then_inc(s_b, 1)
            dve.wait_ge(s_b, 1)
            dve.tensor_tensor(sb["hmax"][:], sb["hmax"][:], sb["bb_f1"][:], ALU.add).then_inc(s_b, 1)
            dve.wait_ge(s_b, 2)
            dve.tensor_copy(sb["stat"][:, 0:NC], sb["hmax"][:])
            dve.tensor_copy(sb["osc_img"][:], sb["osc"][:])
    input_scale(nc, sb, sem, "hid", "f2")

    s_m, s_h, s_n, s_q, s_o, s_y, s_x = (sem(n) for n in (
        "f2_product", "f2_relu", "f2_rounded", "f2_q", "f2_out", "f2_y", "f2_x"))
    hf, hq = sb["h_f"], sb["h_q"]
    x4 = sb["x"][:].rearrange("p (g j) f -> p g (j f)", j=4)
    OB = ps[4:6]
    with nc.Block() as block:
        @block.tensor
        def _(pe):
            def hidden(g, k):
                for c in range(NC):
                    after(pe, s_h, NC * g + c - 3)
                    product(pe, ps[c], g, c).then_inc(s_m, 1)

            def down(g, k):
                pe.wait_ge(s_q, NC * (g + 1))
                after(pe, s_y, g - 1)
                for j in range(4):
                    for c in range(NC):
                        mm = pe.matmul(OB[k % 2][:, P * j:P * j + P], lhsT=hq[:, k % 2, c, P * j:P * j + P],
                                       rhs=sb["t_f2"][:, P * c:P * c + P], start=(c == 0), stop=(c == NC - 1))
                mm.then_inc(s_o, 1)

            def step(s, k):
                for lag, do in ((0, hidden), (1, down)):
                    g = group_of(s, lag)
                    if g is not None:
                        do(g, k - lag)

            run_groups(pe, step, 1)

        @block.scalar
        def _(act):
            def relus(g, k):
                for c in range(NC):
                    act.wait_ge(s_m, g * NC + c + 1)
                    after(act, s_n, g * NC + c - 3)
                    act.activation(hf[:, c, :], ps[c][:, :], ACT.Relu, bias=sb["bb_f1"][:, c:c + 1],
                                   scale=sb["osc_img"][:, w1]).then_inc(s_h, 1)

            run_groups(act, relus, 0)

        @block.vector
        def _(dve):
            def quantise_hidden(g, k):
                after(dve, s_o, g - 1)
                for c in range(NC):
                    dve.wait_ge(s_h, NC * g + c + 1)
                    dve.tensor_scalar(sb["h_r"][:, c % 2, :], hf[:, c, :], sb["inv"][:, 0:1], ROUND,
                                      ALU.mult, ALU.add).then_inc(s_n, 1)
                    dve.wait_ge(s_n, NC * g + c + 1)
                    dve.tensor_scalar(hq[:, k % 2, c, :], sb["h_r"][:, c % 2, :], ROUND, 127.0,
                                      ALU.subtract, ALU.min).then_inc(s_q, 1)

            def update(g, k):
                dve.wait_ge(s_o, g + 1)
                dve.scalar_tensor_tensor(out=sb["h_y"][:].rearrange("p (j n) -> p j n", j=4),
                                         in0=OB[k % 2][:, :].rearrange("p (j n) -> p j n", j=4),
                                         scalar=sb["osc"][:, w2],
                                         in1=sb["bB_f2"][:].unsqueeze(1).to_broadcast([P, 4, P]),
                                         op0=ALU.mult, op1=ALU.add).then_inc(s_y, 1)
                dve.wait_ge(s_y, g + 1)
                dve.tensor_tensor(x4[:, g, :], sb["h_y"][:], x4[:, g, :], ALU.add).then_inc(s_x, 1)
                settle(dve, sb, s_x, g + 1)
                stats_of_group(dve, sb, g)

            def step(s, k):
                for lag, do in ((0, quantise_hidden), (1, update)):
                    g = group_of(s, lag)
                    if g is not None:
                        do(g, k - lag)

            run_groups(dve, step, 1)


def experts(nc, sb, ps, sem):
    names = ("normed", "turned", "ht", "logits", "lmax", "lshift", "lexp", "chain", "comb", "combT", "combT_ready",
             "gate", "up", "silu", "spread", "hid", "weighted", "down", "x", "stat", "mv", "turned_all")
    s = {n: sem("e_" + n) for n in names}
    NC, NR = HID_MOE // P, EXPERTS * MID // P
    x4 = sb["x"][:].rearrange("p (g j) f -> p g (j f)", j=4)
    hid, sg = sb["e_hid"], sb["e_sg"]
    CB, LB, DB, TB = ps[4], ps[5], ps[6], ps[7]
    CH = 16

    with nc.Block() as block:
        @block.tensor
        def _(pe):
            def turn(g, k):
                pe.wait_ge(s["normed"], g + 1)
                after(pe, s["ht"], g)
                for j in range(4):
                    mm = pe.transpose(TB[:, P * j:P * j + P], sb["xn4"][:, k % 2, j, :], sb["ident"][:])
                mm.then_inc(s["turned"], 1)

            def logits(g, k):
                pe.wait_ge(s["ht"], g + 1)
                after(pe, s["combT_ready"], g)
                for j in range(4):
                    mm = pe.matmul(LB[:, EXPERTS * j:EXPERTS * j + EXPERTS], lhsT=sb["hT4"][:, k % 2, P * j:P * j + P],
                                   rhs=sb["w_router"][:], start=True, stop=True)
                mm.then_inc(s["logits"], 1)

            def turn_comb(g, k):
                pe.wait_ge(s["comb"], g + 1)
                for j in range(4):
                    mm = pe.transpose(LB[0:EXPERTS, P * j:P * j + P], sb["r_comb"][:, k % 2, j, :], sb["ident"][:])
                mm.then_inc(s["combT"], 1)

            def spread(g, k, c):
                if c == 0:
                    pe.wait_ge(s["combT_ready"], g + 1)
                after(pe, s["weighted"], NR * g + c)
                pe.matmul(CB[:, :], lhsT=sb["sel_m"][:, c, :], rhs=sb["r_combT"][:], start=True,
                          stop=True).then_inc(s["spread"], 1)

            def gate_up(g, k, c):
                pe.wait_ge(s["ht"], g + 1)
                a = 2 * ((NC * k + c) % 2)
                b = a + 1
                after(pe, s["hid"], g * NC + c - 1)
                rhs = sb["hT4"][:, k % 2, :]
                pe.matmul(ps[a][:, :], lhsT=sb["w_gate"][:, c, :], rhs=rhs, start=True, stop=True).then_inc(s["gate"], 1)
                pe.matmul(ps[b][:, :], lhsT=sb["w_up"][:, c, :], rhs=rhs, start=True, stop=True).then_inc(s["up"], 1)

            def down(g, k):
                pe.wait_ge(s["weighted"], NR * (g + 1))
                after(pe, s["x"], g)
                for j in range(4):
                    for c in range(NC):
                        mm = pe.matmul(DB[:, P * j:P * j + P], lhsT=hid[:, k % 2, c, P * j:P * j + P],
                                       rhs=sb["w_down"][:, c, :], start=(c == 0), stop=(c == NC - 1))
                mm.then_inc(s["down"], 1)

            def step(st, k):
                g3, g2, g1 = group_of(st, 3), group_of(st, 2), group_of(st, 1)
                if g3 is not None:
                    turn_comb(g3, k - 3)
                for c in range(NC):
                    if g3 is not None and c < NR:
                        spread(g3, k - 3, c)
                    if g2 is not None:
                        gate_up(g2, k - 2, c)
                if g2 is not None:
                    logits(g2, k - 2)
                if g3 is not None:
                    down(g3, k - 3)
                if g1 is not None:
                    turn(g1, k - 1)

            run_groups(pe, step, 4)

        @block.scalar
        def _(act):
            def copy_ht(g, k):
                act.wait_ge(s["turned"], g + 1)
                after(act, s["logits"], g - 1)
                after(act, s["up"], NC * (g - 1))
                act.activation(sb["hT4"][:, k % 2, :], TB[:, :], ACT.Copy).then_inc(s["ht"], 1)

            def copy_combT(g, k):
                act.wait_ge(s["combT"], g + 1)
                after(act, s["spread"], NR * g)
                act.activation(sb["r_combT"][:], LB[0:EXPERTS, :], ACT.Copy).then_inc(s["combT_ready"], 1)

            def silus(g, k):
                for c in range(NC):
                    act.wait_ge(s["gate"], NC * g + c + 1)
                    after(act, s["hid"], NC * g + c - 1)
                    act.activation(sg[:, (NC * k + c) % 2, :], ps[2 * ((NC * k + c) % 2)][:, :], ACT.Silu).then_inc(s["silu"], 1)

            def exps(g, k):
                act.wait_ge(s["lshift"], g + 1)
                act.activation(sb["r_p"][:], sb["r_p"][:], ACT.Exp).then_inc(s["lexp"], 1)

            def step(st, k):
                for lag, do in ((3, copy_combT), (2, silus), (2, exps), (1, copy_ht)):
                    g = group_of(st, lag)
                    if g is not None:
                        do(g, k - lag)

            run_groups(act, step, 4)

        @block.vector
        def _(dve):
            R = lambda ap: ap.unsqueeze(2).to_broadcast([P, 4, EXPERTS])
            p, e, oh1, oh2 = sb["r_p"], sb["r_e"], sb["r_oh1"], sb["r_oh2"]
            m1, m2, den, first = sb["r_m1"], sb["r_m2"], sb["r_den"], sb["r_first"]
            order = sb["order"][:].unsqueeze(1).to_broadcast([P, 4, EXPERTS])

            def normalise(g, k):
                after(dve, s["turned"], g - 1)
                normalise_group(dve, sb, g, k, s["normed"])

            def route(g, k):
                n = [0]

                def link(ins):
                    n[0] += 1
                    ins.then_inc(s["chain"], 1)
                    dve.wait_ge(s["chain"], g * CHAIN + n[0])

                dve.wait_ge(s["logits"], g + 1)
                lg = LB[:, 0:4 * EXPERTS].rearrange("p (j e) -> p j e", e=EXPERTS)
                link(dve.tensor_reduce(out=m1[:], in_=lg, axis=AX.X, op=ALU.max))
                dve.tensor_tensor(p[:], lg, R(m1[:]), ALU.subtract).then_inc(s["lshift"], 1)
                dve.wait_ge(s["lexp"], g + 1)
                link(dve.tensor_reduce(out=den[:], in_=p[:], axis=AX.X, op=ALU.add))
                link(dve.reciprocal(den[:], den[:]))
                link(dve.tensor_tensor(p[:], p[:], R(den[:]), ALU.mult))
                link(dve.tensor_reduce(out=m1[:], in_=p[:], axis=AX.X, op=ALU.max))
                link(dve.tensor_tensor(e[:], p[:], R(m1[:]), ALU.is_ge))
                link(dve.tensor_tensor(e[:], e[:], order, ALU.mult))
                link(dve.tensor_reduce(out=first[:], in_=e[:], axis=AX.X, op=ALU.max))
                link(dve.tensor_tensor(oh1[:], order, R(first[:]), ALU.is_equal))
                link(dve.scalar_tensor_tensor(out=oh2[:], in0=oh1[:], scalar=-2.0, in1=p[:], op0=ALU.mult, op1=ALU.add))
                link(dve.tensor_reduce(out=m2[:], in_=oh2[:], axis=AX.X, op=ALU.max))
                link(dve.tensor_tensor(e[:], oh2[:], R(m2[:]), ALU.is_ge))
                link(dve.tensor_tensor(e[:], e[:], order, ALU.mult))
                link(dve.tensor_reduce(out=first[:], in_=e[:], axis=AX.X, op=ALU.max))
                link(dve.tensor_tensor(oh2[:], order, R(first[:]), ALU.is_equal))
                link(dve.tensor_tensor(oh1[:], oh1[:], oh2[:], ALU.add))
                link(dve.scalar_tensor_tensor(out=den[:], in0=m1[:], scalar=1e-9, in1=m2[:], op0=ALU.add, op1=ALU.add))
                link(dve.reciprocal(den[:], den[:]))
                link(dve.tensor_tensor(p[:], p[:], oh1[:], ALU.mult))
                after(dve, s["combT"], g - 1)
                dve.tensor_tensor(sb["r_comb"][:, k % 2], p[:], R(den[:]), ALU.mult).then_inc(s["comb"], 1)
                assert n[0] == CHAIN

            CHAIN = 19

            def weigh(g, k, c):
                dve.wait_ge(s["spread"], NR * g + c + 1)
                v = hid[:, k % 2, c, :]
                dve.tensor_tensor(v, CB[:, :], v, ALU.mult).then_inc(s["weighted"], 1)

            def hidden(g, k, c):
                dve.wait_ge(s["silu"], NC * g + c + 1)
                dve.wait_ge(s["up"], NC * g + c + 1)
                after(dve, s["down"], g - 1)
                dve.tensor_tensor(hid[:, k % 2, c, :], ps[2 * ((NC * k + c) % 2) + 1][:, :], sg[:, (NC * k + c) % 2, :],
                                  ALU.mult).then_inc(s["hid"], 1)

            def update(g, k):
                dve.wait_ge(s["down"], g + 1)
                dve.tensor_tensor(x4[:, g, :], DB[:, :], x4[:, g, :], ALU.add).then_inc(s["x"], 1)

            def step(st, k):
                g3, g2, g0 = group_of(st, 3), group_of(st, 2), group_of(st, 0)
                for c in range(NC):
                    if g3 is not None and c < NR:
                        if c == 0:
                            dve.wait_ge(s["hid"], NC * (g3 + 1))
                        weigh(g3, k - 3, c)
                    if g2 is not None:
                        hidden(g2, k - 2, c)
                if g2 is not None:
                    route(g2, k - 2)
                if g3 is not None:
                    update(g3, k - 3)
                if g0 is not None:
                    normalise(g0, k)

            run_groups(dve, step, 4)


def decoder_kernel(nc, d, out, upto=6):
    with ExitStack() as ctx:
        sb = {}

        def sbuf(name, shape, dt=F32):
            sb[name] = ctx.enter_context(nc.sbuf_tensor("sb_" + name, shape, dt))
            return sb[name]

        held = []

        def sem(name):
            held.append(nc.alloc_semaphore(name))
            return held[-1]

        def next_phase():
            nc.clear_and_free_semaphores(list(held))
            held.clear()
            nc.all_engine_barrier()

        ps = [ctx.enter_context(nc.psum_tensor(f"bank{i}", [P, 512], F32)) for i in range(8)]
        sbuf("x", [P, NT, DIM])
        for g in ("G1", "G2", "G3"):
            sbuf(g, [P, TOK])
        sb["G3v"] = sb["G3"][:].rearrange("p (t f) -> p t f", f=DIM)
        used = 0
        for name, shape in SMALL.items():
            if name not in EARLY:
                sbuf(name, list(shape))
                continue
            width = int(shape[1]) * (int(shape[2]) if len(shape) == 3 else 1)
            view = sb["G2"][0:shape[0], used:used + width]
            sb[name] = view if len(shape) == 2 else view.rearrange("p (c n) -> p c n", c=shape[1])
            used += width
        sbuf("st6", [P, NT, 6])
        for name in ("mean", "rstd", "dif", "var"):
            sbuf(name, [P, NT])
        sbuf("scratch", [P, 1])
        sbuf("ones_row", [1, P])
        sbuf("zeros", [P, 64])
        sbuf("bqs_x0", [P, 1])
        sbuf("bqs_a1", [P, 1])
        sbuf("vblk", [P, 4, 2 * PAIRS, 2 * VW])
        ring = sbuf("ring", [P, 7040])
        at = [0]

        def part(name, *shape):
            n = 1
            for v in shape:
                n *= v
            names = "abc"[:len(shape)]
            sb[name] = ring[:, at[0]:at[0] + n].rearrange(
                f"p ({' '.join(names)}) -> p {' '.join(names)}", **dict(zip(names, shape)))
            at[0] += n

        part("xn", 2, P)
        part("hT", 2, P)
        part("cT", 4, P)
        part("qT", 2, P)
        part("km", 2, 4, P)
        part("sx", 2, 1024)
        part("pt", 2, 1024)
        part("y", 2, P)
        part("yT", 2, P)
        part("nmx", 2, HEADS)
        part("rec", 2, HEADS)
        at[0] = 0
        part("xn4", 2, 4, P)
        part("hT4", 2, 512)
        part("sT", 2, 512)
        part("e_sg", 2, 512)
        at[0] = 0
        part("b_kT", 2, 512)
        part("b_k", 4, 512)
        part("b_f", 2, 512)
        part("b_s", 2, 512)
        part("b_pT", 2, 512)
        part("b_mx", 2, 4)
        part("b_sm", 2, 4)
        at[0] = 0
        part("rnd", 2, 1024)
        part("wtmp", 1024)
        at[0] = 0
        part("h_f", 4, 512)
        part("h_r", 2, 512)
        part("h_y", 512)
        sb["h_q"] = ring[:, at[0]:at[0] + 2048].bitcast(BF16).rearrange("p (a b c) -> p a b c", a=2, b=4)
        sb["e_hid"] = sb["G1"][:, 0:2 * 5 * 512].rearrange("p (a b c) -> p a b c", a=2, b=5)

        for name, width in (("wsum", 7), ("wall", 7), ("wscale", 7), ("wthr", 7), ("wnthr", 7), ("osc", 7),
                            ("osc_img", 7), ("roundc", 1), ("stat", 16), ("amax", 1), ("amaxall", 1), ("isc", 1),
                            ("inv", 1), ("avg", BATCH), ("hmax", 4)):
            sbuf(name, [P, width])
        sbuf("pmax", [P, 4, NG])
        sbuf("qavg", [P, BATCH], BF16)
        sbuf("row", [1, DIM])
        for n in WS:
            sbuf("t_" + n, [P, SMALL["b_" + n][1]], BF16)
        for n in ("r_p", "r_e", "r_oh1", "r_oh2"):
            sbuf(n, [P, 4, EXPERTS])
        for n in ("r_m1", "r_m2", "r_den", "r_first"):
            sbuf(n, [P, 4])
        sbuf("r_comb", [P, 2, 4, EXPERTS])
        sbuf("r_combT", [EXPERTS, 512])
        sb["bk_a0"] = sb["zeros"][:, 0:1]

        load_inputs(nc, sb, sem, d)
        set_constants(nc, sb, sem)
        first_stats(nc, sb, sem)
        mean_and_rstd(nc, sb, sem, "ln1", LN_EPS)
        attention(nc, sb, ps, sem, "a0")
        mean_and_rstd(nc, sb, sem, "ln1o", 1e-3)
        second_norm(nc, sb, sem)
        if upto >= 2:
            next_phase()
            mean_and_rstd(nc, sb, sem, "ln2", LN_EPS)
            attention(nc, sb, ps, sem, "x0")
        if upto >= 3:
            next_phase()
            mean_and_rstd(nc, sb, sem, "ln3", LN_EPS)
            shrink_ffn(nc, sb, ps, sem)
        if upto >= 4:
            next_phase()
            mean_and_rstd(nc, sb, sem, "ln4", LN_EPS)
            attention(nc, sb, ps, sem, "a1")
        if upto >= 5:
            next_phase()
            mean_and_rstd(nc, sb, sem, "ln5", LN_EPS)
            bitnet(nc, sb, ps, sem, next_phase)
        if upto >= 6:
            next_phase()
            mean_and_rstd(nc, sb, sem, "ln6", LN_EPS)
            experts(nc, sb, ps, sem)
        store(nc, sb, sem, out)
        next_phase()


EARLY = ("sel_e", "w_out", "b_d2v", "b_img", "b_txt", "b_att0", "b_att1", "b_f1", "b_f2")

SMALL = {
    "ident": (P, P), "head_mask": (P, 4), "alibi": (P, HEADS * SEQ), "biasT": (P, PAIRS, SEQ),
    "gammaB": (P, DIM), "betaB": (P, DIM),
    "wq_a0": (P, P), "wk_a0": (P, P), "wv_a0": (P, 2, 64), "bv_a0": (P, P),
    "wq_x0": (P, P), "wk_x0": (CTX, P), "wv_x0": (CTX, 2, 64), "wo_x0": (P, P),
    "bq_x0": (P, 1), "bk_x0": (P, 1), "bv_x0": (P, P), "bo_x0": (1, P),
    "wq_a1": (P, P), "wk_a1": (P, P), "wv_a1": (P, 2, 64), "wo_a1": (P, P),
    "w_in": (P, M_SHRINK), "b_in": (M_SHRINK, 1), "sel_e": (M_SHRINK, 8, P), "w_1": (P, 8), "b_1": (P, 8),
    "w_2": (P, 8), "b_2": (M_SHRINK, 1), "w_outp": (M_SHRINK, DIM), "w_out": (P, 8, DIM), "b_out": (1, DIM),
    "b_d2v": (CTX, P), "b_img": (P, P), "b_txt": (P, P), "b_att0": (P, P), "b_att1": (P, P),
    "b_f1": (P, 2 * FFN), "b_f2": (P, FFN), "block_mask": (P, P),
    "bb_d2v": (P, 1), "bb_img": (P, 1), "bb_txt": (P, 1), "bb_att0": (P, 1), "bb_att1": (P, 1),
    "bB_att0": (P, P), "bB_att1": (P, P), "bb_f1": (P, 4), "bB_f2": (P, P),
    "w_router": (P, EXPERTS), "order": (P, EXPERTS), "sel_m": (EXPERTS, 4, P),
    "w_gate": (P, 5, P), "w_up": (P, 5, P), "w_down": (P, 5, DIM),
    "bq_a1": (P, 1), "bk_a1": (P, 1), "bv_a1": (P, P), "bo_a1": (1, P),
}


def laid_out(i):
    import numpy as np

    f = np.float32
    o = {}
    o["x"] = np.ascontiguousarray(i["x"].reshape(NT, P, DIM).transpose(1, 0, 2))
    o["ctxT"] = np.ascontiguousarray(i["ctx_768"].reshape(TOK, CTX).T)
    o["ident"] = np.eye(P, dtype=f)
    p = np.arange(P)
    o["head_mask"] = (((p % 32) // HD)[:, None] == np.arange(4)[None, :]).astype(f)
    slopes = (2.0 ** (-(8.0 / HEADS) * np.arange(1, HEADS + 1))).astype(f)
    pos = np.arange(SEQ)
    alibi = slopes[None, :, None] * pos[None, None, :].astype(f)
    alibi = np.where(pos[None, None, :] <= (p % SEQ)[:, None, None], alibi, f(-1e30)).astype(f)
    o["alibi"] = alibi.reshape(P, HEADS * SEQ)
    h, q, k = np.arange(HEADS)[:, None, None], pos[None, :, None], pos[None, None, :]
    table = i["L0_attn_rel_table"].reshape(-1)
    flat = h * SEQ * SEQ + q * SEQ + k
    qi, kj, hh = flat // (SEQ * HEADS), (flat // HEADS) % SEQ, flat % HEADS
    bias = table[(kj - qi + SEQ - 1) * HEADS + hh]
    o["biasT"] = np.ascontiguousarray(
        bias.reshape(PAIRS, 2, SEQ, SEQ).transpose(1, 3, 0, 2).reshape(P, PAIRS, SEQ))
    o["gammaB"] = np.tile(i["L0_attn_gamma"][None], (P, 1))
    o["betaB"] = np.tile(i["L0_attn_beta"][None], (P, 1))

    def values(w):
        return np.ascontiguousarray(w.reshape(-1, PAIRS, 2, HD).transpose(0, 2, 1, 3).reshape(-1, 2, 64))

    def value_bias(b):
        both = b.reshape(PAIRS, 2, HD).transpose(1, 0, 2).reshape(2, 1, 1, 64)
        return np.ascontiguousarray(np.broadcast_to(both, (2, 64, 2, 64)).reshape(P, P))

    o["wq_a0"], o["wk_a0"], o["wv_a0"] = i["L0_attn_Wq"], i["L0_attn_Wk"], values(i["L0_attn_Wv"])
    o["bv_a0"] = np.zeros((P, P), f)
    o["wq_x0"], o["wk_x0"], o["wv_x0"] = i["L0_xattn_wq"], i["L0_xattn_wk"], values(i["L0_xattn_wv"])
    o["wo_x0"], o["bo_x0"] = i["L0_xattn_wo"], i["L0_xattn_bo"][None]
    o["bq_x0"], o["bk_x0"] = i["L0_xattn_bq"][:, None], i["L0_xattn_bk"][:, None]
    o["bv_x0"] = value_bias(i["L0_xattn_bv"])
    w, b = i["L1_attn_w_attn"], i["L1_attn_b_attn"]
    o["wq_a1"], o["wk_a1"], o["wv_a1"] = w[:, 0:P], w[:, P:2 * P], values(w[:, 2 * P:])
    o["wo_a1"], o["bo_a1"] = i["L1_attn_w_proj"], i["L1_attn_b_proj"][None]
    o["bq_a1"], o["bk_a1"], o["bv_a1"] = b[0:P, None], b[P:2 * P, None], value_bias(b[2 * P:])

    def columns(a):
        return a.reshape(-1, P).T

    hid = np.arange(M_SHRINK * INNER).reshape(8, P)
    o["w_in"], o["b_in"] = i["L0_ffn_Win"], i["L0_ffn_bin_"][:, None]
    o["sel_e"] = (np.arange(M_SHRINK)[:, None, None] == hid[None] // INNER).astype(f)
    o["w_1"], o["b_1"], o["w_2"] = columns(i["L0_ffn_W1"]), columns(i["L0_ffn_b1"]), columns(i["L0_ffn_W2"])
    o["b_2"], o["w_outp"], o["b_out"] = i["L0_ffn_b2"][:, None], i["L0_ffn_Wout"], i["L0_ffn_bout"][None]
    o["w_out"] = i["L0_ffn_Wout"][hid // INNER].transpose(1, 0, 2)

    w = {n: i["L1_xattn_W_" + n].T for n in ("d2v", "img", "txt", "att0", "att1")}
    o["b_d2v"], o["b_img"], o["b_txt"] = w["d2v"], w["img"], w["txt"]
    for n in ("att0", "att1"):
        o["b_" + n] = np.concatenate([w[n], w[n]], axis=1)
        b = i["L1_xattn_b_" + n]
        o["bb_" + n] = np.concatenate([b, b])[:, None]
        o["bB_" + n] = np.tile(np.concatenate([b, b])[None], (P, 1))
    o["b_f1"] = i["L1_xattn_W_f1"].T.reshape(2, P, FFN).transpose(1, 0, 2).reshape(P, 2 * FFN)
    o["b_f2"] = i["L1_xattn_W_f2"].T.reshape(4, P, P).transpose(1, 0, 2).reshape(P, FFN)
    for n in ("d2v", "img", "txt"):
        o["bb_" + n] = i["L1_xattn_b_" + n][:, None]
    o["bb_f1"] = columns(i["L1_xattn_b_f1"])
    o["bB_f2"] = np.tile(i["L1_xattn_b_f2"][None], (P, 1))
    batch = p // SEQ
    o["block_mask"] = np.where(batch[:, None] == batch[None], f(0), f(-1e30)).astype(f)

    def hidden(routed, shared):
        r = i[routed].transpose(1, 0, 2).reshape(P, EXPERTS * MID)
        s = i[shared].transpose(1, 0, 2).reshape(P, P)
        return np.concatenate([r, s], axis=1).reshape(P, 5, P)

    o["w_router"] = i["L1_ffn_router_w"]
    o["order"] = np.tile(np.arange(EXPERTS, 0, -1)[None].astype(f), (P, 1))
    o["sel_m"] = (np.arange(EXPERTS)[:, None, None]
                  == np.arange(EXPERTS * MID).reshape(4, P)[None] // MID).astype(f)
    o["w_gate"], o["w_up"] = hidden("L1_ffn_wg_r", "L1_ffn_wg_s"), hidden("L1_ffn_wu_r", "L1_ffn_wu_s")
    down = np.concatenate([i["L1_ffn_wd_r"].reshape(-1, DIM), i["L1_ffn_wd_s"].reshape(-1, DIM)])
    o["w_down"] = down.reshape(5, P, DIM).transpose(1, 0, 2)
    return {k: np.ascontiguousarray(v) for k, v in o.items()}


def kernel(**inputs):
    import numpy as _np
    import concourse.bacc as _bacc
    from concourse.bass_utils import run_bass_kernel_spmd as _run

    arrays = laid_out({k: _np.asarray(v) for k, v in inputs.items()})
    nc = _bacc.Bacc("TRN2", target_bir_lowering=False, num_devices=1)
    d = {k: nc.dram_tensor("in_" + k, v.shape, F32, kind="ExternalInput").ap() for k, v in arrays.items()}
    d["_small"] = [k for k in arrays if k not in ("x", "ctxT")]
    out = nc.dram_tensor("out_x", (P, NT, DIM), F32, kind="ExternalOutput").ap()
    decoder_kernel(nc, d, out)
    r = _run(nc, [{"in_" + k: v for k, v in arrays.items()}], core_ids=[0])
    return r.results[0]["out_x"].transpose(1, 0, 2).reshape(BATCH, SEQ, DIM)
```

```python
import concourse.bass as bass
from concourse import mybir
from contextlib import ExitStack

F32 = mybir.dt.float32
BF16 = mybir.dt.bfloat16
ACT = mybir.ActivationFunctionType
ALU = mybir.AluOpType
AX = mybir.AxisListType

P = 128
BATCH, SEQ, DIM, CTX = 128, 64, 128, 96
TOK = BATCH * SEQ
NT = TOK // P
NG = TOK // 512
HEADS, HD = 16, 8
PAIRS = HEADS // 2
VW = HD + 1
M_SHRINK, INNER = 64, 16
FFN = 512
EXPERTS, MID = 16, 32
HID_MOE = EXPERTS * MID + 2 * 64
LN_EPS = 1e-5
ROUND = 12582912.0

LAYERS = ("a0", "x0", "a1")


def after(eng, sem, count):
    if isinstance(count, int) and count <= 0:
        return
    eng.wait_ge(sem, count)


def tile_of(step, lag):
    t = step - lag
    if isinstance(t, int) and not 0 <= t < NT:
        return None
    return t


def run_steps(eng, body, last_lag):
    for s in range(8):
        body(s, s)
    with eng.Fori(2, NT // 4) as q:
        for u in range(4):
            body(q * 4 + u, u)
    for s in range(NT, NT + last_lag):
        body(s, s)


def load_inputs(nc, sb, sem, d):
    loaded, ctx_loaded = sem("loaded"), sem("ctx_loaded")
    with nc.Block() as block:
        @block.sync
        def _(sp):
            n = 0
            for c in range(4):
                sp.dma_start(sb["x"][:, 16 * c:16 * c + 16, :], d["x"][:, 16 * c:16 * c + 16, :]).then_inc(loaded, 16)
                n += 16
            for name in d["_small"]:
                sp.dma_start(sb[name][:], d[name]).then_inc(loaded, 16)
                n += 16
            sp.wait_ge(loaded, n)

        @block.scalar
        def _(act):
            act.dma_start(sb["G1"][0:CTX, :], d["ctxT"]).then_inc(ctx_loaded, 16)
            act.wait_ge(ctx_loaded, 16)


def set_constants(nc, sb, sem):
    made = sem("made")
    with nc.Block() as block:
        @block.vector
        def _(dve):
            dve.memset(sb["ones_row"][:], 1.0)
            dve.memset(sb["zeros"][:], 0.0)
            dve.memset(sb["bkm_a0"][:], 0.0)
            dve.memset(sb["own_half"][:], 0.0)
            dve.memset(sb["vblk"][:], 0.0).then_inc(made, 1)
            dve.wait_ge(made, 1)
            for i in range(2):
                h = slice(64 * i, 64 * i + 64)
                dve.memset(sb["vblk"][h, 0, :, :, :, i * VW + HD:i * VW + VW], 1.0)
                dve.memset(sb["own_half"][h, i:i + 1], 1.0)
            for layer in ("x0", "a1"):
                dve.tensor_scalar(sb["bkm_" + layer][:], sb["head_mask"][:], sb["bk_" + layer][:, 0:1], None, ALU.mult)
            dve.tensor_copy(sb["biasP"][:, 0], sb["biasT"][:]).then_inc(made, 1)
            dve.wait_ge(made, 2)
            dve.tensor_tensor(sb["biasP"][:, 1], sb["biasT"][:], sb["biasP"][:, 0], ALU.subtract)
            for layer, scale in (("x0", HD ** -0.5), ("a1", HD ** -0.5)):
                dve.tensor_scalar(sb["bqs_" + layer][:], sb["bq_" + layer][:], scale, None, ALU.mult)


def first_stats(nc, sb, sem):
    with nc.Block() as block:
        @block.vector
        def _(dve):
            with dve.Fori(0, NT // 2) as q:
                for u in range(2):
                    t = q * 2 + u
                    dve.bn_stats(sb["st6"][:, t, :], sb["x"][:, t, :])


def settle(dve, sb, sem, count):
    after(dve, sem, count)
    dve.memset(sb["scratch"][:], 0.0)


def mean_and_rstd(nc, sb, sem, name, eps):
    s_in, s_d, s_v, s_rooted, s_inv = (sem(name + n) for n in ("_halves", "_squares", "_variance", "_rooted", "_inverted"))
    st6, mean, rstd, dif, var = (sb[n] for n in ("st6", "mean", "rstd", "dif", "var"))
    with nc.Block() as block:
        @block.vector
        def _(dve):
            dve.tensor_tensor(mean[:], st6[:, :, 1], st6[:, :, 4], ALU.add)
            dve.tensor_tensor(dif[:], st6[:, :, 1], st6[:, :, 4], ALU.subtract)
            dve.tensor_tensor(var[:], st6[:, :, 2], st6[:, :, 5], ALU.add).then_inc(s_in, 1)
            dve.wait_ge(s_in, 1)
            dve.tensor_scalar(mean[:], mean[:], 0.5, None, ALU.mult)
            dve.tensor_tensor(dif[:], dif[:], dif[:], ALU.mult)
            dve.tensor_scalar(var[:], var[:], 1.0 / DIM, eps, ALU.mult, ALU.add).then_inc(s_d, 1)
            dve.wait_ge(s_d, 1)
            dve.scalar_tensor_tensor(out=var[:], in0=dif[:], scalar=0.25, in1=var[:], op0=ALU.mult,
                                     op1=ALU.add).then_inc(s_v, 1)
            dve.wait_ge(s_rooted, 1)
            dve.reciprocal(rstd[:], rstd[:]).then_inc(s_inv, 1)
            dve.wait_ge(s_inv, 1)
            dve.scalar_tensor_tensor(out=sb["nmr"][:], in0=mean[:], scalar=-1.0, in1=rstd[:], op0=ALU.mult,
                                     op1=ALU.mult)

        @block.scalar
        def _(act):
            act.wait_ge(s_v, 1)
            act.activation(rstd[:], var[:], ACT.Sqrt).then_inc(s_rooted, 1)


def attention(nc, sb, ps, sem, layer):
    cross, causal, plain = layer == "x0", layer == "a1", layer == "a0"
    S = lambda n: sem(n + "_" + layer)
    s_norm, s_ctx, s_turn, s_ht, s_proj = S("normed"), S("ctx_copied"), S("turned"), S("ht_ready"), S("projected")
    s_q, s_k, s_v, s_vb = S("q_ready"), S("k_ready"), S("v_ready"), S("v_split")
    s_sc, s_max, s_add, s_sub = S("scored"), S("maxed"), S("alibi_added"), S("shifted")
    s_exp, s_pt, s_pe, s_mix = S("exp_ready"), S("p_turned"), S("pt_high"), S("mixed")
    s_pl, s_vh, s_vm = S("pt_low"), S("v_high"), S("v_placed")
    s_rec, s_y, s_yb = S("sum_inverted"), S("y_ready"), S("y_biased")
    s_yt, s_yc, s_out, s_x = S("y_turned"), S("yt_ready"), S("out_ready"), S("x_updated")
    x, ctxT, ao = sb["x"], sb["G1"], sb["G3v"]
    wq, wk, wv = sb["wq_" + layer], sb["wk_" + layer], sb["wv_" + layer]
    bkm, bv = sb["bkm_" + layer], sb["bv_" + layer]
    xn, hT, cT, qT, km, v32, vb = sb["xn"], sb["hT"], sb["cT"], sb["qT"], sb["km"], sb["v32"], sb["vblk"]
    vp = sb["vp"]
    sx, pt, y, yT, nmx, rec = sb["sx"], sb["pt"], sb["y"], sb["yT"], sb["nmx"], sb["rec"]
    SB, TB, PB, OB = ps[0:4], ps[4:6], ps[6], ps[7]
    XT, YT = SB[0][:, 256:384], SB[1][:, 256:384]
    s_free = s_add if causal else s_sub
    LAST = 6 if plain else 7
    KIN = CTX if cross else P
    MO = OB[:, 0:288].rearrange("p (b n) -> p b n", b=2)
    MB = SB[2][:, 256:512].rearrange("p (b c i d) -> p b c i d", b=2, c=PAIRS, i=2)
    scale = DIM ** -0.5 if plain else HD ** -0.5

    with nc.Block() as block:
        @block.tensor
        def _(pe):
            def turn(t, k):
                pe.wait_ge(s_norm, t + 1)
                after(pe, s_ht, t)
                after(pe, s_free, 4 * (t - (3 if plain else 2)) + 1)
                pe.transpose(XT, xn[:, k % 2, :], sb["ident"][:]).then_inc(s_turn, 1)

            def project(t, k):
                pe.wait_ge(s_ht, t + 1)
                after(pe, s_q, t)
                after(pe, s_k, t)
                after(pe, s_v, t)
                if cross:
                    pe.wait_ge(s_ctx, t + 1)
                src = cT[0:CTX, k % 4] if cross else hT[:, k % 2]
                pe.matmul(PB[:, 0:128], lhsT=wq[:], rhs=hT[:, k % 2], start=True, stop=True)
                pe.matmul(PB[:, 128:256], lhsT=wk[:], rhs=src, start=True, stop=True)
                for b in range(2):
                    for i in range(2):
                        mm = pe.matmul(PB[64 * i:64 * i + 64, 256 + 64 * b:320 + 64 * b],
                                       lhsT=src[:, 64 * b:64 * b + 64], rhs=wv[:, i, :], start=True, stop=True)
                mm.then_inc(s_proj, 1)

            def score(t, k):
                pe.wait_ge(s_q, t + 1)
                pe.wait_ge(s_k, t + 1)
                for g in range(4):
                    after(pe, s_free, 4 * (t - 1) + g + 1 if not isinstance(t, int) or t else 0)
                    if g == 0:
                        n = 3 if plain else 2
                        after(pe, s_ht, t + n if not isinstance(t, int) or t + n <= NT else NT)
                    if g == 1 and not plain:
                        after(pe, s_yc, t - 3)
                    if g == 2 and plain:
                        after(pe, s_y, t - 2)
                    r = slice(32 * g, 32 * g + 32)
                    for b in range(2):
                        mm = pe.matmul(SB[g][64 * b:64 * b + 64, 0:256], lhsT=qT[r, k % 2, 64 * b:64 * b + 64],
                                       rhs=km[r, k % 2, :, 64 * b:64 * b + 64], start=True, stop=True)
                    mm.then_inc(s_sc, 1)

            def turn_p(t, k):
                pe.wait_ge(s_exp, t + 1)
                after(pe, s_pl, 2 * t)
                for n in range(2):
                    for c in range(4):
                        mm = pe.transpose(TB[n][:, 128 * c:128 * c + 128],
                                          sx[:, k % 2, 512 * n + 128 * c:512 * n + 128 * c + 128], sb["ident"][:])
                    mm.then_inc(s_pt, 1)

            def mix(t, k):
                pe.wait_ge(s_pl, 2 * t + 2)
                pe.wait_ge(s_vb, t + 1)
                after(pe, s_y, t)
                if not plain:
                    after(pe, s_x, t - 2)

                def products(out, parts, values):
                    for n, (a, b) in enumerate(((0, 0), (0, 1), (1, 0))):
                        ins = pe.matmul(out, lhsT=parts[a], rhs=values[b], start=(n == 0), stop=(n == 2))
                    return ins

                for c in range(PAIRS):
                    mm = products(MO[:, :, 18 * c:18 * c + 18], [pt[:, h, k % 2, 128 * c:128 * c + 128] for h in range(2)],
                                  [vb[:, h, k % 4, :, c, :] for h in range(2)])
                if plain:
                    after(pe, s_free, 4 * (t + 2) + 3 if not isinstance(t, int) or t + 3 <= NT else 4 * NT)
                    for c in range(PAIRS):
                        mm = products(MB[:, :, c], [sb["biasP"][:, h, c, :] for h in range(2)],
                                      [vb[:, h, k % 4, :, c, :].rearrange("p b (i e) -> p b i e", e=VW)[:, :, :, 0:HD]
                                       for h in range(2)])
                mm.then_inc(s_mix, 1)

            def turn_y(t, k):
                pe.wait_ge(s_y, t + 1)
                after(pe, s_yc, t)
                after(pe, s_free, 4 * (t + 3) + 2 if not isinstance(t, int) or t + 4 <= NT else 4 * NT)
                pe.transpose(YT, y[:, k % 2, :], sb["ident"][:]).then_inc(s_yt, 1)

            def project_out(t, k):
                pe.wait_ge(s_yc, t + 1)
                after(pe, s_x, t)
                after(pe, s_y, t + 2 if not isinstance(t, int) or t + 2 <= NT else NT)
                pe.matmul(OB[:, 384:512], lhsT=yT[:, k % 2, :], rhs=sb["wo_" + layer][:], start=True, stop=False)
                pe.matmul(OB[:, 384:512], lhsT=sb["ones_row"][:], rhs=sb["bo_" + layer][:],
                          start=False, stop=True).then_inc(s_out, 1)

            def step(s, k):
                for lag, do in (((1, turn), (2, project), (3, score), (4, turn_p), (5, mix)) if plain else
                                ((3, score), (2, project), (4, turn_p), (1, turn), (6, turn_y), (7, project_out), (5, mix))):
                    t = tile_of(s, lag)
                    if t is not None:
                        do(t, k - lag)

            run_steps(pe, step, LAST)

        @block.scalar
        def _(act):
            def copy_q(t, k):
                act.wait_ge(s_proj, t + 1)
                after(act, s_sc, 4 * (t - 1))
                if plain:
                    act.activation(qT[:, k % 2, :], PB[:, 0:128], ACT.Copy, scale=scale).then_inc(s_q, 1)
                else:
                    act.activation(qT[:, k % 2, :], PB[:, 0:128], ACT.Identity, bias=sb["bqs_" + layer][:, 0:1],
                                   scale=scale).then_inc(s_q, 1)

            def copy_k(t, k):
                for j in range(4):
                    ins = act.activation(km[:, k % 2, j, :], PB[:, 128:256], ACT.Identity,
                                         bias=bkm[:, j:j + 1], scale=sb["head_mask"][:, j:j + 1])
                ins.then_inc(s_k, 1)

            def normalise(t, k):
                after(act, s_turn, t - 1)
                act.activation(xn[:, k % 2, :], x[:, t, :], ACT.Identity, bias=sb["nmr"][:, bass.ds(t, 1)],
                               scale=sb["rstd"][:, bass.ds(t, 1)]).then_inc(s_norm, 1)

            def copy_yt(t, k):
                act.wait_ge(s_yt, t + 1)
                act.activation(yT[:, k % 2, :], YT, ACT.Copy).then_inc(s_yc, 1)

            def copy_pt(t, k):
                after(act, s_mix, t - 1)
                for n in range(2):
                    act.wait_ge(s_pt, 2 * t + n + 1)
                    act.activation(pt[:, 0, k % 2, 512 * n:512 * n + 512], TB[n][:, :], ACT.Copy).then_inc(s_pe, 1)

            def exps(t, k):
                act.wait_ge(s_sub, 4 * t + 4)
                act.activation(sx[:, k % 2, :], sx[:, k % 2, :], ACT.Exp).then_inc(s_exp, 1)

            def copy_ht(t, k):
                act.wait_ge(s_turn, t + 1)
                after(act, s_proj, t - 1)
                act.activation(hT[:, k % 2], XT, ACT.Copy).then_inc(s_ht, 1)

            def step(s, k):
                for lag, do in (((1, copy_ht), (2, copy_q), (2, copy_k), (4, copy_pt), (0, normalise), (3, exps)) if plain
                                else ((2, copy_q), (2, copy_k), (4, copy_pt), (1, copy_ht), (6, copy_yt), (0, normalise),
                                      (3, exps))):
                    t = tile_of(s, lag)
                    if t is not None:
                        do(t, k - lag)

            run_steps(act, step, LAST)

        @block.vector
        def _(dve):
            def copy_v(t, k):
                dve.wait_ge(s_k, t + 1)
                after(dve, s_vb, t - 1)
                dve.tensor_tensor(vp[:, k % 2], PB[:, 256:384], bv[:], ALU.add).then_inc(s_v, 1)

            def low_part(t, k):
                after(dve, s_mix, t - 1)
                for n in range(2):
                    dve.wait_ge(s_pe, 2 * t + n + 1)
                    dve.tensor_tensor(pt[:, 1, k % 2, 512 * n:512 * n + 512], TB[n][:, :],
                                      pt[:, 0, k % 2, 512 * n:512 * n + 512], ALU.subtract).then_inc(s_pl, 1)

            def shift(t, k):
                after(dve, s_pt, 2 * (t - 1))
                two = lambda a, n: a[:, 512 * n:512 * n + 512].rearrange("p (g c) -> p g c", g=2)
                if causal:
                    for n in range(2):
                        dve.wait_ge(s_sc, 4 * t + 2 * n + 2)
                        dve.tensor_tensor(two(sx[:, k % 2, :], n), sb["banks"][:, 2 * n:2 * n + 2, 0:256],
                                          two(sb["alibi"], n), ALU.add).then_inc(s_add, 2)
                    dve.wait_ge(s_add, 4 * t + 4)
                    v = sx[:, k % 2, :].rearrange("p (h k) -> p h k", k=SEQ)
                    dve.tensor_reduce(out=nmx[:, k % 2, :], in_=v, axis=AX.X, op=ALU.max).then_inc(s_max, 1)
                    dve.wait_ge(s_max, t + 1)
                    dve.tensor_tensor(v, v, nmx[:, k % 2, :].unsqueeze(2).to_broadcast([P, HEADS, SEQ]),
                                      ALU.subtract).then_inc(s_sub, 4)
                    return
                heads = lambda a: a.rearrange("p g (h k) -> p g h k", k=SEQ)
                for n in range(2):
                    dve.wait_ge(s_sc, 4 * t + 2 * n + 2)
                    dve.tensor_reduce(out=nmx[:, k % 2, 8 * n:8 * n + 8].rearrange("p (g h) -> p g h", g=2),
                                      in_=heads(sb["banks"][:, 2 * n:2 * n + 2, 0:256]),
                                      axis=AX.X, op=ALU.max).then_inc(s_max, 1)
                for n in range(2):
                    dve.wait_ge(s_max, 2 * t + n + 1)
                    dve.tensor_tensor(
                        heads(two(sx[:, k % 2, :], n)), heads(sb["banks"][:, 2 * n:2 * n + 2, 0:256]),
                        nmx[:, k % 2, 8 * n:8 * n + 8].rearrange("p (g h) -> p g h", g=2).unsqueeze(3)
                        .to_broadcast([P, 2, 4, SEQ]), ALU.subtract).then_inc(s_sub, 2)

            def finish(t, k):
                dve.wait_ge(s_mix, t + 1)
                halves = [(slice(64 * b, 64 * b + 64), b) for b in range(2)]
                for r, b in halves:
                    o = MO[r, b, :].rearrange("p (h e) -> p h e", e=VW)
                    dve.reciprocal(rec[r, k % 2, :], o[:, :, HD]).then_inc(s_rec, 1)
                dve.wait_ge(s_rec, 2 * t + 2)
                if not plain:
                    after(dve, s_yt, t - 1)
                for r, b in halves:
                    o = MO[r, b, :].rearrange("p (h e) -> p h e", e=VW)
                    ins = dve.tensor_tensor(y[r, k % 2, :].rearrange("p (h d) -> p h d", d=HD), o[:, :, 0:HD],
                                            rec[r, k % 2, :].unsqueeze(2).to_broadcast([64, HEADS, HD]), ALU.mult)
                if not plain:
                    ins.then_inc(s_y, 1)
                    return
                ins.then_inc(s_yb, 1)
                dve.wait_ge(s_yb, t + 1)
                for r, b in halves:
                    ins = dve.tensor_tensor(ao[r, t, :], SB[2][r, 256 + 128 * b:384 + 128 * b], y[r, k % 2, :], ALU.add)
                ins.then_inc(s_y, 1)

            def update_x(t, k):
                dve.wait_ge(s_out, t + 1)
                dve.tensor_tensor(x[:, t, :], OB[:, 384:512], x[:, t, :], ALU.add).then_inc(s_x, 1)

            def stats(t, k, finished):
                if not finished:
                    dve.wait_ge(s_y if plain else s_x, t + 1)
                dve.bn_stats(sb["st6"][:, t, :], (ao if plain else x)[:, t, :])

            def step(s, k):
                t = tile_of(s, 3)
                if t is not None:
                    shift(t, k - 3)
                for lag, do in ((2, copy_v), (4, low_part)) if plain else ((4, low_part), (2, copy_v)):
                    t = tile_of(s, lag)
                    if t is not None:
                        do(t, k - lag)
                if not plain:
                    t = tile_of(s, 5)
                    if t is not None:
                        dve.wait_ge(s_mix, t + 1)
                    t = tile_of(s, 7)
                    if t is not None:
                        update_x(t, k - 7)
                t = tile_of(s, 5)
                if t is not None:
                    finish(t, k - 5)
                lag = 6 if plain else 7
                if tile_of(s, lag) is not None:
                    stats(tile_of(s, lag), k - lag, t is not None)

            run_steps(dve, step, LAST)

        @block.gpsimd
        def _(pool):
            def copy_ctx(t, k):
                after(pool, s_proj, t - 3)
                pool.tensor_copy(cT[0:CTX, k % 4], ctxT[0:CTX, bass.ds(t * P, P)]).then_inc(s_ctx, 1)

            def split_v(t, k):
                pool.wait_ge(s_v, t + 1)
                v = v32[:, k % 2].rearrange("p b c i d -> p (b c) i d")
                pool.tensor_tensor(v, vp[:, k % 2].rearrange("p (m d) -> p m d", d=HD).unsqueeze(2)
                                   .to_broadcast([P, 2 * PAIRS, 2, HD]),
                                   sb["own_half"][:].unsqueeze(1).unsqueeze(3).to_broadcast([P, 2 * PAIRS, 2, HD]),
                                   ALU.mult).then_inc(s_vm, 1)
                pool.wait_ge(s_vm, t + 1)
                after(pool, s_mix, t - 3)
                zeros = sb["zeros"][:, 0:HD].unsqueeze(1).unsqueeze(1).to_broadcast([P, 2 * PAIRS, 2, HD])
                high, low = (vb[:, h, k % 4].rearrange("p b c (i e) -> p (b c) i e", e=VW)[:, :, :, 0:HD]
                             for h in range(2))
                pool.tensor_tensor(high, v, zeros, ALU.add).then_inc(s_vh, 1)
                pool.wait_ge(s_vh, t + 1)
                ins = pool.tensor_tensor(low, v, high, ALU.subtract)
                ins.then_inc(s_vb, 1)

            def step(s, k):
                t = tile_of(s, 0)
                if t is not None and cross:
                    copy_ctx(t, k)
                t = tile_of(s, 2)
                if t is not None:
                    split_v(t, k - 2)

            run_steps(pool, step, 3)


def second_norm(nc, sb, sem):
    s_n, s_g, s_b, s_x = (sem(n) for n in ("o_normed", "o_scaled", "o_shifted", "o_added"))
    x, ao = sb["x"], sb["G3v"]
    tiles = lambda a, g: a[:, bass.ds(g * 4, 4), :]
    wide = lambda b: b[:].unsqueeze(1).to_broadcast([P, 4, DIM])
    with nc.Block() as block:
        @block.vector
        def _(dve):
            def scale(g, k):
                for j in range(4):
                    t = g * 4 + j
                    ins = dve.tensor_scalar(ao[:, t, :], ao[:, t, :], sb["mean"][:, bass.ds(t, 1)],
                                            sb["rstd"][:, bass.ds(t, 1)], ALU.subtract, ALU.mult)
                ins.then_inc(s_n, 1)
                dve.wait_ge(s_n, g + 1)
                dve.tensor_tensor(tiles(ao, g), tiles(ao, g), wide(sb["gammaB"]), ALU.mult).then_inc(s_g, 1)

            def add(g, k):
                dve.wait_ge(s_b, g + 1)
                dve.tensor_tensor(tiles(x, g), tiles(ao, g), tiles(x, g), ALU.add).then_inc(s_x, 1)
                settle(dve, sb, s_x, g + 1)
                stats_of_group(dve, sb, g)

            def step(s, k):
                for lag, do in ((0, scale), (1, add)):
                    g = group_of(s, lag)
                    if g is not None:
                        do(g, k - lag)

            run_groups(dve, step, 1)

        @block.gpsimd
        def _(pool):
            def shift(g, k):
                pool.wait_ge(s_g, g + 1)
                pool.tensor_tensor(tiles(ao, g), tiles(ao, g), wide(sb["betaB"]), ALU.add).then_inc(s_b, 1)

            run_groups(pool, shift, 0)


def store(nc, sb, sem, out):
    stored = sem("stored")
    with nc.Block() as block:
        @block.sync
        def _(sp):
            for c in range(4):
                sp.dma_start(out[:, 16 * c:16 * c + 16, :], sb["x"][:, 16 * c:16 * c + 16, :]).then_inc(stored, 16)
            sp.wait_ge(stored, 64)


def run_groups(eng, body, last_lag, unroll=2):
    for s in range(4):
        body(s, s)
    with eng.Fori(4 // unroll, NG // unroll) as q:
        for u in range(unroll):
            body(q * unroll + u, u)
    for s in range(NG, NG + last_lag):
        body(s, s)


def group_of(step, lag):
    g = step - lag
    if isinstance(g, int) and not 0 <= g < NG:
        return None
    return g


def normalise_group(dve, sb, g, k, done):
    for j in range(4):
        t = g * 4 + j
        ins = dve.tensor_scalar(sb["xn4"][:, k % 2, j, :], sb["x"][:, t, :], sb["mean"][:, bass.ds(t, 1)],
                                sb["rstd"][:, bass.ds(t, 1)], ALU.subtract, ALU.mult)
    ins.then_inc(done, 1)


def stats_of_group(dve, sb, g):
    for j in range(4):
        dve.bn_stats(sb["st6"][:, g * 4 + j, :], sb["x"][:, g * 4 + j, :])


def shrink_ffn(nc, sb, ps, sem):
    s_fold, s_row = sem("w2_folded"), sem("row_ready")
    s_norm, s_turn, s_ht, s_sh, s_sT = sem("f_normed"), sem("f_turned"), sem("f_ht_ready"), sem("f_shrunk"), sem("f_sT_ready")
    s_ex, s_hid, s_dn, s_x = (sem(n) for n in ("f_expanded", "f_hid_ready", "f_down", "f_x"))
    NC = M_SHRINK * INNER // P
    x4 = sb["x"][:].rearrange("p (g j) f -> p g (j f)", j=4)
    hid = sb["G3"][:].rearrange("p (r c n) -> p r c n", r=2, c=NC)
    EB, DB, TB, SB = ps[0:4], ps[4:6], ps[6], ps[7]

    with nc.Block() as block:
        @block.vector
        def _(dve):
            for c in range(NC):
                ins = dve.tensor_scalar(sb["w_out"][:, c, :], sb["w_out"][:, c, :], sb["w_2"][:, c:c + 1], None, ALU.mult)
            dve.wait_ge(s_fold, 1)
            dve.tensor_tensor(sb["row"][:], ps[0][0:1, 0:DIM], sb["b_out"][:], ALU.add)

        @block.tensor
        def _(pe):
            pe.matmul(ps[0][0:1, 0:DIM], lhsT=sb["b_2"][:], rhs=sb["w_outp"][:], start=True, stop=True).then_inc(s_fold, 1)

    with nc.Block() as block:
        @block.tensor
        def _(pe):
            def turn(g, k):
                pe.wait_ge(s_norm, g + 1)
                after(pe, s_ht, g)
                for j in range(4):
                    mm = pe.transpose(TB[:, P * j:P * j + P], sb["xn4"][:, k % 2, j, :], sb["ident"][:])
                mm.then_inc(s_turn, 1)

            def shrink(g, k):
                pe.wait_ge(s_ht, g + 1)
                after(pe, s_sT, g)
                pe.matmul(SB[0:M_SHRINK, :], lhsT=sb["w_in"][:], rhs=sb["hT4"][:, k % 2, :],
                          start=True, stop=True).then_inc(s_sh, 1)

            def expand(g, k):
                pe.wait_ge(s_sT, g + 1)
                for c in range(NC):
                    if c >= 4:
                        pe.wait_ge(s_hid, NC * g + c - 3)
                    else:
                        after(pe, s_hid, NC * g + c - 3)
                    pe.matmul(EB[c % 4][:, :], lhsT=sb["sel_e"][:, c, :], rhs=sb["sT"][0:M_SHRINK, k % 2, :],
                              start=True, stop=True).then_inc(s_ex, 1)

            def down(g, k):
                pe.wait_ge(s_hid, NC * (g + 1))
                after(pe, s_x, g)
                for j in range(4):
                    o = DB[k % 2][:, DIM * j:DIM * j + DIM]
                    for c in range(NC):
                        pe.matmul(o, lhsT=hid[:, k % 2, c, P * j:P * j + P], rhs=sb["w_out"][:, c, :],
                                  start=(c == 0), stop=False)
                    mm = pe.matmul(o, lhsT=sb["ones_row"][:], rhs=sb["row"][:], start=False, stop=True)
                mm.then_inc(s_dn, 1)

            def step(s, k):
                for lag, do in ((2, shrink), (3, down), (2, expand), (1, turn)):
                    g = group_of(s, lag)
                    if g is not None:
                        do(g, k - lag)

            run_groups(pe, step, 4)

        @block.scalar
        def _(act):
            def copy_ht(g, k):
                act.wait_ge(s_turn, g + 1)
                after(act, s_sh, g - 1)
                act.activation(sb["hT4"][:, k % 2, :], TB[:, :], ACT.Copy).then_inc(s_ht, 1)

            def copy_sT(g, k):
                act.wait_ge(s_sh, g + 1)
                after(act, s_ex, NC * (g - 1))
                act.activation(sb["sT"][0:M_SHRINK, k % 2, :], SB[0:M_SHRINK, :], ACT.Identity,
                               bias=sb["b_in"][:, 0:1]).then_inc(s_sT, 1)

            def relus(g, k):
                after(act, s_dn, g - 1)
                for c in range(NC):
                    act.wait_ge(s_ex, NC * g + c + 1)
                    act.activation(hid[:, k % 2, c, :], EB[c % 4][:, :], ACT.Relu, bias=sb["b_1"][:, c:c + 1],
                                   scale=sb["w_1"][:, c:c + 1]).then_inc(s_hid, 1)

            def step(s, k):
                for lag, do in ((2, copy_sT), (2, relus), (1, copy_ht)):
                    g = group_of(s, lag)
                    if g is not None:
                        do(g, k - lag)

            run_groups(act, step, 4)

        @block.vector
        def _(dve):
            def normalise(g, k):
                after(dve, s_turn, g - 1)
                normalise_group(dve, sb, g, k, s_norm)

            def update(g, k):
                dve.wait_ge(s_dn, g + 1)
                dve.tensor_tensor(x4[:, g, :], DB[k % 2][:, :], x4[:, g, :], ALU.add).then_inc(s_x, 1)
                settle(dve, sb, s_x, g + 1)
                stats_of_group(dve, sb, g)

            def step(s, k):
                for lag, do in ((0, normalise), (3, update)):
                    g = group_of(s, lag)
                    if g is not None:
                        do(g, k - lag)

            run_groups(dve, step, 4)


WS = {n: i for i, n in enumerate(("d2v", "img", "txt", "att0", "att1", "f1", "f2"))}
WCOUNT = {"d2v": CTX * P, "img": P * P, "txt": P * P, "att0": P * P, "att1": P * P,
          "f1": 2 * P * FFN, "f2": P * FFN}


def weights_to_ternary(nc, sb, sem):
    s_zero, s_sum, s_all, s_scale, s_thr, s_lt = (sem(n) for n in ("q_zeroed", "q_summed", "q_all", "q_scaled", "q_thr", "q_lt"))
    names = list(WS)
    with nc.Block() as block:
        @block.vector
        def _(dve):
            dve.memset(sb["wsum"][:], 0.0).then_inc(s_zero, 1)
            dve.memset(sb["roundc"][:], ROUND)
            dve.memset(sb["stat"][:], 0.0)
            dve.wait_ge(s_zero, 1)
            for n in names:
                k = CTX if n == "d2v" else P
                ins = dve.tensor_reduce(out=sb["wsum"][0:k, WS[n]:WS[n] + 1], in_=sb["b_" + n][0:k, :], axis=AX.X,
                                        op=ALU.add, apply_absolute_value=True)
            ins.then_inc(s_sum, 1)
            dve.wait_ge(s_all, 1)
            for n in names:
                w = slice(WS[n], WS[n] + 1)
                ins = dve.tensor_scalar(sb["wscale"][:, w], sb["wall"][:, w], 1.0 / WCOUNT[n], 1e-5, ALU.mult, ALU.max)
            ins.then_inc(s_scale, 1)
            dve.wait_ge(s_scale, 1)
            dve.tensor_scalar(sb["wthr"][:], sb["wscale"][:], 0.5, None, ALU.mult)
            dve.tensor_scalar(sb["wnthr"][:], sb["wscale"][:], -0.5, None, ALU.mult).then_inc(s_thr, 1)
            dve.wait_ge(s_thr, 1)
            for i, n in enumerate(names):
                k = CTX if n == "d2v" else P
                w, width = slice(WS[n], WS[n] + 1), sb["b_" + n].shape[1]
                dve.tensor_scalar(sb["wtmp"][0:k, 0:width], sb["b_" + n][0:k, :], sb["wnthr"][0:k, w], None,
                                  ALU.is_lt).then_inc(s_lt, 1)
                dve.wait_ge(s_lt, 2 * i + 1)
                dve.scalar_tensor_tensor(out=sb["t_" + n][0:k, 0:width], in0=sb["b_" + n][0:k, :],
                                         scalar=sb["wthr"][0:k, w], in1=sb["wtmp"][0:k, 0:width],
                                         op0=ALU.is_gt, op1=ALU.subtract).then_inc(s_lt, 1)
                dve.wait_ge(s_lt, 2 * i + 2)

        @block.gpsimd
        def _(pool):
            pool.wait_ge(s_sum, 1)
            pool.partition_all_reduce(sb["wall"][:], sb["wsum"][:], P, bass.bass_isa.ReduceOp.add).then_inc(s_all, 1)


def input_scale(nc, sb, sem, tag, weight, parts=P, extra=None):
    s_max, s_all, s_a, s_b = (sem(n + tag) for n in ("max_", "allmax_", "iscale_", "inv_"))
    with nc.Block() as block:
        @block.vector
        def _(dve):
            dve.tensor_reduce(out=sb["amax"][:], in_=sb["stat"][:], axis=AX.X, op=ALU.max).then_inc(s_max, 1)
            dve.wait_ge(s_all, 1)
            dve.tensor_scalar(sb["isc"][:], sb["amaxall"][:], 1e-8, 1.0 / 127.0, ALU.max, ALU.mult).then_inc(s_a, 1)
            dve.wait_ge(s_a, 1)
            dve.reciprocal(sb["inv"][:], sb["isc"][:])
            dve.tensor_scalar(sb["osc"][:], sb["wscale"][:], sb["isc"][:, 0:1], None, ALU.mult).then_inc(s_b, 1)
            dve.wait_ge(s_b, 1)
            dve.memset(sb["stat"][:], 0.0)

        @block.gpsimd
        def _(pool):
            pool.wait_ge(s_max, 1)
            pool.partition_all_reduce(sb["amaxall"][:], sb["amax"][:], P, bass.bass_isa.ReduceOp.max).then_inc(s_all, 1)


def quantise(nc, sb, sem, tag, src, dst, parts=P):
    s_r, s_q = sem("rounded_" + tag), sem("quantised_" + tag)
    W, N = 1024, TOK // 1024
    with nc.Block() as block:
        @block.scalar
        def _(act):
            def add_round(c, k):
                after(act, s_q, c - 1)
                act.activation(sb["rnd"][0:parts, k % 2, :], src[0:parts, bass.ds(c * W, W)], ACT.Identity,
                               bias=sb["roundc"][0:parts, 0:1], scale=sb["inv"][0:parts, 0:1]).then_inc(s_r, 1)

            add_round(0, 0)
            add_round(1, 1)
            with act.Fori(1, N // 2) as q:
                for u in range(2):
                    add_round(q * 2 + u, u)

        @block.vector
        def _(dve):
            with dve.Fori(0, N // 2) as q:
                for u in range(2):
                    c = q * 2 + u
                    dve.wait_ge(s_r, c + 1)
                    dve.tensor_scalar(dst[0:parts, bass.ds(c * W, W)], sb["rnd"][0:parts, u, :], ROUND, 127.0,
                                      ALU.subtract, ALU.min).then_inc(s_q, 1)


def bit_linear(nc, sb, ps, sem, tag, weight, bias, src, dst, parts=P):
    s_m, s_d, s_a = sem("mm_" + tag), sem("dst_" + tag), sem("absmax_" + tag)
    w = slice(WS[weight], WS[weight] + 1)
    with nc.Block() as block:
        @block.tensor
        def _(pe):
            def multiply(g, k):
                after(pe, s_d, g - 3)
                pe.matmul(ps[k % 4][:, :], lhsT=sb["t_" + weight][0:parts, 0:P],
                          rhs=src[0:parts, bass.ds(g * 512, 512)], start=True, stop=True).then_inc(s_m, 1)

            run_groups(pe, multiply, 0, 4)

        @block.scalar
        def _(act):
            def scale_out(g, k):
                act.wait_ge(s_m, g + 1)
                act.activation(dst[:, bass.ds(g * 512, 512)], ps[k % 4][:, :], ACT.Identity, bias=sb[bias][:, 0:1],
                               scale=sb["osc"][:, w]).then_inc(s_d, 1)

            run_groups(act, scale_out, 0, 4)

        @block.vector
        def _(dve):
            def absmax(g, k):
                dve.wait_ge(s_d, g + 1)
                dve.tensor_reduce(out=sb["stat"][:, bass.ds(g, 1)], in_=dst[:, bass.ds(g * 512, 512)], axis=AX.X,
                                  op=ALU.max, apply_absolute_value=True)

            run_groups(dve, absmax, 0)


def bit_attention(nc, sb, ps, sem, r, qimg):
    S = lambda n: sem(n + f"_r{r}")
    s_kt, s_ktc, s_kk, s_kkc, s_f = S("kT"), S("kT_ready"), S("k"), S("k_ready"), S("fused_copied")
    s_s, s_t, s_m, s_sh, s_e, s_su, s_rc, s_p = (S(n) for n in ("s", "s_masked", "s_max", "s_shift", "s_exp", "s_sum", "s_rec", "p"))
    s_pt, s_ptc, s_o, s_u = S("pT"), S("pT_ready"), S("o"), S("upd")
    name = f"att{r}"
    w = slice(WS[name], WS[name] + 1)
    fused = sb["G3"]
    kT, kk, fz, st, pT, mx, sm = (sb[n] for n in ("b_kT", "b_k", "b_f", "b_s", "b_pT", "b_mx", "b_sm"))
    KT, KK, SS, PT, OO = ps[0:5]
    c = DIM ** -0.5

    def tiles(ap):
        return ap.rearrange("p (j n) -> p j n", j=4)

    with nc.Block() as block:
        @block.tensor
        def _(pe):
            def keys(g, k):
                after(pe, s_ktc, g)
                pe.matmul(KT[:, :], lhsT=sb["t_" + name][:], rhs=qimg[:, bass.ds(g * 512, 512)],
                          start=True, stop=True).then_inc(s_kt, 1)
                after(pe, s_kkc, g)
                for j in range(4):
                    mm = pe.matmul(KK[:, P * j:P * j + P], lhsT=qimg[:, bass.ds(g * 512 + P * j, P)],
                                   rhs=sb["t_" + name][:], start=True, stop=True)
                mm.then_inc(s_kk, 1)

            def scores(g, k):
                pe.wait_ge(s_ktc, g + 1)
                pe.wait_ge(s_f, g + 1)
                after(pe, s_t, g)
                for j in range(4):
                    n = slice(P * j, P * j + P)
                    mm = pe.matmul(SS[:, n], lhsT=fz[:, k % 2, n], rhs=kT[:, k % 2, n], start=True, stop=True)
                mm.then_inc(s_s, 1)

            def turn(g, k):
                pe.wait_ge(s_p, g + 1)
                after(pe, s_ptc, g)
                for j in range(4):
                    n = slice(P * j, P * j + P)
                    mm = pe.transpose(PT[:, n], st[:, k % 2, n], sb["ident"][:])
                mm.then_inc(s_pt, 1)

            def mix(g, k):
                pe.wait_ge(s_ptc, g + 1)
                pe.wait_ge(s_kkc, g + 1)
                after(pe, s_u, g)
                for j in range(4):
                    n = slice(P * j, P * j + P)
                    mm = pe.matmul(OO[:, n], lhsT=kk[:, k % 4, n], rhs=pT[:, k % 2, n], start=True, stop=True)
                mm.then_inc(s_o, 1)

            def step(s, k):
                for lag, do in ((1, scores), (2, turn), (0, keys), (3, mix)):
                    g = group_of(s, lag)
                    if g is not None:
                        do(g, k - lag)

            run_groups(pe, step, 3, 4)

        @block.scalar
        def _(act):
            def copy_kT(g, k):
                act.wait_ge(s_kt, g + 1)
                after(act, s_s, g - 1)
                act.activation(kT[:, k % 2, :], KT[:, :], ACT.Identity, bias=sb[f"bb_{name}"][:, 0:1],
                               scale=sb["osc"][:, w]).then_inc(s_ktc, 1)

            def exps(g, k):
                act.wait_ge(s_sh, g + 1)
                act.activation(st[:, k % 2, :], st[:, k % 2, :], ACT.Exp).then_inc(s_e, 1)

            def copy_pT(g, k):
                act.wait_ge(s_pt, g + 1)
                after(act, s_o, g - 1)
                act.activation(pT[:, k % 2, :], PT[:, :], ACT.Copy).then_inc(s_ptc, 1)

            def step(s, k):
                for lag, do in ((2, copy_pT), (1, exps), (0, copy_kT)):
                    g = group_of(s, lag)
                    if g is not None:
                        do(g, k - lag)

            run_groups(act, step, 3, 4)

        @block.vector
        def _(dve):
            def copy_k(g, k):
                dve.wait_ge(s_kk, g + 1)
                after(dve, s_o, g - 3)
                dve.scalar_tensor_tensor(out=tiles(kk[:, k % 4, :]), in0=tiles(KK[:, :]), scalar=sb["osc"][:, w],
                                         in1=sb[f"bB_{name}"][:].unsqueeze(1).to_broadcast([P, 4, P]),
                                         op0=ALU.mult, op1=ALU.add).then_inc(s_kkc, 1)

            def shift(g, k):
                dve.wait_ge(s_s, g + 1)
                after(dve, s_pt, g - 1)
                v = tiles(st[:, k % 2, :])
                dve.scalar_tensor_tensor(out=v, in0=tiles(SS[:, :]), scalar=c,
                                         in1=sb["block_mask"][:].unsqueeze(1).to_broadcast([P, 4, P]),
                                         op0=ALU.mult, op1=ALU.add).then_inc(s_t, 1)
                dve.wait_ge(s_t, g + 1)
                dve.tensor_reduce(out=mx[:, k % 2, :], in_=v, axis=AX.X, op=ALU.max).then_inc(s_m, 1)
                dve.wait_ge(s_m, g + 1)
                dve.tensor_tensor(v, v, mx[:, k % 2, :].unsqueeze(2).to_broadcast([P, 4, P]),
                                  ALU.subtract).then_inc(s_sh, 1)

            def divide(g, k):
                dve.wait_ge(s_e, g + 1)
                v = tiles(st[:, k % 2, :])
                dve.tensor_reduce(out=sm[:, k % 2, :], in_=v, axis=AX.X, op=ALU.add).then_inc(s_su, 1)
                dve.wait_ge(s_su, g + 1)
                dve.reciprocal(sm[:, k % 2, :], sm[:, k % 2, :]).then_inc(s_rc, 1)
                dve.wait_ge(s_rc, g + 1)
                dve.tensor_tensor(v, v, sm[:, k % 2, :].unsqueeze(2).to_broadcast([P, 4, P]),
                                  ALU.mult).then_inc(s_p, 1)

            def update(g, k):
                dve.wait_ge(s_o, g + 1)
                v = fused[:, bass.ds(g * 512, 512)]
                dve.scalar_tensor_tensor(out=v, in0=OO[:, :], scalar=0.1, in1=v, op0=ALU.mult,
                                         op1=ALU.add).then_inc(s_u, 1)

            def step(s, k):
                for lag, do in ((1, shift), (0, copy_k), (1, divide), (3, update)):
                    g = group_of(s, lag)
                    if g is not None:
                        do(g, k - lag)

            run_groups(dve, step, 3, 4)
            dve.wait_ge(s_u, NG)
            dve.tensor_reduce(out=sb["stat"][:, 0:1], in_=fused[:], axis=AX.X, op=ALU.max, apply_absolute_value=True)

        @block.gpsimd
        def _(pool):
            def copy_fused(g, k):
                after(pool, s_s, g - 1)
                after(pool, s_f, g)
                pool.tensor_tensor(sb["scratch"][:], sb["zeros"][:, 0:1], sb["zeros"][:, 0:1], ALU.add)
                pool.tensor_copy(fz[:, k % 2, :], fused[:, bass.ds(g * 512, 512)]).then_inc(s_f, 1)

            run_groups(pool, copy_fused, 0)


def bitnet(nc, sb, ps, sem, next_phase):
    ctxT = sb["G1"]
    half = sb["G2"][:].bitcast(BF16)
    qa, qb = half[:, 0:TOK], half[:, TOK:2 * TOK]

    weights_to_ternary(nc, sb, sem)
    with nc.Block() as block:
        @block.vector
        def _(dve):
            dve.tensor_reduce(out=sb["stat"][0:CTX, 0:1], in_=ctxT[0:CTX, :], axis=AX.X, op=ALU.max,
                              apply_absolute_value=True)
    input_scale(nc, sb, sem, "ctx", "d2v")
    quantise(nc, sb, sem, "ctx", ctxT, qa, CTX)
    bit_linear(nc, sb, ps, sem, "vis", "d2v", "bb_d2v", qa, sb["G3"], CTX)
    input_scale(nc, sb, sem, "vis", "img")
    quantise(nc, sb, sem, "vis", sb["G3"], qb)
    bit_linear(nc, sb, ps, sem, "img", "img", "bb_img", qb, sb["G1"])
    input_scale(nc, sb, sem, "img", "att0")

    s_av = sem("averaged")
    with nc.Block() as block:
        @block.vector
        def _(dve):
            dve.tensor_copy(sb["osc_img"][:], sb["osc"][:])
            dve.tensor_reduce(out=sb["avg"][:], in_=sb["G1"][:].rearrange("p (b s) -> p b s", s=SEQ), axis=AX.X,
                              op=ALU.add).then_inc(s_av, 1)
            dve.wait_ge(s_av, 1)
            dve.tensor_scalar(sb["avg"][:], sb["avg"][:], 1.0 / SEQ, None, ALU.mult)
    quantise(nc, sb, sem, "img", sb["G1"], qa)
    turn_x(nc, sb, ps, sem, "text")
    input_scale(nc, sb, sem, "text", "txt")
    quantise(nc, sb, sem, "text", sb["G3"], qb)
    bit_linear(nc, sb, ps, sem, "txt", "txt", "bb_txt", qb, sb["G3"])
    with nc.Block() as block:
        @block.vector
        def _(dve):
            dve.tensor_copy(sb["osc"][:], sb["osc_img"][:])
            dve.memset(sb["stat"][:], 0.0)
    for r in range(2):
        next_phase()
        bit_attention(nc, sb, ps, sem, r, qa)
    with nc.Block() as block:
        @block.vector
        def _(dve):
            dve.tensor_reduce(out=sb["stat"][:, 1:2], in_=sb["avg"][:], axis=AX.X, op=ALU.max, apply_absolute_value=True)
    input_scale(nc, sb, sem, "cat", "f1")
    quantise(nc, sb, sem, "cat", sb["G3"], qa)
    s_ra = sem("avg_rounded")
    with nc.Block() as block:
        @block.vector
        def _(dve):
            dve.tensor_scalar(sb["avg"][:], sb["avg"][:], sb["inv"][:, 0:1], ROUND, ALU.mult, ALU.add).then_inc(s_ra, 1)
            dve.wait_ge(s_ra, 1)
            dve.tensor_scalar(sb["qavg"][:], sb["avg"][:], ROUND, 127.0, ALU.subtract, ALU.min)
    next_phase()
    bit_ffn(nc, sb, ps, sem, qa)


def turn_x(nc, sb, ps, sem, tag):
    s_norm, s_turn, s_ht = sem("t_normed" + tag), sem("t_turned" + tag), sem("t_ready" + tag)
    TB = ps[0:2]
    with nc.Block() as block:
        @block.vector
        def _(dve):
            def step(s, k):
                g = group_of(s, 0)
                if g is not None:
                    after(dve, s_turn, g - 1)
                    normalise_group(dve, sb, g, k, s_norm)
                g = group_of(s, 2)
                if g is not None:
                    dve.wait_ge(s_ht, g + 1)
                    dve.tensor_reduce(out=sb["stat"][:, bass.ds(g, 1)], in_=sb["G3"][:, bass.ds(g * 512, 512)],
                                      axis=AX.X, op=ALU.max, apply_absolute_value=True)

            run_groups(dve, step, 2)

        @block.tensor
        def _(pe):
            def turn(g, k):
                pe.wait_ge(s_norm, g + 1)
                after(pe, s_ht, g - 1)
                for j in range(4):
                    mm = pe.transpose(TB[k % 2][:, P * j:P * j + P], sb["xn4"][:, k % 2, j, :], sb["ident"][:])
                mm.then_inc(s_turn, 1)

            run_groups(pe, turn, 0)

        @block.scalar
        def _(act):
            def copy_ht(g, k):
                act.wait_ge(s_turn, g + 1)
                act.activation(sb["G3"][:, bass.ds(g * 512, 512)], TB[k % 2][:, :], ACT.Copy).then_inc(s_ht, 1)

            run_groups(act, copy_ht, 0)


def bit_ffn(nc, sb, ps, sem, qx):
    NC = FFN // P
    s_m, s_r = sem("f1_product"), sem("f1_max")
    s_a, s_b = sem("f1_maxed"), sem("f1_scaled")
    w1 = slice(WS["f1"], WS["f1"] + 1)
    w2 = slice(WS["f2"], WS["f2"] + 1)

    def product(pe, bank, g, c):
        pe.matmul(bank[:, :], lhsT=sb["t_f1"][:, P * c:P * c + P], rhs=qx[:, bass.ds(g * 512, 512)],
                  start=True, stop=False)
        return pe.matmul(bank[:, :].rearrange("p (b s) -> p b s", s=SEQ), lhsT=sb["t_f1"][:, FFN + P * c:FFN + P * c + P],
                         rhs=sb["qavg"][:, bass.ds(g * 8, 8)].unsqueeze(2).to_broadcast([P, 8, SEQ]),
                         start=False, stop=True)

    with nc.Block() as block:
        @block.tensor
        def _(pe):
            def products(g, k):
                for c in range(NC):
                    after(pe, s_r, g * NC + c - 3)
                    product(pe, ps[c], g, c).then_inc(s_m, 1)

            run_groups(pe, products, 0)

        @block.vector
        def _(dve):
            def maxima(g, k):
                for c in range(NC):
                    dve.wait_ge(s_m, g * NC + c + 1)
                    dve.tensor_reduce(out=sb["pmax"][:, c, bass.ds(g, 1)], in_=ps[c][:, :], axis=AX.X,
                                      op=ALU.max).then_inc(s_r, 1)

            run_groups(dve, maxima, 0)
            dve.wait_ge(s_r, NG * NC)
            dve.tensor_reduce(out=sb["hmax"][:], in_=sb["pmax"][:], axis=AX.X, op=ALU.max).then_inc(s_a, 1)
            dve.wait_ge(s_a, 1)
            dve.tensor_scalar(sb["hmax"][:], sb["hmax"][:], sb["osc"][:, w1], None, ALU.mult).then_inc(s_b, 1)
            dve.wait_ge(s_b, 1)
            dve.tensor_tensor(sb["hmax"][:], sb["hmax"][:], sb["bb_f1"][:], ALU.add).then_inc(s_b, 1)
            dve.wait_ge(s_b, 2)
            dve.tensor_copy(sb["stat"][:, 0:NC], sb["hmax"][:])
            dve.tensor_copy(sb["osc_img"][:], sb["osc"][:])
    input_scale(nc, sb, sem, "hid", "f2")

    s_m, s_h, s_n, s_q, s_o, s_y, s_x = (sem(n) for n in (
        "f2_product", "f2_relu", "f2_rounded", "f2_q", "f2_out", "f2_y", "f2_x"))
    hf, hq = sb["h_f"], sb["h_q"]
    x4 = sb["x"][:].rearrange("p (g j) f -> p g (j f)", j=4)
    OB = ps[4:6]
    with nc.Block() as block:
        @block.tensor
        def _(pe):
            def hidden(g, k):
                for c in range(NC):
                    after(pe, s_h, NC * g + c - 3)
                    product(pe, ps[c], g, c).then_inc(s_m, 1)

            def down(g, k):
                pe.wait_ge(s_q, NC * (g + 1))
                after(pe, s_y, g - 1)
                for j in range(4):
                    for c in range(NC):
                        mm = pe.matmul(OB[k % 2][:, P * j:P * j + P], lhsT=hq[:, k % 2, c, P * j:P * j + P],
                                       rhs=sb["t_f2"][:, P * c:P * c + P], start=(c == 0), stop=(c == NC - 1))
                mm.then_inc(s_o, 1)

            def step(s, k):
                for lag, do in ((0, hidden), (1, down)):
                    g = group_of(s, lag)
                    if g is not None:
                        do(g, k - lag)

            run_groups(pe, step, 1)

        @block.scalar
        def _(act):
            def relus(g, k):
                for c in range(NC):
                    act.wait_ge(s_m, g * NC + c + 1)
                    after(act, s_n, g * NC + c - 3)
                    act.activation(hf[:, c, :], ps[c][:, :], ACT.Relu, bias=sb["bb_f1"][:, c:c + 1],
                                   scale=sb["osc_img"][:, w1]).then_inc(s_h, 1)

            run_groups(act, relus, 0)

        @block.vector
        def _(dve):
            def quantise_hidden(g, k):
                after(dve, s_o, g - 1)
                for c in range(NC):
                    dve.wait_ge(s_h, NC * g + c + 1)
                    dve.tensor_scalar(sb["h_r"][:, c % 2, :], hf[:, c, :], sb["inv"][:, 0:1], ROUND,
                                      ALU.mult, ALU.add).then_inc(s_n, 1)
                    dve.wait_ge(s_n, NC * g + c + 1)
                    dve.tensor_scalar(hq[:, k % 2, c, :], sb["h_r"][:, c % 2, :], ROUND, 127.0,
                                      ALU.subtract, ALU.min).then_inc(s_q, 1)

            def update(g, k):
                dve.wait_ge(s_o, g + 1)
                dve.scalar_tensor_tensor(out=sb["h_y"][:].rearrange("p (j n) -> p j n", j=4),
                                         in0=OB[k % 2][:, :].rearrange("p (j n) -> p j n", j=4),
                                         scalar=sb["osc"][:, w2],
                                         in1=sb["bB_f2"][:].unsqueeze(1).to_broadcast([P, 4, P]),
                                         op0=ALU.mult, op1=ALU.add).then_inc(s_y, 1)
                dve.wait_ge(s_y, g + 1)
                dve.tensor_tensor(x4[:, g, :], sb["h_y"][:], x4[:, g, :], ALU.add).then_inc(s_x, 1)
                settle(dve, sb, s_x, g + 1)
                stats_of_group(dve, sb, g)

            def step(s, k):
                for lag, do in ((0, quantise_hidden), (1, update)):
                    g = group_of(s, lag)
                    if g is not None:
                        do(g, k - lag)

            run_groups(dve, step, 1)


def experts(nc, sb, ps, sem):
    names = ("normed", "turned", "ht", "logits", "lmax", "lshift", "lexp", "chain", "comb", "combT", "combT_ready",
             "gate", "up", "silu", "spread", "hid", "weighted", "down", "x", "stat", "mv", "turned_all")
    s = {n: sem("e_" + n) for n in names}
    NC, NR = HID_MOE // P, EXPERTS * MID // P
    x4 = sb["x"][:].rearrange("p (g j) f -> p g (j f)", j=4)
    hid, sg = sb["e_hid"], sb["e_sg"]
    CB, LB, DB, TB = ps[4], ps[5], ps[6], ps[7]
    CH = 16

    with nc.Block() as block:
        @block.tensor
        def _(pe):
            def turn(g, k):
                pe.wait_ge(s["normed"], g + 1)
                after(pe, s["ht"], g)
                for j in range(4):
                    mm = pe.transpose(TB[:, P * j:P * j + P], sb["xn4"][:, k % 2, j, :], sb["ident"][:])
                mm.then_inc(s["turned"], 1)

            def logits(g, k):
                pe.wait_ge(s["ht"], g + 1)
                after(pe, s["combT_ready"], g)
                for j in range(4):
                    mm = pe.matmul(LB[:, EXPERTS * j:EXPERTS * j + EXPERTS], lhsT=sb["hT4"][:, k % 2, P * j:P * j + P],
                                   rhs=sb["w_router"][:], start=True, stop=True)
                mm.then_inc(s["logits"], 1)

            def turn_comb(g, k):
                pe.wait_ge(s["comb"], g + 1)
                for j in range(4):
                    mm = pe.transpose(LB[0:EXPERTS, P * j:P * j + P], sb["r_comb"][:, k % 2, j, :], sb["ident"][:])
                mm.then_inc(s["combT"], 1)

            def spread(g, k, c):
                if c == 0:
                    pe.wait_ge(s["combT_ready"], g + 1)
                after(pe, s["weighted"], NR * g + c)
                pe.matmul(CB[:, :], lhsT=sb["sel_m"][:, c, :], rhs=sb["r_combT"][:], start=True,
                          stop=True).then_inc(s["spread"], 1)

            def gate_up(g, k, c):
                pe.wait_ge(s["ht"], g + 1)
                a = 2 * ((NC * k + c) % 2)
                b = a + 1
                after(pe, s["hid"], g * NC + c - 1)
                rhs = sb["hT4"][:, k % 2, :]
                pe.matmul(ps[a][:, :], lhsT=sb["w_gate"][:, c, :], rhs=rhs, start=True, stop=True).then_inc(s["gate"], 1)
                pe.matmul(ps[b][:, :], lhsT=sb["w_up"][:, c, :], rhs=rhs, start=True, stop=True).then_inc(s["up"], 1)

            def down(g, k):
                pe.wait_ge(s["weighted"], NR * (g + 1))
                after(pe, s["x"], g)
                for j in range(4):
                    for c in range(NC):
                        mm = pe.matmul(DB[:, P * j:P * j + P], lhsT=hid[:, k % 2, c, P * j:P * j + P],
                                       rhs=sb["w_down"][:, c, :], start=(c == 0), stop=(c == NC - 1))
                mm.then_inc(s["down"], 1)

            def step(st, k):
                g3, g2, g1 = group_of(st, 3), group_of(st, 2), group_of(st, 1)
                if g3 is not None:
                    turn_comb(g3, k - 3)
                for c in range(NC):
                    if g3 is not None and c < NR:
                        spread(g3, k - 3, c)
                    if g2 is not None:
                        gate_up(g2, k - 2, c)
                if g2 is not None:
                    logits(g2, k - 2)
                if g3 is not None:
                    down(g3, k - 3)
                if g1 is not None:
                    turn(g1, k - 1)

            run_groups(pe, step, 4)

        @block.scalar
        def _(act):
            def copy_ht(g, k):
                act.wait_ge(s["turned"], g + 1)
                after(act, s["logits"], g - 1)
                after(act, s["up"], NC * (g - 1))
                act.activation(sb["hT4"][:, k % 2, :], TB[:, :], ACT.Copy).then_inc(s["ht"], 1)

            def copy_combT(g, k):
                act.wait_ge(s["combT"], g + 1)
                after(act, s["spread"], NR * g)
                act.activation(sb["r_combT"][:], LB[0:EXPERTS, :], ACT.Copy).then_inc(s["combT_ready"], 1)

            def silus(g, k):
                for c in range(NC):
                    act.wait_ge(s["gate"], NC * g + c + 1)
                    after(act, s["hid"], NC * g + c - 1)
                    act.activation(sg[:, (NC * k + c) % 2, :], ps[2 * ((NC * k + c) % 2)][:, :], ACT.Silu).then_inc(s["silu"], 1)

            def exps(g, k):
                act.wait_ge(s["lshift"], g + 1)
                act.activation(sb["r_p"][:], sb["r_p"][:], ACT.Exp).then_inc(s["lexp"], 1)

            def step(st, k):
                for lag, do in ((3, copy_combT), (2, silus), (2, exps), (1, copy_ht)):
                    g = group_of(st, lag)
                    if g is not None:
                        do(g, k - lag)

            run_groups(act, step, 4)

        @block.vector
        def _(dve):
            R = lambda ap: ap.unsqueeze(2).to_broadcast([P, 4, EXPERTS])
            p, e, oh1, oh2 = sb["r_p"], sb["r_e"], sb["r_oh1"], sb["r_oh2"]
            m1, m2, den, first = sb["r_m1"], sb["r_m2"], sb["r_den"], sb["r_first"]
            order = sb["order"][:].unsqueeze(1).to_broadcast([P, 4, EXPERTS])

            def normalise(g, k):
                after(dve, s["turned"], g - 1)
                normalise_group(dve, sb, g, k, s["normed"])

            def route(g, k):
                n = [0]

                def link(ins):
                    n[0] += 1
                    ins.then_inc(s["chain"], 1)
                    dve.wait_ge(s["chain"], g * CHAIN + n[0])

                dve.wait_ge(s["logits"], g + 1)
                lg = LB[:, 0:4 * EXPERTS].rearrange("p (j e) -> p j e", e=EXPERTS)
                link(dve.tensor_reduce(out=m1[:], in_=lg, axis=AX.X, op=ALU.max))
                dve.tensor_tensor(p[:], lg, R(m1[:]), ALU.subtract).then_inc(s["lshift"], 1)
                dve.wait_ge(s["lexp"], g + 1)
                link(dve.tensor_reduce(out=den[:], in_=p[:], axis=AX.X, op=ALU.add))
                link(dve.reciprocal(den[:], den[:]))
                link(dve.tensor_tensor(p[:], p[:], R(den[:]), ALU.mult))
                link(dve.tensor_reduce(out=m1[:], in_=p[:], axis=AX.X, op=ALU.max))
                link(dve.tensor_tensor(e[:], p[:], R(m1[:]), ALU.is_ge))
                link(dve.tensor_tensor(e[:], e[:], order, ALU.mult))
                link(dve.tensor_reduce(out=first[:], in_=e[:], axis=AX.X, op=ALU.max))
                link(dve.tensor_tensor(oh1[:], order, R(first[:]), ALU.is_equal))
                link(dve.scalar_tensor_tensor(out=oh2[:], in0=oh1[:], scalar=-2.0, in1=p[:], op0=ALU.mult, op1=ALU.add))
                link(dve.tensor_reduce(out=m2[:], in_=oh2[:], axis=AX.X, op=ALU.max))
                link(dve.tensor_tensor(e[:], oh2[:], R(m2[:]), ALU.is_ge))
                link(dve.tensor_tensor(e[:], e[:], order, ALU.mult))
                link(dve.tensor_reduce(out=first[:], in_=e[:], axis=AX.X, op=ALU.max))
                link(dve.tensor_tensor(oh2[:], order, R(first[:]), ALU.is_equal))
                link(dve.tensor_tensor(oh1[:], oh1[:], oh2[:], ALU.add))
                link(dve.scalar_tensor_tensor(out=den[:], in0=m1[:], scalar=1e-9, in1=m2[:], op0=ALU.add, op1=ALU.add))
                link(dve.reciprocal(den[:], den[:]))
                link(dve.tensor_tensor(p[:], p[:], oh1[:], ALU.mult))
                after(dve, s["combT"], g - 1)
                dve.tensor_tensor(sb["r_comb"][:, k % 2], p[:], R(den[:]), ALU.mult).then_inc(s["comb"], 1)
                assert n[0] == CHAIN

            CHAIN = 19

            def weigh(g, k, c):
                dve.wait_ge(s["spread"], NR * g + c + 1)
                v = hid[:, k % 2, c, :]
                dve.tensor_tensor(v, CB[:, :], v, ALU.mult).then_inc(s["weighted"], 1)

            def hidden(g, k, c):
                dve.wait_ge(s["silu"], NC * g + c + 1)
                dve.wait_ge(s["up"], NC * g + c + 1)
                after(dve, s["down"], g - 1)
                dve.tensor_tensor(hid[:, k % 2, c, :], ps[2 * ((NC * k + c) % 2) + 1][:, :], sg[:, (NC * k + c) % 2, :],
                                  ALU.mult).then_inc(s["hid"], 1)

            def update(g, k):
                dve.wait_ge(s["down"], g + 1)
                dve.tensor_tensor(x4[:, g, :], DB[:, :], x4[:, g, :], ALU.add).then_inc(s["x"], 1)

            def step(st, k):
                g3, g2, g0 = group_of(st, 3), group_of(st, 2), group_of(st, 0)
                for c in range(NC):
                    if g3 is not None and c < NR:
                        if c == 0:
                            dve.wait_ge(s["hid"], NC * (g3 + 1))
                        weigh(g3, k - 3, c)
                    if g2 is not None:
                        hidden(g2, k - 2, c)
                if g2 is not None:
                    route(g2, k - 2)
                if g3 is not None:
                    update(g3, k - 3)
                if g0 is not None:
                    normalise(g0, k)

            run_groups(dve, step, 4)


def decoder_kernel(nc, d, out, upto=6):
    with ExitStack() as ctx:
        sb = {}

        def sbuf(name, shape, dt=F32):
            sb[name] = ctx.enter_context(nc.sbuf_tensor("sb_" + name, shape, dt))
            return sb[name]

        held = []

        def sem(name):
            held.append(nc.alloc_semaphore(name))
            return held[-1]

        def next_phase():
            nc.clear_and_free_semaphores(list(held))
            held.clear()
            nc.all_engine_barrier()

        banks = ctx.enter_context(nc.psum_tensor("banks", [P, 8, 512], F32))
        ps = [banks[:, i, :] for i in range(8)]
        sb["banks"] = banks
        sbuf("x", [P, NT, DIM])
        for g in ("G1", "G2", "G3"):
            sbuf(g, [P, TOK])
        sb["G3v"] = sb["G3"][:].rearrange("p (t f) -> p t f", f=DIM)
        used = 0
        for name, shape in SMALL.items():
            if name not in EARLY:
                sbuf(name, list(shape))
                continue
            width = int(shape[1]) * (int(shape[2]) if len(shape) == 3 else 1)
            view = sb["G2"][0:shape[0], used:used + width]
            sb[name] = view if len(shape) == 2 else view.rearrange("p (c n) -> p c n", c=shape[1])
            used += width
        sbuf("st6", [P, NT, 6])
        for name in ("mean", "rstd", "nmr", "dif", "var"):
            sbuf(name, [P, NT])
        sbuf("scratch", [P, 1])
        sbuf("own_half", [P, 2])
        sbuf("ones_row", [1, P])
        sbuf("zeros", [P, 64])
        sbuf("bqs_x0", [P, 1])
        sbuf("bqs_a1", [P, 1])
        sbuf("vblk", [P, 2, 4, 2, PAIRS, 2 * VW], BF16)
        sbuf("v32", [P, 2, 2, PAIRS, 2, HD])
        sbuf("biasP", [P, 2, PAIRS, P], BF16)
        for layer in LAYERS:
            sbuf("bkm_" + layer, [P, 4])
        ring = sbuf("ring", [P, 7744])
        at = [0]

        def part(name, *shape):
            n = 1
            for v in shape:
                n *= v
            names = "abc"[:len(shape)]
            sb[name] = ring[:, at[0]:at[0] + n].rearrange(
                f"p ({' '.join(names)}) -> p {' '.join(names)}", **dict(zip(names, shape)))
            at[0] += n

        part("xn", 2, P)
        part("hT", 2, P)
        part("cT", 4, P)
        part("vp", 2, P)
        part("qT", 2, P)
        part("km", 2, 4, P)
        part("sx", 2, 1024)
        sb["pt"] = ring[:, at[0]:at[0] + 2048].bitcast(BF16).rearrange("p (h r n) -> p h r n", h=2, r=2)
        at[0] += 2048
        part("y", 2, P)
        part("yT", 2, P)
        part("nmx", 2, HEADS)
        part("rec", 2, HEADS)
        at[0] = 0
        part("xn4", 2, 4, P)
        part("hT4", 2, 512)
        part("sT", 2, 512)
        part("e_sg", 2, 512)
        sb["r_combT"] = ring[0:EXPERTS, at[0]:at[0] + 512]
        at[0] = 0
        part("b_kT", 2, 512)
        part("b_k", 4, 512)
        part("b_f", 2, 512)
        part("b_s", 2, 512)
        part("b_pT", 2, 512)
        part("b_mx", 2, 4)
        part("b_sm", 2, 4)
        at[0] = 0
        part("rnd", 2, 1024)
        part("wtmp", 1024)
        at[0] = 0
        part("h_f", 4, 512)
        part("h_r", 2, 512)
        part("h_y", 512)
        sb["h_q"] = ring[:, at[0]:at[0] + 2048].bitcast(BF16).rearrange("p (a b c) -> p a b c", a=2, b=4)
        sb["e_hid"] = sb["G1"][:, 0:2 * 5 * 512].rearrange("p (a b c) -> p a b c", a=2, b=5)

        for name, width in (("wsum", 7), ("wall", 7), ("wscale", 7), ("wthr", 7), ("wnthr", 7), ("osc", 7),
                            ("osc_img", 7), ("roundc", 1), ("stat", 16), ("amax", 1), ("amaxall", 1), ("isc", 1),
                            ("inv", 1), ("avg", BATCH), ("hmax", 4)):
            sbuf(name, [P, width])
        sbuf("pmax", [P, 4, NG])
        sbuf("qavg", [P, BATCH], BF16)
        sbuf("row", [1, DIM])
        for n in WS:
            sbuf("t_" + n, [P, SMALL["b_" + n][1]], BF16)
        for n in ("r_p", "r_e", "r_oh1", "r_oh2"):
            sbuf(n, [P, 4, EXPERTS])
        for n in ("r_m1", "r_m2", "r_den", "r_first"):
            sbuf(n, [P, 4])
        sbuf("r_comb", [P, 2, 4, EXPERTS])

        load_inputs(nc, sb, sem, d)
        set_constants(nc, sb, sem)
        first_stats(nc, sb, sem)
        mean_and_rstd(nc, sb, sem, "ln1", LN_EPS)
        attention(nc, sb, ps, sem, "a0")
        mean_and_rstd(nc, sb, sem, "ln1o", 1e-3)
        second_norm(nc, sb, sem)
        if upto >= 2:
            next_phase()
            mean_and_rstd(nc, sb, sem, "ln2", LN_EPS)
            attention(nc, sb, ps, sem, "x0")
        if upto >= 3:
            next_phase()
            mean_and_rstd(nc, sb, sem, "ln3", LN_EPS)
            shrink_ffn(nc, sb, ps, sem)
        if upto >= 4:
            next_phase()
            mean_and_rstd(nc, sb, sem, "ln4", LN_EPS)
            attention(nc, sb, ps, sem, "a1")
        if upto >= 5:
            next_phase()
            mean_and_rstd(nc, sb, sem, "ln5", LN_EPS)
            bitnet(nc, sb, ps, sem, next_phase)
        if upto >= 6:
            next_phase()
            mean_and_rstd(nc, sb, sem, "ln6", LN_EPS)
            experts(nc, sb, ps, sem)
        store(nc, sb, sem, out)
        next_phase()


EARLY = ("biasT", "sel_e", "w_out", "b_d2v", "b_img", "b_txt", "b_att0", "b_att1", "b_f1", "b_f2")

SMALL = {
    "ident": (P, P), "head_mask": (P, 4), "alibi": (P, HEADS * SEQ), "biasT": (P, PAIRS, P),
    "gammaB": (P, DIM), "betaB": (P, DIM),
    "wq_a0": (P, P), "wk_a0": (P, P), "wv_a0": (P, 2, 64), "bv_a0": (P, P),
    "wq_x0": (P, P), "wk_x0": (CTX, P), "wv_x0": (CTX, 2, 64), "wo_x0": (P, P),
    "bq_x0": (P, 1), "bk_x0": (P, 1), "bv_x0": (P, P), "bo_x0": (1, P),
    "wq_a1": (P, P), "wk_a1": (P, P), "wv_a1": (P, 2, 64), "wo_a1": (P, P),
    "w_in": (P, M_SHRINK), "b_in": (M_SHRINK, 1), "sel_e": (M_SHRINK, 8, P), "w_1": (P, 8), "b_1": (P, 8),
    "w_2": (P, 8), "b_2": (M_SHRINK, 1), "w_outp": (M_SHRINK, DIM), "w_out": (P, 8, DIM), "b_out": (1, DIM),
    "b_d2v": (CTX, P), "b_img": (P, P), "b_txt": (P, P), "b_att0": (P, P), "b_att1": (P, P),
    "b_f1": (P, 2 * FFN), "b_f2": (P, FFN), "block_mask": (P, P),
    "bb_d2v": (P, 1), "bb_img": (P, 1), "bb_txt": (P, 1), "bb_att0": (P, 1), "bb_att1": (P, 1),
    "bB_att0": (P, P), "bB_att1": (P, P), "bb_f1": (P, 4), "bB_f2": (P, P),
    "w_router": (P, EXPERTS), "order": (P, EXPERTS), "sel_m": (EXPERTS, 4, P),
    "w_gate": (P, 5, P), "w_up": (P, 5, P), "w_down": (P, 5, DIM),
    "bq_a1": (P, 1), "bk_a1": (P, 1), "bv_a1": (P, P), "bo_a1": (1, P),
}


def laid_out(i):
    import numpy as np

    f = np.float32
    o = {}
    o["x"] = np.ascontiguousarray(i["x"].reshape(NT, P, DIM).transpose(1, 0, 2))
    o["ctxT"] = np.ascontiguousarray(i["ctx_768"].reshape(TOK, CTX).T)
    o["ident"] = np.eye(P, dtype=f)
    p = np.arange(P)
    o["head_mask"] = (((p % 32) // HD)[:, None] == np.arange(4)[None, :]).astype(f)
    slopes = (2.0 ** (-(8.0 / HEADS) * np.arange(1, HEADS + 1))).astype(f)
    pos = np.arange(SEQ)
    alibi = slopes[None, :, None] * pos[None, None, :].astype(f)
    alibi = np.where(pos[None, None, :] <= (p % SEQ)[:, None, None], alibi, f(-1e30)).astype(f)
    o["alibi"] = alibi.reshape(P, HEADS * SEQ)
    h, q, k = np.arange(HEADS)[:, None, None], pos[None, :, None], pos[None, None, :]
    table = i["L0_attn_rel_table"].reshape(-1)
    flat = h * SEQ * SEQ + q * SEQ + k
    qi, kj, hh = flat // (SEQ * HEADS), (flat // HEADS) % SEQ, flat % HEADS
    bias = table[(kj - qi + SEQ - 1) * HEADS + hh]
    bias = bias.reshape(PAIRS, 2, SEQ, SEQ).transpose(1, 3, 0, 2).reshape(P, PAIRS, SEQ)
    o["biasT"] = np.concatenate([bias, bias], axis=2)
    o["gammaB"] = np.tile(i["L0_attn_gamma"][None], (P, 1))
    o["betaB"] = np.tile(i["L0_attn_beta"][None], (P, 1))

    def values(w):
        return np.ascontiguousarray(w.reshape(-1, PAIRS, 2, HD).transpose(0, 2, 1, 3).reshape(-1, 2, 64))

    def value_bias(b):
        both = b.reshape(PAIRS, 2, HD).transpose(1, 0, 2).reshape(2, 1, 1, 64)
        return np.ascontiguousarray(np.broadcast_to(both, (2, 64, 2, 64)).reshape(P, P))

    o["wq_a0"], o["wk_a0"], o["wv_a0"] = i["L0_attn_Wq"], i["L0_attn_Wk"], values(i["L0_attn_Wv"])
    o["bv_a0"] = np.zeros((P, P), f)
    o["wq_x0"], o["wk_x0"], o["wv_x0"] = i["L0_xattn_wq"], i["L0_xattn_wk"], values(i["L0_xattn_wv"])
    o["wo_x0"], o["bo_x0"] = i["L0_xattn_wo"], i["L0_xattn_bo"][None]
    o["bq_x0"], o["bk_x0"] = i["L0_xattn_bq"][:, None], i["L0_xattn_bk"][:, None]
    o["bv_x0"] = value_bias(i["L0_xattn_bv"])
    w, b = i["L1_attn_w_attn"], i["L1_attn_b_attn"]
    o["wq_a1"], o["wk_a1"], o["wv_a1"] = w[:, 0:P], w[:, P:2 * P], values(w[:, 2 * P:])
    o["wo_a1"], o["bo_a1"] = i["L1_attn_w_proj"], i["L1_attn_b_proj"][None]
    o["bq_a1"], o["bk_a1"], o["bv_a1"] = b[0:P, None], b[P:2 * P, None], value_bias(b[2 * P:])

    def columns(a):
        return a.reshape(-1, P).T

    hid = np.arange(M_SHRINK * INNER).reshape(8, P)
    o["w_in"], o["b_in"] = i["L0_ffn_Win"], i["L0_ffn_bin_"][:, None]
    o["sel_e"] = (np.arange(M_SHRINK)[:, None, None] == hid[None] // INNER).astype(f)
    o["w_1"], o["b_1"], o["w_2"] = columns(i["L0_ffn_W1"]), columns(i["L0_ffn_b1"]), columns(i["L0_ffn_W2"])
    o["b_2"], o["w_outp"], o["b_out"] = i["L0_ffn_b2"][:, None], i["L0_ffn_Wout"], i["L0_ffn_bout"][None]
    o["w_out"] = i["L0_ffn_Wout"][hid // INNER].transpose(1, 0, 2)

    w = {n: i["L1_xattn_W_" + n].T for n in ("d2v", "img", "txt", "att0", "att1")}
    o["b_d2v"], o["b_img"], o["b_txt"] = w["d2v"], w["img"], w["txt"]
    for n in ("att0", "att1"):
        o["b_" + n] = np.concatenate([w[n], w[n]], axis=1)
        b = i["L1_xattn_b_" + n]
        o["bb_" + n] = np.concatenate([b, b])[:, None]
        o["bB_" + n] = np.tile(np.concatenate([b, b])[None], (P, 1))
    o["b_f1"] = i["L1_xattn_W_f1"].T.reshape(2, P, FFN).transpose(1, 0, 2).reshape(P, 2 * FFN)
    o["b_f2"] = i["L1_xattn_W_f2"].T.reshape(4, P, P).transpose(1, 0, 2).reshape(P, FFN)
    for n in ("d2v", "img", "txt"):
        o["bb_" + n] = i["L1_xattn_b_" + n][:, None]
    o["bb_f1"] = columns(i["L1_xattn_b_f1"])
    o["bB_f2"] = np.tile(i["L1_xattn_b_f2"][None], (P, 1))
    batch = p // SEQ
    o["block_mask"] = np.where(batch[:, None] == batch[None], f(0), f(-1e30)).astype(f)

    def hidden(routed, shared):
        r = i[routed].transpose(1, 0, 2).reshape(P, EXPERTS * MID)
        s = i[shared].transpose(1, 0, 2).reshape(P, P)
        return np.concatenate([r, s], axis=1).reshape(P, 5, P)

    o["w_router"] = i["L1_ffn_router_w"]
    o["order"] = np.tile(np.arange(EXPERTS, 0, -1)[None].astype(f), (P, 1))
    o["sel_m"] = (np.arange(EXPERTS)[:, None, None]
                  == np.arange(EXPERTS * MID).reshape(4, P)[None] // MID).astype(f)
    o["w_gate"], o["w_up"] = hidden("L1_ffn_wg_r", "L1_ffn_wg_s"), hidden("L1_ffn_wu_r", "L1_ffn_wu_s")
    down = np.concatenate([i["L1_ffn_wd_r"].reshape(-1, DIM), i["L1_ffn_wd_s"].reshape(-1, DIM)])
    o["w_down"] = down.reshape(5, P, DIM).transpose(1, 0, 2)
    return {k: np.ascontiguousarray(v) for k, v in o.items()}


def kernel(**inputs):
    import numpy as _np
    import concourse.bacc as _bacc
    from concourse.bass_utils import run_bass_kernel_spmd as _run

    arrays = laid_out({k: _np.asarray(v) for k, v in inputs.items()})
    nc = _bacc.Bacc("TRN2", target_bir_lowering=False, num_devices=1)
    d = {k: nc.dram_tensor("in_" + k, v.shape, F32, kind="ExternalInput").ap() for k, v in arrays.items()}
    d["_small"] = [k for k in arrays if k not in ("x", "ctxT")]
    out = nc.dram_tensor("out_x", (P, NT, DIM), F32, kind="ExternalOutput").ap()
    decoder_kernel(nc, d, out)
    r = _run(nc, [{"in_" + k: v for k, v in arrays.items()}], core_ids=[0])
    return r.results[0]["out_x"].transpose(1, 0, 2).reshape(BATCH, SEQ, DIM)
```

```python
import concourse.bass as bass
from concourse import mybir
from contextlib import ExitStack

F32 = mybir.dt.float32
BF16 = mybir.dt.bfloat16
ACT = mybir.ActivationFunctionType
ALU = mybir.AluOpType
AX = mybir.AxisListType

P = 128
BATCH, SEQ, DIM, CTX = 128, 64, 128, 96
TOK = BATCH * SEQ
NT = TOK // P
NG = TOK // 512
HEADS, HD = 16, 8
PAIRS = HEADS // 2
VW = HD + 1
M_SHRINK, INNER = 64, 16
FFN = 512
EXPERTS, MID = 16, 32
HID_MOE = EXPERTS * MID + 2 * 64
LN_EPS = 1e-5
ROUND = 12582912.0

LAYERS = ("a0", "x0", "a1")


def after(eng, sem, count):
    if isinstance(count, int) and count <= 0:
        return
    eng.wait_ge(sem, count)


def tile_of(step, lag):
    t = step - lag
    if isinstance(t, int) and not 0 <= t < NT:
        return None
    return t


def run_steps(eng, body, last_lag):
    for s in range(8):
        body(s, s)
    with eng.Fori(2, NT // 4) as q:
        for u in range(4):
            body(q * 4 + u, u)
    for s in range(NT, NT + last_lag):
        body(s, s)


def load_inputs(nc, sb, sem, d):
    PARTS = 8
    x_loaded = [sem(f"x_loaded_{c}") for c in range(PARTS)]
    loaded = sem("loaded")
    n = NT // PARTS
    with nc.Block() as block:
        @block.sync
        def _(sp):
            for c in range(PARTS):
                sp.dma_start(sb["x"][:, n * c:n * c + n, :], d["x"][:, n * c:n * c + n, :]).then_inc(x_loaded[c], 16)
            for name in d["_small"]:
                sp.dma_start(sb[name][:], d[name]).then_inc(loaded, 16)
            sp.dma_start(sb["G1"][0:CTX, :], d["ctxT"]).then_inc(loaded, 16)
            sp.wait_ge(loaded, 16 * (len(d["_small"]) + 1))

        @block.vector
        def _(dve):
            for c in range(PARTS):
                dve.wait_ge(x_loaded[c], 16)
                with dve.Fori(0, n // 4) as q:
                    for u in range(4):
                        t = q * 4 + (n * c + u)
                        dve.bn_stats(sb["st6"][:, t, :], sb["x"][:, t, :])


def set_constants(nc, sb, sem):
    made = sem("made")
    with nc.Block() as block:
        @block.vector
        def _(dve):
            dve.memset(sb["ones_row"][:], 1.0)
            dve.memset(sb["zeros"][:], 0.0)
            dve.memset(sb["bkm_a0"][:], 0.0)
            dve.memset(sb["own_half"][:], 0.0)
            dve.memset(sb["vblk"][:], 0.0).then_inc(made, 1)
            dve.wait_ge(made, 1)
            for i in range(2):
                h = slice(64 * i, 64 * i + 64)
                dve.memset(sb["vblk"][h, 0, :, :, :, i * VW + HD:i * VW + VW], 1.0)
                dve.memset(sb["own_half"][h, i:i + 1], 1.0)
            for layer in ("x0", "a1"):
                dve.tensor_scalar(sb["bkm_" + layer][:], sb["head_mask"][:], sb["bk_" + layer][:, 0:1], None, ALU.mult)
            dve.tensor_copy(sb["biasP"][:, 0], sb["biasT"][:]).then_inc(made, 1)
            dve.wait_ge(made, 2)
            dve.tensor_tensor(sb["biasP"][:, 1], sb["biasT"][:], sb["biasP"][:, 0], ALU.subtract)
            dve.tensor_copy(sb["row_of"][:], sb["row_of32"])
            dve.tensor_copy(sb["alibi"][:], sb["alibi32"])
            for layer, scale in (("x0", HD ** -0.5), ("a1", HD ** -0.5)):
                dve.tensor_scalar(sb["bqs_" + layer][:], sb["bq_" + layer][:], scale, None, ALU.mult)


def settle(dve, sb, sem, count):
    after(dve, sem, count)
    dve.memset(sb["scratch"][:], 0.0)


def mean_and_rstd(nc, sb, sem, name, eps):
    s_in, s_d, s_v, s_rooted, s_inv = (sem(name + n) for n in ("_halves", "_squares", "_variance", "_rooted", "_inverted"))
    st6, mean, rstd, dif, var = (sb[n] for n in ("st6", "mean", "rstd", "dif", "var"))
    with nc.Block() as block:
        @block.vector
        def _(dve):
            dve.tensor_tensor(mean[:], st6[:, :, 1], st6[:, :, 4], ALU.add)
            dve.tensor_tensor(dif[:], st6[:, :, 1], st6[:, :, 4], ALU.subtract)
            dve.tensor_tensor(var[:], st6[:, :, 2], st6[:, :, 5], ALU.add).then_inc(s_in, 1)
            dve.wait_ge(s_in, 1)
            dve.tensor_scalar(mean[:], mean[:], 0.5, None, ALU.mult)
            dve.tensor_tensor(dif[:], dif[:], dif[:], ALU.mult)
            dve.tensor_scalar(var[:], var[:], 1.0 / DIM, eps, ALU.mult, ALU.add).then_inc(s_d, 1)
            dve.wait_ge(s_d, 1)
            dve.scalar_tensor_tensor(out=var[:], in0=dif[:], scalar=0.25, in1=var[:], op0=ALU.mult,
                                     op1=ALU.add).then_inc(s_v, 1)
            dve.wait_ge(s_rooted, 1)
            dve.reciprocal(rstd[:], rstd[:]).then_inc(s_inv, 1)
            dve.wait_ge(s_inv, 1)
            dve.scalar_tensor_tensor(out=sb["nmr"][:], in0=mean[:], scalar=-1.0, in1=rstd[:], op0=ALU.mult,
                                     op1=ALU.mult)

        @block.scalar
        def _(act):
            act.wait_ge(s_v, 1)
            act.activation(rstd[:], var[:], ACT.Sqrt).then_inc(s_rooted, 1)


def attention(nc, sb, ps, sem, layer):
    cross, causal, plain = layer == "x0", layer == "a1", layer == "a0"
    S = lambda n: sem(n + "_" + layer)
    s_norm, s_ctx, s_turn, s_ht, s_proj = S("normed"), S("ctx_copied"), S("turned"), S("ht_ready"), S("projected")
    s_q, s_k, s_v, s_vb = S("q_ready"), S("k_ready"), S("v_ready"), S("v_split")
    s_sc, s_max, s_sub = S("scored"), S("maxed"), S("shifted")
    s_exp, s_pt, s_pe, s_mix = S("exp_ready"), S("p_turned"), S("pt_high"), S("mixed")
    s_pl, s_vh, s_vm = S("pt_low"), S("v_high"), S("v_placed")
    s_rec, s_y, s_yb = S("sum_inverted"), S("y_ready"), S("y_biased")
    s_yt, s_yc, s_out, s_x = S("y_turned"), S("yt_ready"), S("out_ready"), S("x_updated")
    x, ctxT, ao = sb["x"], sb["G1"], sb["G3v"]
    wq, wk, wv = sb["wq_" + layer], sb["wk_" + layer], sb["wv_" + layer]
    bkm, bv = sb["bkm_" + layer], sb["bv_" + layer]
    xn, hT, cT, qT, km, v32, vb = sb["xn"], sb["hT"], sb["cT"], sb["qT"], sb["km"], sb["v32"], sb["vblk"]
    vp = sb["vp"]
    sx, pt, y, yT, nmx, rec = sb["sx"], sb["pt"], sb["y"], sb["yT"], sb["nmx"], sb["rec"]
    SB, TB, PB, OB = ps[0:4], ps[4:6], ps[6], ps[7]
    XT, YT = SB[0][:, 256:384], SB[1][:, 256:384]
    s_free = s_sub
    LAST = 6 if plain else 7
    MO = OB[:, 0:288].rearrange("p (b n) -> p b n", b=2)
    MB = SB[3][:, 256:512].rearrange("p (b c i d) -> p b c i d", b=2, c=PAIRS, i=2)
    scale = DIM ** -0.5 if plain else HD ** -0.5

    with nc.Block() as block:
        @block.tensor
        def _(pe):
            def turn(t, k):
                pe.wait_ge(s_norm, t + 1)
                after(pe, s_ht, t)
                after(pe, s_free, 4 * (t - (3 if plain else 2)) + 1)
                pe.transpose(XT, xn[:, k % 2, :], sb["ident"][:]).then_inc(s_turn, 1)

            def project(t, k):
                if t is None:
                    return
                pe.wait_ge(s_ht, t + 1)
                after(pe, s_q, t)
                after(pe, s_k, t)
                after(pe, s_v, t)
                if cross:
                    pe.wait_ge(s_ctx, t + 1)
                src = cT[0:CTX, k % 4] if cross else hT[:, k % 2]
                pe.matmul(PB[:, 0:128], lhsT=wq[:], rhs=hT[:, k % 2], start=True, stop=True)
                pe.matmul(PB[:, 128:256], lhsT=wk[:], rhs=src, start=True, stop=True)
                for b in range(2):
                    for i in range(2):
                        mm = pe.matmul(PB[64 * i:64 * i + 64, 256 + 64 * b:320 + 64 * b],
                                       lhsT=src[:, 64 * b:64 * b + 64], rhs=wv[:, i, :], start=True, stop=True)
                mm.then_inc(s_proj, 1)

            def score(t, k, between):
                pe.wait_ge(s_q, t + 1)
                pe.wait_ge(s_k, t + 1)
                for g in range(4):
                    after(pe, s_free, 4 * (t - 1) + g + 1 if not isinstance(t, int) or t else 0)
                    if g == 0:
                        n = 3 if plain else 2
                        after(pe, s_ht, t + n if not isinstance(t, int) or t + n <= NT else NT)
                    if g == 1 and not plain:
                        after(pe, s_yc, t - 3)
                    if g == 2 and not plain:
                        project(*between)
                    if g == 3 and plain:
                        after(pe, s_y, t - 2)
                    r = slice(32 * g, 32 * g + 32)
                    for b in range(2):
                        mm = pe.matmul(SB[g][64 * b:64 * b + 64, 0:256], lhsT=qT[r, k % 2, 64 * b:64 * b + 64],
                                       rhs=km[r, k % 2, :, 64 * b:64 * b + 64], start=True, stop=not causal)
                    if causal:
                        mm = pe.matmul(SB[g][:, 0:256], lhsT=sb["row_of"][:], rhs=sb["alibi"][:, 256 * g:256 * g + 256],
                                       start=False, stop=True)
                    mm.then_inc(s_sc, 1)

            def turn_p(t, k):
                pe.wait_ge(s_exp, t + 1)
                after(pe, s_pl, 2 * t)
                for n in range(2):
                    for c in range(4):
                        mm = pe.transpose(TB[n][:, 128 * c:128 * c + 128],
                                          sx[:, k % 2, 512 * n + 128 * c:512 * n + 128 * c + 128], sb["ident"][:])
                    mm.then_inc(s_pt, 1)

            def mix(t, k):
                pe.wait_ge(s_pl, 2 * t + 2)
                pe.wait_ge(s_vb, t + 1)
                after(pe, s_y, t)
                if not plain:
                    after(pe, s_x, t - 2)

                def products(out, parts, values):
                    for n, (a, b) in enumerate(((0, 0), (0, 1), (1, 0))):
                        ins = pe.matmul(out, lhsT=parts[a], rhs=values[b], start=(n == 0), stop=(n == 2))
                    return ins

                for c in range(PAIRS):
                    mm = products(MO[:, :, 18 * c:18 * c + 18], [pt[:, h, k % 2, 128 * c:128 * c + 128] for h in range(2)],
                                  [vb[:, h, k % 4, :, c, :] for h in range(2)])
                if plain:
                    after(pe, s_free, 4 * (t + 2) + 4 if not isinstance(t, int) or t + 3 <= NT else 4 * NT)
                    for c in range(PAIRS):
                        mm = products(MB[:, :, c], [sb["biasP"][:, h, c, :] for h in range(2)],
                                      [vb[:, h, k % 4, :, c, :].rearrange("p b (i e) -> p b i e", e=VW)[:, :, :, 0:HD]
                                       for h in range(2)])
                mm.then_inc(s_mix, 1)

            def turn_y(t, k):
                pe.wait_ge(s_y, t + 1)
                after(pe, s_yc, t)
                after(pe, s_free, 4 * (t + 3) + 2 if not isinstance(t, int) or t + 4 <= NT else 4 * NT)
                pe.transpose(YT, y[:, k % 2, :], sb["ident"][:]).then_inc(s_yt, 1)

            def project_out(t, k):
                pe.wait_ge(s_yc, t + 1)
                after(pe, s_x, t)
                after(pe, s_y, t + 2 if not isinstance(t, int) or t + 2 <= NT else NT)
                pe.matmul(OB[:, 384:512], lhsT=yT[:, k % 2, :], rhs=sb["wo_" + layer][:], start=True, stop=False)
                pe.matmul(OB[:, 384:512], lhsT=sb["ones_row"][:], rhs=sb["bo_" + layer][:],
                          start=False, stop=True).then_inc(s_out, 1)

            def step(s, k):
                for lag, do in (((1, turn), (2, project), (3, score), (4, turn_p), (5, mix)) if plain else
                                ((3, score), (2, project), (4, turn_p), (1, turn), (6, turn_y), (5, mix), (7, project_out))):
                    t = tile_of(s, lag)
                    if t is None:
                        continue
                    if do is score:
                        score(t, k - lag, (tile_of(s, 2), k - 2))
                    elif not (do is project and not plain and tile_of(s, 3) is not None):
                        do(t, k - lag)

            run_steps(pe, step, LAST)

        @block.scalar
        def _(act):
            def copy_q(t, k):
                act.wait_ge(s_proj, t + 1)
                after(act, s_sc, 4 * (t - 1))
                if plain:
                    act.activation(qT[:, k % 2, :], PB[:, 0:128], ACT.Copy, scale=scale).then_inc(s_q, 1)
                else:
                    act.activation(qT[:, k % 2, :], PB[:, 0:128], ACT.Identity, bias=sb["bqs_" + layer][:, 0:1],
                                   scale=scale).then_inc(s_q, 1)

            def copy_k(t, k):
                for j in range(4):
                    ins = act.activation(km[:, k % 2, j, :], PB[:, 128:256], ACT.Identity,
                                         bias=bkm[:, j:j + 1], scale=sb["head_mask"][:, j:j + 1])
                ins.then_inc(s_k, 1)

            def normalise(t, k):
                after(act, s_turn, t - 1)
                act.activation(xn[:, k % 2, :], x[:, t, :], ACT.Identity, bias=sb["nmr"][:, bass.ds(t, 1)],
                               scale=sb["rstd"][:, bass.ds(t, 1)]).then_inc(s_norm, 1)

            def copy_yt(t, k):
                act.wait_ge(s_yt, t + 1)
                act.activation(yT[:, k % 2, :], YT, ACT.Copy).then_inc(s_yc, 1)

            def copy_pt(t, k):
                after(act, s_mix, t - 1)
                for n in range(2):
                    act.wait_ge(s_pt, 2 * t + n + 1)
                    act.activation(pt[:, 0, k % 2, 512 * n:512 * n + 512], TB[n][:, :], ACT.Copy).then_inc(s_pe, 1)

            def exps(t, k):
                act.wait_ge(s_sub, 4 * t + 4)
                act.activation(sx[:, k % 2, :], sx[:, k % 2, :], ACT.Exp).then_inc(s_exp, 1)

            def copy_ht(t, k):
                act.wait_ge(s_turn, t + 1)
                after(act, s_proj, t - 1)
                act.activation(hT[:, k % 2], XT, ACT.Copy).then_inc(s_ht, 1)

            def step(s, k):
                for lag, do in (((1, copy_ht), (2, copy_q), (2, copy_k), (4, copy_pt), (0, normalise), (3, exps)) if plain
                                else ((2, copy_q), (2, copy_k), (4, copy_pt), (1, copy_ht), (6, copy_yt), (0, normalise),
                                      (3, exps))):
                    t = tile_of(s, lag)
                    if t is not None:
                        do(t, k - lag)

            run_steps(act, step, LAST)

        @block.vector
        def _(dve):
            def copy_v(t, k):
                dve.wait_ge(s_k, t + 1)
                after(dve, s_vb, t - 1)
                dve.tensor_tensor(vp[:, k % 2], PB[:, 256:384], bv[:], ALU.add).then_inc(s_v, 1)

            def low_part(t, k):
                after(dve, s_mix, t - 1)
                for n in range(2):
                    dve.wait_ge(s_pe, 2 * t + n + 1)
                    dve.tensor_tensor(pt[:, 1, k % 2, 512 * n:512 * n + 512], TB[n][:, :],
                                      pt[:, 0, k % 2, 512 * n:512 * n + 512], ALU.subtract).then_inc(s_pl, 1)

            def shift(t, k):
                after(dve, s_pt, 2 * (t - 1))
                two = lambda a, n: a[:, 512 * n:512 * n + 512].rearrange("p (g c) -> p g c", g=2)
                heads = lambda a: a.rearrange("p g (h k) -> p g h k", k=SEQ)
                def maxima(n):
                    dve.wait_ge(s_sc, 4 * t + 2 * n + 2)
                    dve.tensor_reduce(out=nmx[:, k % 2, 8 * n:8 * n + 8].rearrange("p (g h) -> p g h", g=2),
                                      in_=heads(sb["banks"][:, 2 * n:2 * n + 2, 0:256]),
                                      axis=AX.X, op=ALU.max).then_inc(s_max, 1)

                def subtract(n):
                    dve.wait_ge(s_max, 2 * t + n + 1)
                    dve.tensor_tensor(
                        heads(two(sx[:, k % 2, :], n)), heads(sb["banks"][:, 2 * n:2 * n + 2, 0:256]),
                        nmx[:, k % 2, 8 * n:8 * n + 8].rearrange("p (g h) -> p g h", g=2).unsqueeze(3)
                        .to_broadcast([P, 2, 4, SEQ]), ALU.subtract).then_inc(s_sub, 2)

                for do, n in ((maxima, 0), (subtract, 0), (maxima, 1), (subtract, 1)) if not plain else (
                        (maxima, 0), (maxima, 1), (subtract, 0), (subtract, 1)):
                    do(n)

            def finish(t, k):
                dve.wait_ge(s_mix, t + 1)
                halves = [(slice(64 * b, 64 * b + 64), b) for b in range(2)]
                for r, b in halves:
                    o = MO[r, b, :].rearrange("p (h e) -> p h e", e=VW)
                    dve.reciprocal(rec[r, k % 2, :], o[:, :, HD]).then_inc(s_rec, 1)
                dve.wait_ge(s_rec, 2 * t + 2)
                if not plain:
                    after(dve, s_yt, t - 1)
                for r, b in halves:
                    o = MO[r, b, :].rearrange("p (h e) -> p h e", e=VW)
                    ins = dve.tensor_tensor(y[r, k % 2, :].rearrange("p (h d) -> p h d", d=HD), o[:, :, 0:HD],
                                            rec[r, k % 2, :].unsqueeze(2).to_broadcast([64, HEADS, HD]), ALU.mult)
                if not plain:
                    ins.then_inc(s_y, 1)
                    return
                ins.then_inc(s_yb, 1)
                dve.wait_ge(s_yb, t + 1)
                for r, b in halves:
                    ins = dve.tensor_tensor(ao[r, t, :], SB[3][r, 256 + 128 * b:384 + 128 * b], y[r, k % 2, :], ALU.add)
                ins.then_inc(s_y, 1)

            def update_x(t, k):
                dve.wait_ge(s_out, t + 1)
                dve.tensor_tensor(x[:, t, :], OB[:, 384:512], x[:, t, :], ALU.add).then_inc(s_x, 1)

            def stats(t, k, finished):
                if not finished:
                    dve.wait_ge(s_y if plain else s_x, t + 1)
                dve.bn_stats(sb["st6"][:, t, :], (ao if plain else x)[:, t, :])

            def step(s, k):
                t = tile_of(s, 3)
                if t is not None:
                    shift(t, k - 3)
                for lag, do in ((2, copy_v), (4, low_part)) if plain else ((4, low_part), (2, copy_v)):
                    t = tile_of(s, lag)
                    if t is not None:
                        do(t, k - lag)
                if not plain:
                    t = tile_of(s, 5)
                    if t is not None:
                        dve.wait_ge(s_mix, t + 1)
                    t = tile_of(s, 7)
                    if t is not None:
                        update_x(t, k - 7)
                t = tile_of(s, 5)
                if t is not None:
                    finish(t, k - 5)
                lag = 6 if plain else 7
                if tile_of(s, lag) is not None:
                    stats(tile_of(s, lag), k - lag, t is not None)

            run_steps(dve, step, LAST)

        @block.gpsimd
        def _(pool):
            def copy_ctx(t, k):
                after(pool, s_proj, t - 3)
                pool.tensor_copy(cT[0:CTX, k % 4], ctxT[0:CTX, bass.ds(t * P, P)]).then_inc(s_ctx, 1)

            def split_v(t, k):
                pool.wait_ge(s_v, t + 1)
                v = v32[:, k % 2].rearrange("p b c i d -> p (b c) i d")
                pool.tensor_tensor(v, vp[:, k % 2].rearrange("p (m d) -> p m d", d=HD).unsqueeze(2)
                                   .to_broadcast([P, 2 * PAIRS, 2, HD]),
                                   sb["own_half"][:].unsqueeze(1).unsqueeze(3).to_broadcast([P, 2 * PAIRS, 2, HD]),
                                   ALU.mult).then_inc(s_vm, 1)
                pool.wait_ge(s_vm, t + 1)
                after(pool, s_mix, t - 3)
                zeros = sb["zeros"][:, 0:HD].unsqueeze(1).unsqueeze(1).to_broadcast([P, 2 * PAIRS, 2, HD])
                high, low = (vb[:, h, k % 4].rearrange("p b c (i e) -> p (b c) i e", e=VW)[:, :, :, 0:HD]
                             for h in range(2))
                pool.tensor_tensor(high, v, zeros, ALU.add).then_inc(s_vh, 1)
                pool.wait_ge(s_vh, t + 1)
                pool.tensor_tensor(low, v, high, ALU.subtract).then_inc(s_vb, 1)

            def step(s, k):
                t = tile_of(s, 0)
                if t is not None and cross:
                    copy_ctx(t, k)
                t = tile_of(s, 2)
                if t is not None:
                    split_v(t, k - 2)

            run_steps(pool, step, 3)


def second_norm(nc, sb, sem):
    s_n, s_g, s_b, s_x = (sem(n) for n in ("o_normed", "o_scaled", "o_shifted", "o_added"))
    x, ao = sb["x"], sb["G3v"]
    tiles = lambda a, g: a[:, bass.ds(g * 4, 4), :]
    wide = lambda b: b[:].unsqueeze(1).to_broadcast([P, 4, DIM])
    with nc.Block() as block:
        @block.scalar
        def _(act):
            def normalise(g, k):
                for j in range(4):
                    t = g * 4 + j
                    ins = act.activation(ao[:, t, :], ao[:, t, :], ACT.Identity, bias=sb["nmr"][:, bass.ds(t, 1)],
                                         scale=sb["rstd"][:, bass.ds(t, 1)])
                ins.then_inc(s_n, 1)

            run_groups(act, normalise, 0)

        @block.vector
        def _(dve):
            def scale(g, k):
                dve.wait_ge(s_n, g + 1)
                dve.tensor_tensor(tiles(ao, g), tiles(ao, g), wide(sb["gammaB"]), ALU.mult).then_inc(s_g, 1)

            def add(g, k):
                dve.wait_ge(s_b, g + 1)
                dve.tensor_tensor(tiles(x, g), tiles(ao, g), tiles(x, g), ALU.add).then_inc(s_x, 1)
                settle(dve, sb, s_x, g + 1)
                stats_of_group(dve, sb, g)

            def step(s, k):
                for lag, do in ((0, scale), (2, add)):
                    g = group_of(s, lag)
                    if g is not None:
                        do(g, k - lag)

            run_groups(dve, step, 2)

        @block.gpsimd
        def _(pool):
            def shift(g, k):
                pool.wait_ge(s_g, g + 1)
                pool.tensor_tensor(tiles(ao, g), tiles(ao, g), wide(sb["betaB"]), ALU.add).then_inc(s_b, 1)

            run_groups(pool, shift, 0)


def run_groups(eng, body, last_lag, unroll=2, peel=4):
    for s in range(peel):
        body(s, s)
    with eng.Fori(peel // unroll, NG // unroll) as q:
        for u in range(unroll):
            body(q * unroll + u, u)
    for s in range(NG, NG + last_lag):
        body(s, s)


def group_of(step, lag):
    g = step - lag
    if isinstance(g, int) and not 0 <= g < NG:
        return None
    return g


def normalise_group(dve, sb, g, k, done):
    for j in range(4):
        t = g * 4 + j
        ins = dve.tensor_scalar(sb["xn4"][:, k % 2, j, :], sb["x"][:, t, :], sb["mean"][:, bass.ds(t, 1)],
                                sb["rstd"][:, bass.ds(t, 1)], ALU.subtract, ALU.mult)
    ins.then_inc(done, 1)


def stats_of_group(dve, sb, g):
    for j in range(4):
        dve.bn_stats(sb["st6"][:, g * 4 + j, :], sb["x"][:, g * 4 + j, :])


def shrink_ffn(nc, sb, ps, sem):
    s_fold, s_row = sem("w2_folded"), sem("row_ready")
    s_norm, s_turn, s_ht, s_sh, s_sT = sem("f_normed"), sem("f_turned"), sem("f_ht_ready"), sem("f_shrunk"), sem("f_sT_ready")
    s_ex, s_hid, s_dn, s_x = (sem(n) for n in ("f_expanded", "f_hid_ready", "f_down", "f_x"))
    s_split, s_wide, s_base = sem("f_split"), sem("f_row_wide"), sem("f_row_added")
    top, rest, mid, low = sb["f_top"], sb["f_rest"], sb["f_mid"], sb["f_low"]
    M = M_SHRINK
    NC = M_SHRINK * INNER // P
    x4 = sb["x"][:].rearrange("p (g j) f -> p g (j f)", j=4)
    hid = sb["G3"][:].rearrange("p (r c n) -> p r c n", r=2, c=NC)
    EB, DB, TB, SB = ps[0:4], ps[4:6], ps[6], ps[7]

    with nc.Block() as block:
        @block.vector
        def _(dve):
            for c in range(NC):
                ins = dve.tensor_scalar(sb["w_out"][:, c, :], sb["w_out"][:, c, :], sb["w_2"][:, c:c + 1], None, ALU.mult)
            dve.tensor_copy(sb["f_sel"], sb["sel_e"][:])
            dve.wait_ge(s_fold, 1)
            dve.tensor_tensor(sb["row"][:], ps[0][0:1, 0:DIM], sb["b_out"][:], ALU.add).then_inc(s_row, 1)
            dve.wait_ge(s_wide, 1)
            dve.tensor_copy(sb["f_rowB"], ps[1][:, 0:DIM])

        @block.tensor
        def _(pe):
            pe.matmul(ps[0][0:1, 0:DIM], lhsT=sb["b_2"][:], rhs=sb["w_outp"][:], start=True, stop=True).then_inc(s_fold, 1)
            pe.wait_ge(s_row, 1)
            pe.matmul(ps[1][:, 0:DIM], lhsT=sb["ones_row"][:], rhs=sb["row"][:], start=True, stop=True).then_inc(s_wide, 1)

    with nc.Block() as block:
        @block.tensor
        def _(pe):
            def turn(g, k):
                pe.wait_ge(s_norm, g + 1)
                after(pe, s_ht, g)
                for j in range(4):
                    mm = pe.transpose(TB[:, P * j:P * j + P], sb["xn4"][:, k % 2, j, :], sb["ident"][:])
                mm.then_inc(s_turn, 1)

            def shrink(g, k):
                pe.wait_ge(s_ht, g + 1)
                after(pe, s_sT, g)
                pe.matmul(SB[:, :], lhsT=sb["w_in"][:], rhs=sb["hT4"][:, k % 2, :],
                          start=True, stop=True).then_inc(s_sh, 1)

            def expand(g, k, c):
                if c == 0:
                    pe.wait_ge(s_split, 4 * g + 4)
                after(pe, s_hid, NC * g + c - 3)
                pe.matmul(EB[c % 4][:, :], lhsT=sb["f_sel"][:, c, :], rhs=top[:, k % 2, :], start=True, stop=False)
                pe.matmul(EB[c % 4][:, :], lhsT=sb["f_sel"][0:M, c, :], rhs=low[:, k % 2, :],
                          start=False, stop=True).then_inc(s_ex, 1)

            def down(g, k, j, half):
                if j == 0 and half == 0:
                    pe.wait_ge(s_hid, NC * (g + 1))
                    after(pe, s_x, g - 1)
                o = DB[k % 2][:, DIM * j:DIM * j + DIM]
                for c in range(NC // 2 * half, NC // 2 * (half + 1)):
                    mm = pe.matmul(o, lhsT=hid[:, k % 2, c, P * j:P * j + P], rhs=sb["w_out"][:, c, :],
                              start=(c == 0), stop=(c == NC - 1))
                if half and j == 3:
                    mm.then_inc(s_dn, 1)

            def step(s, k):
                for lag, do in ((1, turn), (2, shrink)):
                    g = group_of(s, lag)
                    if g is not None:
                        do(g, k - lag)
                g3, g4 = group_of(s, 3), group_of(s, 4)
                for c in range(NC):
                    if g3 is not None:
                        expand(g3, k - 3, c)
                    if g4 is not None:
                        down(g4, k - 4, c // 2, c % 2)

            run_groups(pe, step, 4, peel=6)

        @block.scalar
        def _(act):
            def copy_ht(g, k):
                act.wait_ge(s_turn, g + 1)
                after(act, s_sh, g - 1)
                act.activation(sb["hT4"][:, k % 2, :], TB[:, :], ACT.Copy).then_inc(s_ht, 1)

            def copy_sT(g, k):
                act.wait_ge(s_sh, g + 1)
                after(act, s_split, 4 * (g - 2) + 2)
                act.activation(sb["sT"][:, k % 2, :], SB[:, :], ACT.Identity,
                               bias=sb["b_in"][:, 0:1]).then_inc(s_sT, 1)

            def relus(g, k):
                after(act, s_dn, g - 1)
                for c in range(NC):
                    act.wait_ge(s_ex, NC * g + c + 1)
                    act.activation(hid[:, k % 2, c, :], EB[c % 4][:, :], ACT.Relu, bias=sb["b_1"][:, c:c + 1],
                                   scale=sb["w_1"][:, c:c + 1]).then_inc(s_hid, 1)

            def step(s, k):
                for lag, do in ((1, copy_ht), (2, copy_sT), (3, relus)):
                    g = group_of(s, lag)
                    if g is not None:
                        do(g, k - lag)

            run_groups(act, step, 4, peel=6)

        @block.vector
        def _(dve):
            def normalise(g, k):
                after(dve, s_turn, g - 1)
                normalise_group(dve, sb, g, k, s_norm)

            def update(g, k):
                v = sb["x"][:, bass.ds(g * 4, 4), :]
                dve.tensor_tensor(v, sb["f_rowB"].unsqueeze(1).to_broadcast([P, 4, DIM]), v, ALU.add).then_inc(s_base, 1)
                dve.wait_ge(s_base, g + 1)
                dve.wait_ge(s_dn, g + 1)
                dve.tensor_tensor(x4[:, g, :], DB[k % 2][:, :], x4[:, g, :], ALU.add).then_inc(s_x, 1)
                settle(dve, sb, s_x, g + 1)
                stats_of_group(dve, sb, g)

            def split(g, k):
                src = sb["sT"][:, k % 2, :]
                dve.wait_ge(s_sT, g + 1)
                after(dve, s_ex, NC * (g - 1))
                after(dve, s_split, 4 * g)
                dve.tensor_copy(top[:, k % 2, :], src).then_inc(s_split, 1)
                dve.wait_ge(s_split, 4 * g + 1)
                dve.tensor_tensor(rest, src, top[:, k % 2, :], ALU.subtract).then_inc(s_split, 1)
                dve.wait_ge(s_split, 4 * g + 2)
                dve.tensor_copy(top[M:2 * M, k % 2, :], rest[M:2 * M])
                dve.tensor_copy(mid, rest[0:M]).then_inc(s_split, 1)
                dve.wait_ge(s_split, 4 * g + 3)
                dve.tensor_tensor(low[:, k % 2, :], rest[0:M], mid, ALU.subtract).then_inc(s_split, 1)

            def step(s, k):
                for lag, do in ((0, normalise), (2, split), (4, update)):
                    g = group_of(s, lag)
                    if g is not None:
                        do(g, k - lag)

            run_groups(dve, step, 4, peel=6)


WS = {n: i for i, n in enumerate(("d2v", "img", "txt", "att0", "att1", "f1", "f2"))}
WCOUNT = {"d2v": CTX * P, "img": P * P, "txt": P * P, "att0": P * P, "att1": P * P,
          "f1": 2 * P * FFN, "f2": P * FFN}


def weights_to_ternary(nc, sb, sem):
    s_zero, s_sum, s_all, s_scale, s_thr, s_lt = (sem(n) for n in ("q_zeroed", "q_summed", "q_all", "q_scaled", "q_thr", "q_lt"))
    names = list(WS)
    with nc.Block() as block:
        @block.vector
        def _(dve):
            dve.memset(sb["wsum"][:], 0.0).then_inc(s_zero, 1)
            dve.memset(sb["roundc"][:], ROUND)
            dve.memset(sb["stat"][:], 0.0)
            dve.wait_ge(s_zero, 1)
            for n in names:
                k = CTX if n == "d2v" else P
                ins = dve.tensor_reduce(out=sb["wsum"][0:k, WS[n]:WS[n] + 1], in_=sb["b_" + n][0:k, :], axis=AX.X,
                                        op=ALU.add, apply_absolute_value=True)
            ins.then_inc(s_sum, 1)
            dve.wait_ge(s_all, 1)
            for n in names:
                w = slice(WS[n], WS[n] + 1)
                ins = dve.tensor_scalar(sb["wscale"][:, w], sb["wall"][:, w], 1.0 / WCOUNT[n], 1e-5, ALU.mult, ALU.max)
            ins.then_inc(s_scale, 1)
            dve.wait_ge(s_scale, 1)
            dve.tensor_scalar(sb["wthr"][:], sb["wscale"][:], 0.5, None, ALU.mult)
            dve.tensor_scalar(sb["wnthr"][:], sb["wscale"][:], -0.5, None, ALU.mult).then_inc(s_thr, 1)
            dve.wait_ge(s_thr, 1)
            for i, n in enumerate(names):
                k = CTX if n == "d2v" else P
                w, width = slice(WS[n], WS[n] + 1), sb["b_" + n].shape[1]
                dve.tensor_scalar(sb["wtmp"][0:k, 0:width], sb["b_" + n][0:k, :], sb["wnthr"][0:k, w], None,
                                  ALU.is_lt).then_inc(s_lt, 1)
                dve.wait_ge(s_lt, 2 * i + 1)
                dve.scalar_tensor_tensor(out=sb["t_" + n][0:k, 0:width], in0=sb["b_" + n][0:k, :],
                                         scalar=sb["wthr"][0:k, w], in1=sb["wtmp"][0:k, 0:width],
                                         op0=ALU.is_gt, op1=ALU.subtract).then_inc(s_lt, 1)
                dve.wait_ge(s_lt, 2 * i + 2)

        @block.gpsimd
        def _(pool):
            pool.wait_ge(s_sum, 1)
            pool.partition_all_reduce(sb["wall"][:], sb["wsum"][:], P, bass.bass_isa.ReduceOp.add).then_inc(s_all, 1)


def input_scale(nc, sb, sem, tag, weight, parts=P, extra=None):
    s_max, s_all, s_a, s_b = (sem(n + tag) for n in ("max_", "allmax_", "iscale_", "inv_"))
    with nc.Block() as block:
        @block.vector
        def _(dve):
            dve.tensor_reduce(out=sb["amax"][:], in_=sb["stat"][:], axis=AX.X, op=ALU.max).then_inc(s_max, 1)
            dve.wait_ge(s_all, 1)
            dve.tensor_scalar(sb["isc"][:], sb["amaxall"][:], 1e-8, 1.0 / 127.0, ALU.max, ALU.mult).then_inc(s_a, 1)
            dve.wait_ge(s_a, 1)
            dve.reciprocal(sb["inv"][:], sb["isc"][:])
            dve.tensor_scalar(sb["osc"][:], sb["wscale"][:], sb["isc"][:, 0:1], None, ALU.mult).then_inc(s_b, 1)
            dve.wait_ge(s_b, 1)
            dve.memset(sb["stat"][:], 0.0)

        @block.gpsimd
        def _(pool):
            pool.wait_ge(s_max, 1)
            pool.partition_all_reduce(sb["amaxall"][:], sb["amax"][:], P, bass.bass_isa.ReduceOp.max).then_inc(s_all, 1)


def quantise(nc, sb, sem, tag, src, dst, parts=P):
    s_r, s_q = sem("rounded_" + tag), sem("quantised_" + tag)
    W, N = 1024, TOK // 1024
    with nc.Block() as block:
        @block.scalar
        def _(act):
            def add_round(c, k):
                after(act, s_q, c - 1)
                act.activation(sb["rnd"][0:parts, k % 2, :], src[0:parts, bass.ds(c * W, W)], ACT.Identity,
                               bias=sb["roundc"][0:parts, 0:1], scale=sb["inv"][0:parts, 0:1]).then_inc(s_r, 1)

            add_round(0, 0)
            add_round(1, 1)
            with act.Fori(1, N // 2) as q:
                for u in range(2):
                    add_round(q * 2 + u, u)

        @block.vector
        def _(dve):
            with dve.Fori(0, N // 2) as q:
                for u in range(2):
                    c = q * 2 + u
                    dve.wait_ge(s_r, c + 1)
                    dve.tensor_scalar(dst[0:parts, bass.ds(c * W, W)], sb["rnd"][0:parts, u, :], ROUND, 127.0,
                                      ALU.subtract, ALU.min).then_inc(s_q, 1)


def bit_linear(nc, sb, ps, sem, tag, weight, bias, src, dst, parts=P):
    s_m, s_d = sem("mm_" + tag), sem("dst_" + tag)
    w = slice(WS[weight], WS[weight] + 1)
    with nc.Block() as block:
        @block.tensor
        def _(pe):
            def multiply(g, k):
                after(pe, s_d, g - 3)
                pe.matmul(ps[k % 4][:, :], lhsT=sb["t_" + weight][0:parts, 0:P],
                          rhs=src[0:parts, bass.ds(g * 512, 512)], start=True, stop=True).then_inc(s_m, 1)

            run_groups(pe, multiply, 0, 4)

        @block.scalar
        def _(act):
            def scale_out(g, k):
                act.wait_ge(s_m, g + 1)
                act.activation(dst[:, bass.ds(g * 512, 512)], ps[k % 4][:, :], ACT.Identity, bias=sb[bias][:, 0:1],
                               scale=sb["osc"][:, w]).then_inc(s_d, 1)

            run_groups(act, scale_out, 0, 4)

        @block.vector
        def _(dve):
            def absmax(g, k):
                dve.wait_ge(s_d, g + 1)
                dve.tensor_reduce(out=sb["stat"][:, bass.ds(g, 1)], in_=dst[:, bass.ds(g * 512, 512)], axis=AX.X,
                                  op=ALU.max, apply_absolute_value=True)

            run_groups(dve, absmax, 0)


def bit_attention(nc, sb, ps, sem, r, qimg):
    S = lambda n: sem(n + f"_r{r}")
    s_kt, s_ktc, s_kk, s_kkc, s_f = S("kT"), S("kT_ready"), S("k"), S("k_ready"), S("fused_copied")
    s_s, s_m, s_sh, s_e, s_su, s_rc, s_p = (S(n) for n in ("s", "s_max", "s_shift", "s_exp", "s_sum", "s_rec", "p"))
    s_pt, s_ptc, s_o, s_u = S("pT"), S("pT_ready"), S("o"), S("upd")
    name = f"att{r}"
    w = slice(WS[name], WS[name] + 1)
    fused = sb["G3"]
    kT, kk, fz, st, pT, mx, sm = (sb[n] for n in ("b_kT", "b_k", "b_f", "b_s", "b_pT", "b_mx", "b_sm"))
    bd = sb["b_bd"]
    KT, KK, SS, PT, OO = ps[0:5]
    c = DIM ** -0.5

    def tiles(ap):
        return ap.rearrange("p (j n) -> p j n", j=4)

    with nc.Block() as block:
        @block.vector
        def _(dve):
            dve.memset(bd[:], 0.0)

    with nc.Block() as block:
        @block.tensor
        def _(pe):
            def keys(g, k):
                after(pe, s_ktc, g)
                pe.matmul(KT[:, :], lhsT=sb["t_" + name][:], rhs=qimg[:, bass.ds(g * 512, 512)],
                          start=True, stop=True).then_inc(s_kt, 1)
                after(pe, s_kkc, g)
                for j in range(4):
                    mm = pe.matmul(KK[:, P * j:P * j + P], lhsT=qimg[:, bass.ds(g * 512 + P * j, P)],
                                   rhs=sb["t_" + name][:], start=True, stop=True)
                mm.then_inc(s_kk, 1)

            def scores(g, k):
                pe.wait_ge(s_ktc, g + 1)
                pe.wait_ge(s_f, g + 1)
                after(pe, s_sh, g)
                for j in range(4):
                    for b in range(2):
                        n = slice(P * j + SEQ * b, P * j + SEQ * b + SEQ)
                        mm = pe.matmul(SS[SEQ * b:SEQ * b + SEQ, SEQ * j:SEQ * j + SEQ], lhsT=fz[:, k % 2, n],
                                       rhs=kT[:, k % 2, n], start=True, stop=True)
                mm.then_inc(s_s, 1)

            def turn(g, k):
                pe.wait_ge(s_p, g + 1)
                after(pe, s_ptc, g)
                for j in range(4):
                    n = slice(P * j, P * j + P)
                    mm = pe.transpose(PT[:, n], bd[:, k % 2, n], sb["ident"][:])
                mm.then_inc(s_pt, 1)

            def mix(g, k):
                pe.wait_ge(s_ptc, g + 1)
                pe.wait_ge(s_kkc, g + 1)
                after(pe, s_u, g)
                for j in range(4):
                    n = slice(P * j, P * j + P)
                    mm = pe.matmul(OO[:, n], lhsT=kk[:, k % 4, n], rhs=pT[:, k % 2, n], start=True, stop=True)
                mm.then_inc(s_o, 1)

            def step(s, k):
                for lag, do in ((1, scores), (2, turn), (0, keys), (3, mix)):
                    g = group_of(s, lag)
                    if g is not None:
                        do(g, k - lag)

            run_groups(pe, step, 3, 4)

        @block.scalar
        def _(act):
            def copy_kT(g, k):
                act.wait_ge(s_kt, g + 1)
                after(act, s_s, g - 1)
                act.activation(kT[:, k % 2, :], KT[:, :], ACT.Identity, bias=sb[f"bb_{name}"][:, 0:1],
                               scale=sb["osc"][:, w]).then_inc(s_ktc, 1)

            def exps(g, k):
                act.wait_ge(s_sh, g + 1)
                act.activation(st[:, k % 2, :], st[:, k % 2, :], ACT.Exp, scale=c).then_inc(s_e, 1)

            def copy_pT(g, k):
                act.wait_ge(s_pt, g + 1)
                after(act, s_o, g - 1)
                act.activation(pT[:, k % 2, :], PT[:, :], ACT.Copy).then_inc(s_ptc, 1)

            def step(s, k):
                for lag, do in ((2, copy_pT), (1, exps), (0, copy_kT)):
                    g = group_of(s, lag)
                    if g is not None:
                        do(g, k - lag)

            run_groups(act, step, 3, 4)

        @block.vector
        def _(dve):
            def copy_k(g, k):
                dve.wait_ge(s_kk, g + 1)
                after(dve, s_o, g - 3)
                dve.scalar_tensor_tensor(out=tiles(kk[:, k % 4, :]), in0=tiles(KK[:, :]), scalar=sb["osc"][:, w],
                                         in1=sb[f"bB_{name}"][:].unsqueeze(1).to_broadcast([P, 4, P]),
                                         op0=ALU.mult, op1=ALU.add).then_inc(s_kkc, 1)

            def shift(g, k):
                dve.wait_ge(s_s, g + 1)
                after(dve, s_p, g - 1)
                scores = tiles(SS[:, 0:4 * SEQ])
                dve.tensor_reduce(out=mx[:, k % 2, :], in_=scores, axis=AX.X, op=ALU.max).then_inc(s_m, 1)
                dve.wait_ge(s_m, g + 1)
                dve.tensor_tensor(tiles(st[:, k % 2, :]), scores, mx[:, k % 2, :].unsqueeze(2).to_broadcast([P, 4, SEQ]),
                                  ALU.subtract).then_inc(s_sh, 1)

            def divide(g, k):
                dve.wait_ge(s_e, g + 1)
                v = tiles(st[:, k % 2, :])
                dve.tensor_reduce(out=sm[:, k % 2, :], in_=v, axis=AX.X, op=ALU.add).then_inc(s_su, 1)
                dve.wait_ge(s_su, g + 1)
                dve.reciprocal(sm[:, k % 2, :], sm[:, k % 2, :]).then_inc(s_rc, 1)
                dve.wait_ge(s_rc, g + 1)
                after(dve, s_pt, g - 1)
                for b in range(2):
                    h = slice(SEQ * b, SEQ * b + SEQ)
                    ins = dve.tensor_tensor(tiles(bd[h, k % 2, :])[:, :, h], v[h], sm[h, k % 2, :].unsqueeze(2)
                                            .to_broadcast([SEQ, 4, SEQ]), ALU.mult)
                ins.then_inc(s_p, 1)

            def update(g, k):
                dve.wait_ge(s_o, g + 1)
                v = fused[:, bass.ds(g * 512, 512)]
                dve.scalar_tensor_tensor(out=v, in0=OO[:, :], scalar=0.1, in1=v, op0=ALU.mult,
                                         op1=ALU.add).then_inc(s_u, 1)

            def step(s, k):
                for lag, do in ((1, shift), (0, copy_k), (3, update), (1, divide)):
                    g = group_of(s, lag)
                    if g is not None:
                        do(g, k - lag)

            run_groups(dve, step, 3, 4)
            dve.wait_ge(s_u, NG)
            dve.tensor_reduce(out=sb["stat"][:, 0:1], in_=fused[:], axis=AX.X, op=ALU.max, apply_absolute_value=True)

        @block.gpsimd
        def _(pool):
            def copy_fused(g, k):
                after(pool, s_s, g - 1)
                after(pool, s_f, g)
                pool.tensor_tensor(sb["scratch"][:], sb["zeros"][:, 0:1], sb["zeros"][:, 0:1], ALU.add)
                pool.tensor_copy(fz[:, k % 2, :], fused[:, bass.ds(g * 512, 512)]).then_inc(s_f, 1)

            run_groups(pool, copy_fused, 0)


def bitnet(nc, sb, ps, sem, next_phase):
    ctxT = sb["G1"]
    half = sb["G2"][:].bitcast(BF16)
    qa, qb = half[:, 0:TOK], half[:, TOK:2 * TOK]

    weights_to_ternary(nc, sb, sem)
    with nc.Block() as block:
        @block.vector
        def _(dve):
            dve.tensor_reduce(out=sb["stat"][0:CTX, 0:1], in_=ctxT[0:CTX, :], axis=AX.X, op=ALU.max,
                              apply_absolute_value=True)
    input_scale(nc, sb, sem, "ctx", "d2v")
    quantise(nc, sb, sem, "ctx", ctxT, qa, CTX)
    bit_linear(nc, sb, ps, sem, "vis", "d2v", "bb_d2v", qa, sb["G3"], CTX)
    input_scale(nc, sb, sem, "vis", "img")
    quantise(nc, sb, sem, "vis", sb["G3"], qb)
    bit_linear(nc, sb, ps, sem, "img", "img", "bb_img", qb, sb["G1"])
    input_scale(nc, sb, sem, "img", "att0")

    s_av = sem("averaged")
    with nc.Block() as block:
        @block.vector
        def _(dve):
            dve.tensor_copy(sb["osc_img"][:], sb["osc"][:])
            dve.tensor_reduce(out=sb["avg"][:], in_=sb["G1"][:].rearrange("p (b s) -> p b s", s=SEQ), axis=AX.X,
                              op=ALU.add).then_inc(s_av, 1)
            dve.wait_ge(s_av, 1)
            dve.tensor_scalar(sb["avg"][:], sb["avg"][:], 1.0 / SEQ, None, ALU.mult)
    quantise(nc, sb, sem, "img", sb["G1"], qa)
    turn_x(nc, sb, ps, sem, "text")
    input_scale(nc, sb, sem, "text", "txt")
    quantise(nc, sb, sem, "text", sb["G3"], qb)
    bit_linear(nc, sb, ps, sem, "txt", "txt", "bb_txt", qb, sb["G3"])
    with nc.Block() as block:
        @block.vector
        def _(dve):
            dve.tensor_copy(sb["osc"][:], sb["osc_img"][:])
            dve.memset(sb["stat"][:], 0.0)
    for r in range(2):
        next_phase()
        bit_attention(nc, sb, ps, sem, r, qa)
    with nc.Block() as block:
        @block.vector
        def _(dve):
            dve.tensor_reduce(out=sb["stat"][:, 1:2], in_=sb["avg"][:], axis=AX.X, op=ALU.max, apply_absolute_value=True)
    input_scale(nc, sb, sem, "cat", "f1")
    quantise(nc, sb, sem, "cat", sb["G3"], qa)
    s_ra = sem("avg_rounded")
    with nc.Block() as block:
        @block.vector
        def _(dve):
            dve.tensor_scalar(sb["avg"][:], sb["avg"][:], sb["inv"][:, 0:1], ROUND, ALU.mult, ALU.add).then_inc(s_ra, 1)
            dve.wait_ge(s_ra, 1)
            dve.tensor_scalar(sb["qavg"][:], sb["avg"][:], ROUND, 127.0, ALU.subtract, ALU.min)
    next_phase()
    bit_ffn(nc, sb, ps, sem, qa)


def turn_x(nc, sb, ps, sem, tag):
    s_norm, s_turn, s_ht = sem("t_normed" + tag), sem("t_turned" + tag), sem("t_ready" + tag)
    TB = ps[0:2]
    with nc.Block() as block:
        @block.vector
        def _(dve):
            def step(s, k):
                g = group_of(s, 0)
                if g is not None:
                    after(dve, s_turn, g - 1)
                    normalise_group(dve, sb, g, k, s_norm)
                g = group_of(s, 2)
                if g is not None:
                    dve.wait_ge(s_ht, g + 1)
                    dve.tensor_reduce(out=sb["stat"][:, bass.ds(g, 1)], in_=sb["G3"][:, bass.ds(g * 512, 512)],
                                      axis=AX.X, op=ALU.max, apply_absolute_value=True)

            run_groups(dve, step, 2)

        @block.tensor
        def _(pe):
            def turn(g, k):
                pe.wait_ge(s_norm, g + 1)
                after(pe, s_ht, g - 1)
                for j in range(4):
                    mm = pe.transpose(TB[k % 2][:, P * j:P * j + P], sb["xn4"][:, k % 2, j, :], sb["ident"][:])
                mm.then_inc(s_turn, 1)

            run_groups(pe, turn, 0)

        @block.scalar
        def _(act):
            def copy_ht(g, k):
                act.wait_ge(s_turn, g + 1)
                act.activation(sb["G3"][:, bass.ds(g * 512, 512)], TB[k % 2][:, :], ACT.Copy).then_inc(s_ht, 1)

            run_groups(act, copy_ht, 0)


def bit_ffn(nc, sb, ps, sem, qx):
    NC = FFN // P
    s_m, s_r = sem("f1_product"), sem("f1_max")
    s_a, s_b = sem("f1_maxed"), sem("f1_scaled")
    w1 = slice(WS["f1"], WS["f1"] + 1)
    w2 = slice(WS["f2"], WS["f2"] + 1)

    def product(pe, bank, g, c):
        pe.matmul(bank[:, :], lhsT=sb["t_f1"][:, P * c:P * c + P], rhs=qx[:, bass.ds(g * 512, 512)],
                  start=True, stop=False)
        return pe.matmul(bank[:, :].rearrange("p (b s) -> p b s", s=SEQ), lhsT=sb["t_f1"][:, FFN + P * c:FFN + P * c + P],
                         rhs=sb["qavg"][:, bass.ds(g * 8, 8)].unsqueeze(2).to_broadcast([P, 8, SEQ]),
                         start=False, stop=True)

    with nc.Block() as block:
        @block.tensor
        def _(pe):
            def products(g, k):
                for c in range(NC):
                    after(pe, s_r, g * NC + c - 3)
                    product(pe, ps[c], g, c).then_inc(s_m, 1)

            run_groups(pe, products, 0)

        @block.vector
        def _(dve):
            def maxima(g, k):
                for c in range(NC):
                    dve.wait_ge(s_m, g * NC + c + 1)
                    dve.tensor_reduce(out=sb["pmax"][:, c, bass.ds(g, 1)], in_=ps[c][:, :], axis=AX.X,
                                      op=ALU.max).then_inc(s_r, 1)

            run_groups(dve, maxima, 0)
            dve.wait_ge(s_r, NG * NC)
            dve.tensor_reduce(out=sb["hmax"][:], in_=sb["pmax"][:], axis=AX.X, op=ALU.max).then_inc(s_a, 1)
            dve.wait_ge(s_a, 1)
            dve.tensor_scalar(sb["hmax"][:], sb["hmax"][:], sb["osc"][:, w1], None, ALU.mult).then_inc(s_b, 1)
            dve.wait_ge(s_b, 1)
            dve.tensor_tensor(sb["hmax"][:], sb["hmax"][:], sb["bb_f1"][:], ALU.add).then_inc(s_b, 1)
            dve.wait_ge(s_b, 2)
            dve.tensor_copy(sb["stat"][:, 0:NC], sb["hmax"][:])
            dve.tensor_copy(sb["osc_img"][:], sb["osc"][:])
    input_scale(nc, sb, sem, "hid", "f2")

    s_m, s_h, s_n, s_na, s_q, s_o, s_y, s_x = (sem(n) for n in (
        "f2_product", "f2_relu", "f2_rounded", "f2_rounded_act", "f2_q", "f2_out", "f2_y", "f2_x"))
    hf, hq = sb["h_f"], sb["h_q"]
    x4 = sb["x"][:].rearrange("p (g j) f -> p g (j f)", j=4)
    OB = ps[4:6]
    with nc.Block() as block:
        @block.tensor
        def _(pe):
            def hidden(g, k):
                for c in range(NC):
                    after(pe, s_h, NC * g + c - 3)
                    product(pe, ps[c], g, c).then_inc(s_m, 1)

            def down(g, k):
                pe.wait_ge(s_q, NC * (g + 1))
                after(pe, s_y, g - 1)
                for j in range(4):
                    for c in range(NC):
                        mm = pe.matmul(OB[k % 2][:, P * j:P * j + P], lhsT=hq[:, k % 2, c, P * j:P * j + P],
                                       rhs=sb["t_f2"][:, P * c:P * c + P], start=(c == 0), stop=(c == NC - 1))
                mm.then_inc(s_o, 1)

            def step(s, k):
                for lag, do in ((0, hidden), (1, down)):
                    g = group_of(s, lag)
                    if g is not None:
                        do(g, k - lag)

            run_groups(pe, step, 1)

        @block.scalar
        def _(act):
            def relus(g, k):
                for c in range(NC):
                    act.wait_ge(s_m, g * NC + c + 1)
                    if c % 2:
                        after(act, s_n, 2 * (g - 1) + c // 2 + 1)
                    else:
                        after(act, s_na, 2 * (g - 1) + c // 2 + 1)
                    act.activation(hf[:, c, :], ps[c][:, :], ACT.Relu, bias=sb["bb_f1"][:, c:c + 1],
                                   scale=sb["osc_img"][:, w1]).then_inc(s_h, 1)
                    if c % 2:
                        act.wait_ge(s_h, NC * g + c)
                        after(act, s_q, NC * g + c - 2)
                        act.activation(sb["h_r"][:, 0, :], hf[:, c - 1, :], ACT.Identity, bias=sb["roundc"][:, 0:1],
                                       scale=sb["inv"][:, 0:1]).then_inc(s_na, 1)

            run_groups(act, relus, 0)

        @block.vector
        def _(dve):
            def quantise_hidden(g, k):
                after(dve, s_o, g - 1)
                for c in range(NC):
                    if c % 2:
                        dve.wait_ge(s_h, NC * g + c + 1)
                        dve.wait_ge(s_q, NC * g + c)
                        dve.tensor_scalar(sb["h_r"][:, 1, :], hf[:, c, :], sb["inv"][:, 0:1], ROUND,
                                          ALU.mult, ALU.add).then_inc(s_n, 1)
                        dve.wait_ge(s_n, 2 * g + c // 2 + 1)
                    else:
                        dve.wait_ge(s_na, 2 * g + c // 2 + 1)
                    dve.tensor_scalar(hq[:, k % 2, c, :], sb["h_r"][:, c % 2, :], ROUND, 127.0,
                                      ALU.subtract, ALU.min).then_inc(s_q, 1)

            def update(g, k):
                dve.wait_ge(s_o, g + 1)
                dve.scalar_tensor_tensor(out=sb["h_y"][:].rearrange("p (j n) -> p j n", j=4),
                                         in0=OB[k % 2][:, :].rearrange("p (j n) -> p j n", j=4),
                                         scalar=sb["osc"][:, w2],
                                         in1=sb["bB_f2"][:].unsqueeze(1).to_broadcast([P, 4, P]),
                                         op0=ALU.mult, op1=ALU.add).then_inc(s_y, 1)
                dve.wait_ge(s_y, g + 1)
                dve.tensor_tensor(x4[:, g, :], sb["h_y"][:], x4[:, g, :], ALU.add).then_inc(s_x, 1)
                settle(dve, sb, s_x, g + 1)
                stats_of_group(dve, sb, g)

            def step(s, k):
                for lag, do in ((0, quantise_hidden), (2, update)):
                    g = group_of(s, lag)
                    if g is not None:
                        do(g, k - lag)

            run_groups(dve, step, 2)


def experts(nc, sb, ps, sem, out):
    hT = sb["G3"]
    x4 = sb["x"][:].rearrange("p (g j) f -> p g (j f)", j=4)
    route_inputs(nc, sb, ps, sem, hT)
    route(nc, sb, sem)
    expert_layers(nc, sb, ps, sem, hT, x4, out)


def route_inputs(nc, sb, ps, sem, hT):
    s_norm, s_turn, s_ht, s_lg, s_max, s_sh = (sem("r_" + n) for n in ("normed", "turned", "ht", "logits", "max", "shifted"))
    TB, LB = ps[0:2], ps[2:4]
    p, m1 = sb["r_p"], sb["r_m1"]
    with nc.Block() as block:
        @block.tensor
        def _(pe):
            def turn(g, k):
                pe.wait_ge(s_norm, g + 1)
                after(pe, s_ht, 2 * (g - 1))
                for j in range(4):
                    mm = pe.transpose(TB[k % 2][:, P * j:P * j + P], sb["xn4"][:, k % 2, j, :], sb["ident"][:])
                mm.then_inc(s_turn, 1)

            def logits(g, k):
                pe.wait_ge(s_ht, 2 * g + 2)
                after(pe, s_sh, g - 1)
                for j in range(4):
                    mm = pe.matmul(LB[k % 2][:, EXPERTS * j:EXPERTS * j + EXPERTS], lhsT=sb["hT4"][:, k % 2, P * j:P * j + P],
                                   rhs=sb["w_router"][:], start=True, stop=True)
                mm.then_inc(s_lg, 1)

            def step(s, k):
                for lag, do in ((1, turn), (2, logits)):
                    g = group_of(s, lag)
                    if g is not None:
                        do(g, k - lag)

            run_groups(pe, step, 3)

        @block.scalar
        def _(act):
            def copies(g, k):
                act.wait_ge(s_turn, g + 1)
                after(act, s_lg, g - 1)
                act.activation(sb["hT4"][:, k % 2, :], TB[k % 2][:, :], ACT.Copy).then_inc(s_ht, 1)
                act.activation(hT[:, bass.ds(g * 512, 512)], TB[k % 2][:, :], ACT.Copy).then_inc(s_ht, 1)

            run_groups(act, copies, 0)

        @block.vector
        def _(dve):
            def normalise(g, k):
                after(dve, s_turn, g - 1)
                normalise_group(dve, sb, g, k, s_norm)

            def shift(g, k):
                dve.wait_ge(s_lg, g + 1)
                lg = LB[k % 2][:, 0:4 * EXPERTS].rearrange("p (j e) -> p j e", e=EXPERTS)
                after(dve, s_sh, g - 1)
                dve.tensor_reduce(out=m1[:, 4 * (k % 2):4 * (k % 2) + 4], in_=lg, axis=AX.X, op=ALU.max).then_inc(s_max, 1)
                dve.wait_ge(s_max, g + 1)
                dve.tensor_tensor(p[:, bass.ds(g * 4, 4), :], lg, m1[:, 4 * (k % 2):4 * (k % 2) + 4].unsqueeze(2)
                                  .to_broadcast([P, 4, EXPERTS]), ALU.subtract).then_inc(s_sh, 1)

            def step(s, k):
                for lag, do in ((0, normalise), (3, shift)):
                    g = group_of(s, lag)
                    if g is not None:
                        do(g, k - lag)

            run_groups(dve, step, 3)


def route(nc, sb, sem):
    s_sel, s_exp, s_chain = (sem("r_" + n) for n in ("constants", "exp", "chain"))
    R = lambda ap: ap.unsqueeze(2).to_broadcast([P, NT, EXPERTS])
    p, e, oh1, oh2 = sb["r_p"], sb["r_e"], sb["r_oh1"], sb["r_oh2"]
    m1, m2, den, first = sb["r_m1"], sb["r_m2"], sb["r_den"], sb["r_first"]
    order = sb["order"][:].unsqueeze(1).to_broadcast([P, NT, EXPERTS])
    part = [sb["r_parts"][:, :, EXPERTS * i:EXPERTS * i + EXPERTS] for i in range(3)]
    with nc.Block() as block:
        @block.scalar
        def _(act):
            act.activation(p, p, ACT.Exp).then_inc(s_exp, 1)
            act.activation(sb["r_sel"], sb["sel_m"][:], ACT.Copy)
            act.activation(sb["r_ident"], sb["ident"][:], ACT.Copy).then_inc(s_sel, 1)

        @block.vector
        def _(dve):
            n = [0]
            dve.memset(sb["r_parts_padded"][:, NT * 3 * EXPERTS:], 0.0)

            def link(ins):
                n[0] += 1
                ins.then_inc(s_chain, 1)
                dve.wait_ge(s_chain, n[0])

            dve.wait_ge(s_exp, 1)
            link(dve.tensor_reduce(out=den[:], in_=p, axis=AX.X, op=ALU.add))
            link(dve.reciprocal(den[:], den[:]))
            link(dve.tensor_tensor(p, p, R(den[:]), ALU.mult))
            link(dve.tensor_reduce(out=m1[:], in_=p, axis=AX.X, op=ALU.max))
            link(dve.tensor_tensor(e, p, R(m1[:]), ALU.is_ge))
            link(dve.tensor_tensor(e, e, order, ALU.mult))
            link(dve.tensor_reduce(out=first[:], in_=e, axis=AX.X, op=ALU.max))
            link(dve.tensor_tensor(oh1, order, R(first[:]), ALU.is_equal))
            link(dve.scalar_tensor_tensor(out=oh2, in0=oh1, scalar=-2.0, in1=p, op0=ALU.mult, op1=ALU.add))
            link(dve.tensor_reduce(out=m2[:], in_=oh2, axis=AX.X, op=ALU.max))
            link(dve.tensor_tensor(e, oh2, R(m2[:]), ALU.is_ge))
            link(dve.tensor_tensor(e, e, order, ALU.mult))
            link(dve.tensor_reduce(out=first[:], in_=e, axis=AX.X, op=ALU.max))
            link(dve.tensor_tensor(oh2, order, R(first[:]), ALU.is_equal))
            link(dve.tensor_tensor(oh1, oh1, oh2, ALU.add))
            link(dve.scalar_tensor_tensor(out=den[:], in0=m1[:], scalar=1e-9, in1=m2[:], op0=ALU.add, op1=ALU.add))
            link(dve.reciprocal(den[:], den[:]))
            link(dve.tensor_tensor(p, p, oh1, ALU.mult))
            link(dve.tensor_tensor(p, p, R(den[:]), ALU.mult))
            link(dve.tensor_copy(part[0], p))
            link(dve.tensor_tensor(e, p, part[0], ALU.subtract))
            link(dve.tensor_copy(part[1], e))
            link(dve.tensor_tensor(part[2], e, part[1], ALU.subtract))


def expert_layers(nc, sb, ps, sem, hT, x4, out):
    stored = sem("stored")
    names = ("combT", "combT_ready", "gate", "up", "silu", "spread", "hid", "weighted", "down", "x")
    s = {n: sem("e_" + n) for n in names}
    NC, NR = HID_MOE // P, EXPERTS * MID // P
    hid, sg = sb["e_hid"], sb["e_sg"]
    CB, LB, DB = ps[4], ps[5], ps[6:8]
    K3 = 3 * EXPERTS
    parts = sb["r_parts_padded"]
    LT = LB[:, 0:256].bitcast(BF16)

    with nc.Block() as block:
        @block.tensor
        def _(pe):
            def turn_comb(g, k):
                after(pe, s["combT_ready"], g)
                for j in range(4):
                    mm = pe.transpose(LT[:, P * j:P * j + P], parts[:, bass.ds((g * 4 + j) * K3, P)], sb["r_ident"])
                mm.then_inc(s["combT"], 1)

            def spread(g, k, c):
                if c == 0:
                    pe.wait_ge(s["combT_ready"], g + 1)
                after(pe, s["weighted"], NR * g + c)
                pe.matmul(CB[:, :], lhsT=sb["r_sel"][:, c, :], rhs=sb["r_combT"][:, k % 2, :], start=True,
                          stop=True).then_inc(s["spread"], 1)

            def gate_up(g, k, c):
                a = 2 * ((NC * k + c) % 2)
                b = a + 1
                after(pe, s["hid"], g * NC + c - 1)
                rhs = hT[:, bass.ds(g * 512, 512)]
                pe.matmul(ps[a][:, :], lhsT=sb["w_gate"][:, c, :], rhs=rhs, start=True, stop=True).then_inc(s["gate"], 1)
                pe.matmul(ps[b][:, :], lhsT=sb["w_up"][:, c, :], rhs=rhs, start=True, stop=True).then_inc(s["up"], 1)

            def down(g, k):
                pe.wait_ge(s["weighted"], NR * (g + 1))
                after(pe, s["x"], g - 1)
                for j in range(4):
                    for c in range(NC):
                        mm = pe.matmul(DB[k % 2][:, P * j:P * j + P], lhsT=hid[:, k % 2, c, P * j:P * j + P],
                                       rhs=sb["w_down"][:, c, :], start=(c == 0), stop=(c == NC - 1))
                mm.then_inc(s["down"], 1)

            def step(st, k):
                g1, g0 = group_of(st, 1), group_of(st, 0)
                for c in range(NC):
                    if g1 is not None and c < NR:
                        spread(g1, k - 1, c)
                    if g0 is not None:
                        gate_up(g0, k, c)
                if g0 is not None:
                    turn_comb(g0, k)
                if g1 is not None:
                    down(g1, k - 1)

            run_groups(pe, step, 1)

        @block.scalar
        def _(act):
            def copy_combT(g, k):
                act.wait_ge(s["combT"], g + 1)
                after(act, s["spread"], NR * (g - 1))
                act.activation(sb["r_combT"][:, k % 2, :], LT[0:K3, :], ACT.Copy).then_inc(s["combT_ready"], 1)

            def silus(g, k):
                for c in range(NC):
                    act.wait_ge(s["gate"], NC * g + c + 1)
                    after(act, s["hid"], NC * g + c - 1)
                    act.activation(sg[:, (NC * k + c) % 2, :], ps[2 * ((NC * k + c) % 2)][:, :], ACT.Silu).then_inc(s["silu"], 1)

            def step(st, k):
                silus(st, k)
                copy_combT(st, k)

            run_groups(act, step, 0)

        @block.vector
        def _(dve):
            def weigh(g, k, c):
                dve.wait_ge(s["spread"], NR * g + c + 1)
                v = hid[:, k % 2, c, :]
                dve.tensor_tensor(v, CB[:, :], v, ALU.mult).then_inc(s["weighted"], 1)

            def hidden(g, k, c):
                dve.wait_ge(s["silu"], NC * g + c + 1)
                dve.wait_ge(s["up"], NC * g + c + 1)
                after(dve, s["down"], g - 1)
                dve.tensor_tensor(hid[:, k % 2, c, :], ps[2 * ((NC * k + c) % 2) + 1][:, :], sg[:, (NC * k + c) % 2, :],
                                  ALU.mult).then_inc(s["hid"], 1)

            def update(g, k):
                dve.wait_ge(s["down"], g + 1)
                dve.tensor_tensor(x4[:, g, :], DB[k % 2][:, :], x4[:, g, :], ALU.add).then_inc(s["x"], 1)

            def step(st, k):
                g2, g1, g0 = group_of(st, 2), group_of(st, 1), group_of(st, 0)
                for c in range(NC):
                    if g1 is not None and c < NR:
                        if c == 0:
                            dve.wait_ge(s["hid"], NC * (g1 + 1))
                        weigh(g1, k - 1, c)
                    if g0 is not None:
                        if c == 0 and g2 is not None:
                            update(g2, k - 2)
                        hidden(g0, k, c)
                if g0 is None and g2 is not None:
                    update(g2, k - 2)

            run_groups(dve, step, 2)

        @block.sync
        def _(sp):
            for g in range(1, NG, 2):
                sp.wait_ge(s["x"], g + 1)
                t = slice(4 * (g - 1), 4 * (g + 1))
                sp.dma_start(out[:, t, :], sb["x"][:, t, :]).then_inc(stored, 16)
            sp.wait_ge(stored, 16 * (NG // 2))


def decoder_kernel(nc, d, out):
    with ExitStack() as ctx:
        sb = {}

        def sbuf(name, shape, dt=F32):
            sb[name] = ctx.enter_context(nc.sbuf_tensor("sb_" + name, shape, dt))
            return sb[name]

        held = []

        def sem(name):
            held.append(nc.alloc_semaphore(name))
            return held[-1]

        def next_phase():
            nc.clear_and_free_semaphores(list(held))
            held.clear()
            nc.all_engine_barrier()

        banks = ctx.enter_context(nc.psum_tensor("banks", [P, 8, 512], F32))
        ps = [banks[:, i, :] for i in range(8)]
        sb["banks"] = banks
        sbuf("x", [P, NT, DIM])
        for g in ("G1", "G2", "G3"):
            sbuf(g, [P, TOK])
        sb["G3v"] = sb["G3"][:].rearrange("p (t f) -> p t f", f=DIM)
        used = 0
        sb["row_of32"] = sb["G3"][0:SEQ + 3, 0:P]
        sb["alibi32"] = sb["G3"][0:SEQ + 3, P:P + HEADS * SEQ]
        for name, shape in SMALL.items():
            if name in ("row_of32", "alibi32"):
                continue
            if name not in EARLY:
                sbuf(name, list(shape))
                continue
            width = int(shape[1]) * (int(shape[2]) if len(shape) == 3 else 1)
            view = sb["G2"][0:shape[0], used:used + width]
            sb[name] = view if len(shape) == 2 else view.rearrange("p (c n) -> p c n", c=shape[1])
            used += width
        at = [used]

        def beside(rows, *shape, dt=F32):
            n = 1
            for v in shape:
                n *= v
            width = n if dt == F32 else n // 2
            view = sb["G2"][0:rows, at[0]:at[0] + width]
            view = view if dt == F32 else view.bitcast(dt)
            at[0] += width
            assert at[0] <= TOK
            return view if len(shape) == 1 else view.rearrange("p (a b) -> p a b", a=shape[0])

        sb["f_sel"] = beside(P, 8, P, dt=BF16)
        sb["f_top"] = beside(P, 2, 512, dt=BF16)
        sb["f_low"] = beside(M_SHRINK, 2, 512, dt=BF16)
        sb["f_mid"] = beside(M_SHRINK, 512, dt=BF16)
        sb["f_rest"] = beside(P, 512)
        sb["f_rowB"] = beside(P, DIM)
        sbuf("st6", [P, NT, 6])
        for name in ("mean", "rstd", "nmr", "dif", "var"):
            sbuf(name, [P, NT])
        sbuf("scratch", [P, 1])
        sbuf("own_half", [P, 2])
        sbuf("ones_row", [1, P])
        sbuf("zeros", [P, 64])
        sbuf("bqs_x0", [P, 1])
        sbuf("bqs_a1", [P, 1])
        sbuf("vblk", [P, 2, 4, 2, PAIRS, 2 * VW], BF16)
        sbuf("v32", [P, 2, 2, PAIRS, 2, HD])
        sbuf("biasP", [P, 2, PAIRS, P], BF16)
        sbuf("row_of", [SEQ + 3, P], BF16)
        sbuf("alibi", [SEQ + 3, HEADS * SEQ], BF16)
        for layer in LAYERS:
            sbuf("bkm_" + layer, [P, 4])
        ring = sbuf("ring", [P, 7744])
        at = [0]

        def part(name, *shape):
            n = 1
            for v in shape:
                n *= v
            names = "abc"[:len(shape)]
            sb[name] = ring[:, at[0]:at[0] + n].rearrange(
                f"p ({' '.join(names)}) -> p {' '.join(names)}", **dict(zip(names, shape)))
            at[0] += n

        part("xn", 2, P)
        part("hT", 2, P)
        part("cT", 4, P)
        part("vp", 2, P)
        part("qT", 2, P)
        part("km", 2, 4, P)
        part("sx", 2, 1024)
        sb["pt"] = ring[:, at[0]:at[0] + 2048].bitcast(BF16).rearrange("p (h r n) -> p h r n", h=2, r=2)
        at[0] += 2048
        part("y", 2, P)
        part("yT", 2, P)
        part("nmx", 2, HEADS)
        part("rec", 2, HEADS)
        at[0] = 0
        part("xn4", 2, 4, P)
        part("hT4", 2, 512)
        part("sT", 2, 512)
        part("e_sg", 2, 512)
        sb["r_combT"] = ring[0:3 * EXPERTS, at[0]:at[0] + 512].bitcast(BF16).rearrange("p (r n) -> p r n", r=2)
        at[0] = 0
        part("b_kT", 2, 512)
        part("b_k", 4, 512)
        part("b_f", 2, 512)
        part("b_s", 2, 256)
        part("b_bd", 2, 512)
        part("b_pT", 2, 512)
        part("b_mx", 2, 4)
        part("b_sm", 2, 4)
        at[0] = 0
        part("rnd", 2, 1024)
        part("wtmp", 1024)
        at[0] = 0
        part("h_f", 4, 512)
        part("h_r", 2, 512)
        part("h_y", 512)
        sb["h_q"] = ring[:, at[0]:at[0] + 2048].bitcast(BF16).rearrange("p (a b c) -> p a b c", a=2, b=4)
        sb["e_hid"] = sb["G1"][:, 0:2 * 5 * 512].rearrange("p (a b c) -> p a b c", a=2, b=5)

        for name, width in (("wsum", 7), ("wall", 7), ("wscale", 7), ("wthr", 7), ("wnthr", 7), ("osc", 7),
                            ("osc_img", 7), ("roundc", 1), ("stat", 16), ("amax", 1), ("amaxall", 1), ("isc", 1),
                            ("inv", 1), ("avg", BATCH), ("hmax", 4)):
            sbuf(name, [P, width])
        sbuf("pmax", [P, 4, NG])
        sbuf("qavg", [P, BATCH], BF16)
        sbuf("row", [1, DIM])
        for n in WS:
            sbuf("t_" + n, [P, SMALL["b_" + n][1]], BF16)
        n = NT * EXPERTS
        for i, name in enumerate(("r_p", "r_e", "r_oh1", "r_oh2")):
            sb[name] = sb["G2"][:, n * i:n * i + n].rearrange("p (t e) -> p t e", e=EXPERTS)
        half = sb["G2"][:, 4 * n:].bitcast(BF16)
        sb["r_parts"] = half[:, 0:3 * n].rearrange("p (t e) -> p t e", e=3 * EXPERTS)
        sb["r_parts_padded"] = half[:, 0:3 * n + P]
        sb["r_ident"] = half[:, 3 * n + P:3 * n + 2 * P]
        sb["r_sel"] = half[0:3 * EXPERTS, 3 * n + 2 * P:3 * n + 6 * P].rearrange("p (c n) -> p c n", n=P)
        for name in ("r_m1", "r_m2", "r_den", "r_first"):
            sbuf(name, [P, NT])

        load_inputs(nc, sb, sem, d)
        set_constants(nc, sb, sem)
        mean_and_rstd(nc, sb, sem, "ln1", LN_EPS)
        attention(nc, sb, ps, sem, "a0")
        mean_and_rstd(nc, sb, sem, "ln1o", 1e-3)
        second_norm(nc, sb, sem)
        next_phase()
        mean_and_rstd(nc, sb, sem, "ln2", LN_EPS)
        attention(nc, sb, ps, sem, "x0")
        next_phase()
        mean_and_rstd(nc, sb, sem, "ln3", LN_EPS)
        shrink_ffn(nc, sb, ps, sem)
        next_phase()
        mean_and_rstd(nc, sb, sem, "ln4", LN_EPS)
        attention(nc, sb, ps, sem, "a1")
        next_phase()
        mean_and_rstd(nc, sb, sem, "ln5", LN_EPS)
        bitnet(nc, sb, ps, sem, next_phase)
        next_phase()
        mean_and_rstd(nc, sb, sem, "ln6", LN_EPS)
        experts(nc, sb, ps, sem, out)
        next_phase()


EARLY = ("biasT", "sel_e", "w_out", "b_d2v", "b_img", "b_txt", "b_att0", "b_att1", "b_f1", "b_f2")

SMALL = {
    "ident": (P, P), "head_mask": (P, 4), "row_of32": (SEQ + 3, P), "alibi32": (SEQ + 3, HEADS * SEQ), "biasT": (P, PAIRS, P),
    "gammaB": (P, DIM), "betaB": (P, DIM),
    "wq_a0": (P, P), "wk_a0": (P, P), "wv_a0": (P, 2, 64), "bv_a0": (P, P),
    "wq_x0": (P, P), "wk_x0": (CTX, P), "wv_x0": (CTX, 2, 64), "wo_x0": (P, P),
    "bq_x0": (P, 1), "bk_x0": (P, 1), "bv_x0": (P, P), "bo_x0": (1, P),
    "wq_a1": (P, P), "wk_a1": (P, P), "wv_a1": (P, 2, 64), "wo_a1": (P, P),
    "w_in": (P, 2 * M_SHRINK), "b_in": (2 * M_SHRINK, 1), "sel_e": (2 * M_SHRINK, 8, P), "w_1": (P, 8), "b_1": (P, 8),
    "w_2": (P, 8), "b_2": (M_SHRINK, 1), "w_outp": (M_SHRINK, DIM), "w_out": (P, 8, DIM), "b_out": (1, DIM),
    "b_d2v": (CTX, P), "b_img": (P, P), "b_txt": (P, P), "b_att0": (P, P), "b_att1": (P, P),
    "b_f1": (P, 2 * FFN), "b_f2": (P, FFN),
    "bb_d2v": (P, 1), "bb_img": (P, 1), "bb_txt": (P, 1), "bb_att0": (P, 1), "bb_att1": (P, 1),
    "bB_att0": (P, P), "bB_att1": (P, P), "bb_f1": (P, 4), "bB_f2": (P, P),
    "w_router": (P, EXPERTS), "order": (P, EXPERTS), "sel_m": (3 * EXPERTS, 4, P),
    "w_gate": (P, 5, P), "w_up": (P, 5, P), "w_down": (P, 5, DIM),
    "bq_a1": (P, 1), "bk_a1": (P, 1), "bv_a1": (P, P), "bo_a1": (1, P),
}


def laid_out(i):
    import numpy as np

    f = np.float32
    o = {}
    o["x"] = np.ascontiguousarray(i["x"].reshape(NT, P, DIM).transpose(1, 0, 2))
    o["ctxT"] = np.ascontiguousarray(i["ctx_768"].reshape(TOK, CTX).T)
    o["ident"] = np.eye(P, dtype=f)
    p = np.arange(P)
    o["head_mask"] = (((p % 32) // HD)[:, None] == np.arange(4)[None, :]).astype(f)
    slopes = (2.0 ** (-(8.0 / HEADS) * np.arange(1, HEADS + 1))).astype(f)
    pos = np.arange(SEQ)
    mask = np.where(pos[None, None, :] <= pos[:, None, None], f(0), f(-1e30))
    left = slopes[:, None] * pos[None].astype(f)
    thirds = []
    for _ in range(3):
        thirds.append((left.view(np.uint32) & np.uint32(0xFFFF0000)).view(f))
        left = left - thirds[-1]
    o["alibi32"] = np.concatenate([np.broadcast_to(mask, (SEQ, HEADS, SEQ)).reshape(SEQ, -1),
                                   np.stack(thirds).reshape(3, -1)]).astype(f)
    o["row_of32"] = np.concatenate([pos[:, None] == (p % SEQ)[None], np.ones((3, P), bool)]).astype(f)
    h, q, k = np.arange(HEADS)[:, None, None], pos[None, :, None], pos[None, None, :]
    table = i["L0_attn_rel_table"].reshape(-1)
    flat = h * SEQ * SEQ + q * SEQ + k
    qi, kj, hh = flat // (SEQ * HEADS), (flat // HEADS) % SEQ, flat % HEADS
    bias = table[(kj - qi + SEQ - 1) * HEADS + hh]
    bias = bias.reshape(PAIRS, 2, SEQ, SEQ).transpose(1, 3, 0, 2).reshape(P, PAIRS, SEQ)
    o["biasT"] = np.concatenate([bias, bias], axis=2)
    o["gammaB"] = np.tile(i["L0_attn_gamma"][None], (P, 1))
    o["betaB"] = np.tile(i["L0_attn_beta"][None], (P, 1))

    def values(w):
        return np.ascontiguousarray(w.reshape(-1, PAIRS, 2, HD).transpose(0, 2, 1, 3).reshape(-1, 2, 64))

    def value_bias(b):
        both = b.reshape(PAIRS, 2, HD).transpose(1, 0, 2).reshape(2, 1, 1, 64)
        return np.ascontiguousarray(np.broadcast_to(both, (2, 64, 2, 64)).reshape(P, P))

    o["wq_a0"], o["wk_a0"], o["wv_a0"] = i["L0_attn_Wq"], i["L0_attn_Wk"], values(i["L0_attn_Wv"])
    o["bv_a0"] = np.zeros((P, P), f)
    o["wq_x0"], o["wk_x0"], o["wv_x0"] = i["L0_xattn_wq"], i["L0_xattn_wk"], values(i["L0_xattn_wv"])
    o["wo_x0"], o["bo_x0"] = i["L0_xattn_wo"], i["L0_xattn_bo"][None]
    o["bq_x0"], o["bk_x0"] = i["L0_xattn_bq"][:, None], i["L0_xattn_bk"][:, None]
    o["bv_x0"] = value_bias(i["L0_xattn_bv"])
    w, b = i["L1_attn_w_attn"], i["L1_attn_b_attn"]
    o["wq_a1"], o["wk_a1"], o["wv_a1"] = w[:, 0:P], w[:, P:2 * P], values(w[:, 2 * P:])
    o["wo_a1"], o["bo_a1"] = i["L1_attn_w_proj"], i["L1_attn_b_proj"][None]
    o["bq_a1"], o["bk_a1"], o["bv_a1"] = b[0:P, None], b[P:2 * P, None], value_bias(b[2 * P:])

    def columns(a):
        return a.reshape(-1, P).T

    hid = np.arange(M_SHRINK * INNER).reshape(8, P)
    o["w_in"] = np.concatenate([i["L0_ffn_Win"]] * 2, axis=1)
    o["b_in"] = np.concatenate([i["L0_ffn_bin_"]] * 2)[:, None]
    o["sel_e"] = (np.arange(2 * M_SHRINK)[:, None, None] % M_SHRINK == hid[None] // INNER).astype(f)
    o["w_1"], o["b_1"], o["w_2"] = columns(i["L0_ffn_W1"]), columns(i["L0_ffn_b1"]), columns(i["L0_ffn_W2"])
    o["b_2"], o["w_outp"], o["b_out"] = i["L0_ffn_b2"][:, None], i["L0_ffn_Wout"], i["L0_ffn_bout"][None]
    o["w_out"] = i["L0_ffn_Wout"][hid // INNER].transpose(1, 0, 2)

    w = {n: i["L1_xattn_W_" + n].T for n in ("d2v", "img", "txt", "att0", "att1")}
    o["b_d2v"], o["b_img"], o["b_txt"] = w["d2v"], w["img"], w["txt"]
    for n in ("att0", "att1"):
        o["b_" + n] = np.concatenate([w[n], w[n]], axis=1)
        b = i["L1_xattn_b_" + n]
        o["bb_" + n] = np.concatenate([b, b])[:, None]
        o["bB_" + n] = np.tile(np.concatenate([b, b])[None], (P, 1))
    o["b_f1"] = i["L1_xattn_W_f1"].T.reshape(2, P, FFN).transpose(1, 0, 2).reshape(P, 2 * FFN)
    o["b_f2"] = i["L1_xattn_W_f2"].T.reshape(4, P, P).transpose(1, 0, 2).reshape(P, FFN)
    for n in ("d2v", "img", "txt"):
        o["bb_" + n] = i["L1_xattn_b_" + n][:, None]
    o["bb_f1"] = columns(i["L1_xattn_b_f1"])
    o["bB_f2"] = np.tile(i["L1_xattn_b_f2"][None], (P, 1))

    def hidden(routed, shared):
        r = i[routed].transpose(1, 0, 2).reshape(P, EXPERTS * MID)
        s = i[shared].transpose(1, 0, 2).reshape(P, P)
        return np.concatenate([r, s], axis=1).reshape(P, 5, P)

    o["w_router"] = i["L1_ffn_router_w"]
    o["order"] = np.tile(np.arange(EXPERTS, 0, -1)[None].astype(f), (P, 1))
    o["sel_m"] = (np.arange(3 * EXPERTS)[:, None, None] % EXPERTS
                  == np.arange(EXPERTS * MID).reshape(4, P)[None] // MID).astype(f)
    o["w_gate"], o["w_up"] = hidden("L1_ffn_wg_r", "L1_ffn_wg_s"), hidden("L1_ffn_wu_r", "L1_ffn_wu_s")
    down = np.concatenate([i["L1_ffn_wd_r"].reshape(-1, DIM), i["L1_ffn_wd_s"].reshape(-1, DIM)])
    o["w_down"] = down.reshape(5, P, DIM).transpose(1, 0, 2)
    return {k: np.ascontiguousarray(v) for k, v in o.items()}


def kernel(**inputs):
    import numpy as _np
    import concourse.bacc as _bacc
    from concourse.bass_utils import run_bass_kernel_spmd as _run

    arrays = laid_out({k: _np.asarray(v) for k, v in inputs.items()})
    nc = _bacc.Bacc("TRN2", target_bir_lowering=False, num_devices=1)
    d = {k: nc.dram_tensor("in_" + k, v.shape, F32, kind="ExternalInput").ap() for k, v in arrays.items()}
    d["_small"] = [k for k in arrays if k not in ("x", "ctxT")]
    out = nc.dram_tensor("out_x", (P, NT, DIM), F32, kind="ExternalOutput").ap()
    decoder_kernel(nc, d, out)
    r = _run(nc, [{"in_" + k: v for k, v in arrays.items()}], core_ids=[0])
    return r.results[0]["out_x"].transpose(1, 0, 2).reshape(BATCH, SEQ, DIM)
```
